# Optimizing a Trainium2 kernel written in Bass

```python
import numpy as np
import jax
import jax.numpy as jnp

def _softmax(x, axis=-1):
    return jax.nn.softmax(x, axis=axis)

def _gelu(x):
    return jax.nn.gelu(x, approximate=True)

def _silu(x):
    return jax.nn.silu(x)

def _sigmoid(x):
    return jax.nn.sigmoid(x)

def _layernorm(x, axis=-1, eps=1e-05):
    m = jnp.mean(x, axis=axis, keepdims=True)
    v = jnp.var(x, axis=axis, keepdims=True)
    return (x - m) / jnp.sqrt(v + eps)

def _scatter_add(tgt, idx, src, axis=0):
    return tgt.at[idx].add(src)

def _segment_sum(src, seg, n):
    return jax.ops.segment_sum(src, seg, n)
kernel_name = 'mk_prb_d2_jaxref_r8_098848'

def setup_inputs(seed: int=0):
    np.random.seed(seed)
    _w = jnp.asarray

    def _L0_attn_setup():
        import jax, jax.numpy as jnp
        import numpy as np
        D_MODEL, D_STATE, D_CONV, EXPAND, NHEADS, NGROUPS = (128, 16, 4, 2, 8, 1)
        D_INNER = D_MODEL * EXPAND
        HEADDIM = D_INNER // NHEADS
        D_XBC = D_INNER + 2 * NGROUPS * D_STATE
        D_IN_PROJ = 3 * D_INNER + D_XBC + NHEADS
        BATCH, SEQLEN = (2, 256)
        LN_EPS = 1e-05

        def _silu(x):
            return x * jax.nn.sigmoid(x)
        key = jax.random.key(seed)
        ks = jax.random.split(key, 8)
        u = jax.random.normal(ks[0], (BATCH, SEQLEN, D_MODEL), dtype=jnp.float32)
        W_in = jax.random.normal(ks[1], (D_IN_PROJ, D_MODEL), jnp.float32) / np.sqrt(D_MODEL)
        conv_w = jax.random.normal(ks[2], (D_XBC, 1, D_CONV), jnp.float32) / np.sqrt(D_CONV)
        conv_b = jnp.zeros((D_XBC,), jnp.float32)
        dt = jnp.exp(jax.random.uniform(ks[3], (NHEADS,)) * (np.log(0.1) - np.log(0.001)) + np.log(0.001))
        dt_bias = dt + jnp.log(-jnp.expm1(-dt))
        A_log = jnp.log(jax.random.uniform(ks[4], (NHEADS,), minval=0.9, maxval=0.999))
        D_param = jnp.ones((NHEADS,), jnp.float32)
        ln_gamma = jnp.ones((D_INNER,), jnp.float32)
        ln_beta = jnp.zeros((D_INNER,), jnp.float32)
        W_gate = jax.random.normal(ks[5], (D_INNER, D_INNER), jnp.float32) / np.sqrt(D_INNER)
        b_gate = jnp.zeros((D_INNER,), jnp.float32)
        W_out = jax.random.normal(ks[6], (D_MODEL, 2 * D_INNER), jnp.float32) / np.sqrt(2 * D_INNER)
        return dict(u=u, W_in=W_in, conv_w=conv_w, conv_b=conv_b, dt_bias=dt_bias, A_log=A_log, D_param=D_param, ln_gamma=ln_gamma, ln_beta=ln_beta, W_gate=W_gate, b_gate=b_gate, W_out=W_out)
    _L0_attn_in = _L0_attn_setup()

    def _L0_ffn_setup():
        import jax, jax.numpy as jnp
        import numpy as np
        H_DIM, E_DIM = (128, 64)
        N_SHARED, N_ROUTED, TOP_K = (2, 16, 4)
        B, S = (4, 256)
        key = jax.random.key(seed)
        ks = jax.random.split(key, 6)
        sc = 1.0 / np.sqrt(H_DIM)
        ec = 1.0 / np.sqrt(E_DIM)
        return {'x': jax.random.normal(ks[0], (B, S, H_DIM), dtype=jnp.float32), 'shared_up': jax.random.uniform(ks[1], (N_SHARED, E_DIM, H_DIM), jnp.float32, -sc, sc), 'shared_down': jax.random.uniform(ks[2], (N_SHARED, H_DIM, E_DIM), jnp.float32, -ec, ec), 'routed_up': jax.random.uniform(ks[3], (N_ROUTED, E_DIM, H_DIM), jnp.float32, -sc, sc), 'routed_down': jax.random.uniform(ks[4], (N_ROUTED, H_DIM, E_DIM), jnp.float32, -ec, ec), 'router_w': jax.random.uniform(ks[5], (N_ROUTED, H_DIM), jnp.float32, -sc, sc)}
    _L0_ffn_in = _L0_ffn_setup()

    def _L1_attn_setup():
        import jax, jax.numpy as jnp
        import numpy as np
        B, S, D, H, W, FFN = (2, 512, 128, 16, 32, 512)
        HD = D // H

        def layer_norm(x, g, b):
            mu = x.mean(-1, keepdims=True)
            var = ((x - mu) ** 2).mean(-1, keepdims=True)
            return (x - mu) * jax.lax.rsqrt(var + 1e-05) * g + b

        def sliding_window_attn(x, Wq, bq, Wk, bk, Wv, bv, Wo, bo):
            b, s, d = x.shape
            nb = s // W
            q = (x @ Wq + bq).reshape(b, nb, W, H, HD)
            k = (x @ Wk + bk).reshape(b, nb, W, H, HD)
            v = (x @ Wv + bv).reshape(b, nb, W, H, HD)
            pad = [(0, 0), (1, 1), (0, 0), (0, 0), (0, 0)]
            kp, vp = (jnp.pad(k, pad), jnp.pad(v, pad))
            kc = jnp.concatenate([kp[:, :-2], kp[:, 1:-1], kp[:, 2:]], axis=2)
            vc = jnp.concatenate([vp[:, :-2], vp[:, 1:-1], vp[:, 2:]], axis=2)
            scale = jnp.asarray(1.0 / np.sqrt(HD), x.dtype)
            scores = jnp.einsum('bnqhd,bnkhd->bhnqk', q, kc) * scale
            i = jnp.arange(W)[:, None]
            j = jnp.arange(3 * W)[None, :]
            band = jnp.abs(i + W - j) <= W
            kidx = jnp.arange(nb)[:, None] * W - W + jnp.arange(3 * W)[None, :]
            valid = (kidx >= 0) & (kidx < s)
            mask = band[None, :, :] & valid[:, None, :]
            scores = jnp.where(mask[None, None], scores, jnp.asarray(-1000000000.0, x.dtype))
            attn = jax.nn.softmax(scores, axis=-1)
            out = jnp.einsum('bhnqk,bnkhd->bnqhd', attn, vc).reshape(b, s, d)
            return out @ Wo + bo
        key = jax.random.key(seed)
        ks = jax.random.split(key, 16)
        s = 1.0 / np.sqrt(D)
        inp = {'x': jax.random.normal(ks[0], (B, S, D), jnp.float32), 'Wq': jax.random.normal(ks[1], (D, D), jnp.float32) * s, 'bq': jnp.zeros((D,), jnp.float32), 'Wk': jax.random.normal(ks[2], (D, D), jnp.float32) * s, 'bk': jnp.zeros((D,), jnp.float32), 'Wv': jax.random.normal(ks[3], (D, D), jnp.float32) * s, 'bv': jnp.zeros((D,), jnp.float32), 'Wo': jax.random.normal(ks[4], (D, D), jnp.float32) * s, 'bo': jnp.zeros((D,), jnp.float32), 'g1': jnp.ones((D,), jnp.float32), 'b1': jnp.zeros((D,), jnp.float32), 'W1': jax.random.normal(ks[5], (D, FFN), jnp.float32) * s, 'c1': jnp.zeros((FFN,), jnp.float32), 'W2': jax.random.normal(ks[6], (FFN, D), jnp.float32) * (1.0 / np.sqrt(FFN)), 'c2': jnp.zeros((D,), jnp.float32), 'g2': jnp.ones((D,), jnp.float32), 'b2': jnp.zeros((D,), jnp.float32)}
        return inp
    _L1_attn_in = _L1_attn_setup()

    def _L1_ffn_setup():
        import jax, jax.numpy as jnp
        import numpy as np
        B, S, D, H, E = (4, 256, 128, 512, 8)
        key = jax.random.key(seed)
        ks = jax.random.split(key, 8)
        s_d = 1.0 / np.sqrt(D)
        s_h = 1.0 / np.sqrt(H)
        return {'x': jax.random.normal(ks[0], (B, S, D), dtype=jnp.float32), 'gate_w': jax.random.uniform(ks[1], (E, D), jnp.float32, -s_d, s_d), 'gate_b': jax.random.uniform(ks[2], (E,), jnp.float32, -s_d, s_d), 'w1': jax.random.uniform(ks[3], (E, H, D), jnp.float32, -s_d, s_d), 'b1': jax.random.uniform(ks[4], (E, H), jnp.float32, -s_d, s_d), 'w2': jax.random.uniform(ks[5], (E, D, H), jnp.float32, -s_h, s_h), 'b2': jax.random.uniform(ks[6], (E, D), jnp.float32, -s_h, s_h)}
    _L1_ffn_in = _L1_ffn_setup()
    _d = {'L0_attn_u': _L0_attn_in['u'], 'L0_attn_W_in': _L0_attn_in['W_in'], 'L0_attn_conv_w': _L0_attn_in['conv_w'], 'L0_attn_conv_b': _L0_attn_in['conv_b'], 'L0_attn_dt_bias': _L0_attn_in['dt_bias'], 'L0_attn_A_log': _L0_attn_in['A_log'], 'L0_attn_D_param': _L0_attn_in['D_param'], 'L0_attn_ln_gamma': _L0_attn_in['ln_gamma'], 'L0_attn_ln_beta': _L0_attn_in['ln_beta'], 'L0_attn_W_gate': _L0_attn_in['W_gate'], 'L0_attn_b_gate': _L0_attn_in['b_gate'], 'L0_attn_W_out': _L0_attn_in['W_out'], 'L0_ffn_shared_up': _L0_ffn_in['shared_up'], 'L0_ffn_shared_down': _L0_ffn_in['shared_down'], 'L0_ffn_routed_up': _L0_ffn_in['routed_up'], 'L0_ffn_routed_down': _L0_ffn_in['routed_down'], 'L0_ffn_router_w': _L0_ffn_in['router_w'], 'L1_attn_Wq': _L1_attn_in['Wq'], 'L1_attn_bq': _L1_attn_in['bq'], 'L1_attn_Wk': _L1_attn_in['Wk'], 'L1_attn_bk': _L1_attn_in['bk'], 'L1_attn_Wv': _L1_attn_in['Wv'], 'L1_attn_bv': _L1_attn_in['bv'], 'L1_attn_Wo': _L1_attn_in['Wo'], 'L1_attn_bo': _L1_attn_in['bo'], 'L1_attn_g1': _L1_attn_in['g1'], 'L1_attn_b1': _L1_attn_in['b1'], 'L1_attn_W1': _L1_attn_in['W1'], 'L1_attn_c1': _L1_attn_in['c1'], 'L1_attn_W2': _L1_attn_in['W2'], 'L1_attn_c2': _L1_attn_in['c2'], 'L1_attn_g2': _L1_attn_in['g2'], 'L1_attn_b2': _L1_attn_in['b2'], 'L1_ffn_gate_w': _L1_ffn_in['gate_w'], 'L1_ffn_gate_b': _L1_ffn_in['gate_b'], 'L1_ffn_w1': _L1_ffn_in['w1'], 'L1_ffn_b1': _L1_ffn_in['b1'], 'L1_ffn_w2': _L1_ffn_in['w2'], 'L1_ffn_b2': _L1_ffn_in['b2']}
    _x0 = _d['L0_attn_u']
    _d['L0_attn_u'] = jax.random.normal(jax.random.fold_in(jax.random.key(seed), 1), (8, 512, 128), dtype=_x0.dtype)
    del _x0
    return _d

def reference(L0_attn_u, L0_attn_W_in, L0_attn_conv_w, L0_attn_conv_b, L0_attn_dt_bias, L0_attn_A_log, L0_attn_D_param, L0_attn_ln_gamma, L0_attn_ln_beta, L0_attn_W_gate, L0_attn_b_gate, L0_attn_W_out, L0_ffn_shared_up, L0_ffn_shared_down, L0_ffn_routed_up, L0_ffn_routed_down, L0_ffn_router_w, L1_attn_Wq, L1_attn_bq, L1_attn_Wk, L1_attn_bk, L1_attn_Wv, L1_attn_bv, L1_attn_Wo, L1_attn_bo, L1_attn_g1, L1_attn_b1, L1_attn_W1, L1_attn_c1, L1_attn_W2, L1_attn_c2, L1_attn_g2, L1_attn_b2, L1_ffn_gate_w, L1_ffn_gate_b, L1_ffn_w1, L1_ffn_b1, L1_ffn_w2, L1_ffn_b2):

    def _L0_attn_ref(u, W_in, conv_w, conv_b, dt_bias, A_log, D_param, ln_gamma, ln_beta, W_gate, b_gate, W_out):
        import jax, jax.numpy as jnp
        import numpy as np
        D_MODEL, D_STATE, D_CONV, EXPAND, NHEADS, NGROUPS = (128, 16, 4, 2, 8, 1)
        D_INNER = D_MODEL * EXPAND
        HEADDIM = D_INNER // NHEADS
        D_XBC = D_INNER + 2 * NGROUPS * D_STATE
        D_IN_PROJ = 3 * D_INNER + D_XBC + NHEADS
        BATCH, SEQLEN = (2, 256)
        LN_EPS = 1e-05

        def _silu(x):
            return x * jax.nn.sigmoid(x)
        B, L, _ = u.shape
        zxbcdt = u @ W_in.T
        z0 = zxbcdt[..., :D_INNER]
        x0 = zxbcdt[..., D_INNER:2 * D_INNER]
        xBC = zxbcdt[..., 3 * D_INNER:3 * D_INNER + D_XBC]
        dt = jax.nn.softplus(zxbcdt[..., -NHEADS:] + dt_bias)
        A = -jnp.exp(A_log)
        xBC_c = jnp.transpose(xBC, (0, 2, 1))
        xBC_c = jax.lax.conv_general_dilated(xBC_c, conv_w, window_strides=(1,), padding=[(D_CONV - 1, 0)], dimension_numbers=('NCH', 'OIH', 'NCH'), feature_group_count=D_XBC)
        xBC = _silu(jnp.transpose(xBC_c, (0, 2, 1)) + conv_b)
        x = xBC[..., :D_INNER].reshape(B, L, NHEADS, HEADDIM)
        Bm = xBC[..., D_INNER:D_INNER + D_STATE]
        Cm = xBC[..., D_INNER + D_STATE:]

        def step(h, inp):
            x_t, B_t, C_t, dt_t = inp
            dA = jnp.exp(dt_t * A)[:, :, None, None]
            h = dA * h + dt_t[:, :, None, None] * x_t[..., None] * B_t[:, None, None, :]
            y_t = jnp.einsum('bhpn,bn->bhp', h, C_t) + D_param[None, :, None] * x_t
            return (h, y_t)
        h0 = jnp.zeros((B, NHEADS, HEADDIM, D_STATE), u.dtype)
        xs = (jnp.moveaxis(x, 1, 0), jnp.moveaxis(Bm, 1, 0), jnp.moveaxis(Cm, 1, 0), jnp.moveaxis(dt, 1, 0))
        _, y = jax.lax.scan(step, h0, xs)
        y = jnp.moveaxis(y, 0, 1).reshape(B, L, D_INNER)
        mu = y.mean(-1, keepdims=True)
        var = ((y - mu) ** 2).mean(-1, keepdims=True)
        y = (y - mu) * jax.lax.rsqrt(var + LN_EPS) * ln_gamma + ln_beta
        gate = jax.nn.sigmoid(y @ W_gate.T + b_gate)
        y = gate * y
        mlp_skip = _silu(z0) * x0
        return jnp.concatenate([mlp_skip, y], axis=-1) @ W_out.T

    def _L0_ffn_ref(x, shared_up, shared_down, routed_up, routed_down, router_w):
        import jax, jax.numpy as jnp
        import numpy as np
        H_DIM, E_DIM = (128, 64)
        N_SHARED, N_ROUTED, TOP_K = (2, 16, 4)
        B, S = (4, 256)
        b, s, h = x.shape
        xt = x.reshape(-1, h)
        up_s = jnp.einsum('th,seh->tse', xt, shared_up)
        shared = jnp.einsum('tse,she->th', jax.nn.gelu(up_s, approximate=False), shared_down)
        probs = jax.nn.softmax(xt @ router_w.T, axis=-1)
        topk_p, topk_i = jax.lax.top_k(probs, TOP_K)
        gate = jnp.zeros_like(probs).at[jnp.arange(xt.shape[0])[:, None], topk_i].add(topk_p)
        up_r = jnp.einsum('th,reh->tre', xt, routed_up)
        act = jax.nn.gelu(up_r, approximate=False) * gate[:, :, None]
        routed = jnp.einsum('tre,rhe->th', act, routed_down)
        return (shared + routed).reshape(b, s, h)

    def _L1_attn_ref(x, Wq, bq, Wk, bk, Wv, bv, Wo, bo, g1, b1, W1, c1, W2, c2, g2, b2):
        import jax, jax.numpy as jnp
        import numpy as np
        B, S, D, H, W, FFN = (2, 512, 128, 16, 32, 512)
        HD = D // H

        def layer_norm(x, g, b):
            mu = x.mean(-1, keepdims=True)
            var = ((x - mu) ** 2).mean(-1, keepdims=True)
            return (x - mu) * jax.lax.rsqrt(var + 1e-05) * g + b

        def sliding_window_attn(x, Wq, bq, Wk, bk, Wv, bv, Wo, bo):
            b, s, d = x.shape
            nb = s // W
            q = (x @ Wq + bq).reshape(b, nb, W, H, HD)
            k = (x @ Wk + bk).reshape(b, nb, W, H, HD)
            v = (x @ Wv + bv).reshape(b, nb, W, H, HD)
            pad = [(0, 0), (1, 1), (0, 0), (0, 0), (0, 0)]
            kp, vp = (jnp.pad(k, pad), jnp.pad(v, pad))
            kc = jnp.concatenate([kp[:, :-2], kp[:, 1:-1], kp[:, 2:]], axis=2)
            vc = jnp.concatenate([vp[:, :-2], vp[:, 1:-1], vp[:, 2:]], axis=2)
            scale = jnp.asarray(1.0 / np.sqrt(HD), x.dtype)
            scores = jnp.einsum('bnqhd,bnkhd->bhnqk', q, kc) * scale
            i = jnp.arange(W)[:, None]
            j = jnp.arange(3 * W)[None, :]
            band = jnp.abs(i + W - j) <= W
            kidx = jnp.arange(nb)[:, None] * W - W + jnp.arange(3 * W)[None, :]
            valid = (kidx >= 0) & (kidx < s)
            mask = band[None, :, :] & valid[:, None, :]
            scores = jnp.where(mask[None, None], scores, jnp.asarray(-1000000000.0, x.dtype))
            attn = jax.nn.softmax(scores, axis=-1)
            out = jnp.einsum('bhnqk,bnkhd->bnqhd', attn, vc).reshape(b, s, d)
            return out @ Wo + bo
        a = sliding_window_attn(x, Wq, bq, Wk, bk, Wv, bv, Wo, bo)
        h = layer_norm(a + x, g1, b1)
        f = jax.nn.gelu(h @ W1 + c1) @ W2 + c2
        return layer_norm(f + h, g2, b2)

    def _L1_ffn_ref(x, gate_w, gate_b, w1, b1, w2, b2):
        import jax, jax.numpy as jnp
        import numpy as np
        B, S, D, H, E = (4, 256, 128, 512, 8)
        b, s, d = x.shape
        xf = x.reshape(-1, d)
        logits = xf @ gate_w.T + gate_b
        top1 = jnp.argmax(logits, axis=-1)
        out = jnp.zeros_like(xf)
        n_experts = w1.shape[0]
        for e in range(n_experts):
            h = jax.nn.relu(xf @ w1[e].T + b1[e])
            y = h @ w2[e].T + b2[e]
            out = out + jnp.where((top1 == e)[:, None], y, jnp.zeros((), y.dtype))
        return out.reshape(b, s, d)
    x = L0_attn_u
    xn = _layernorm(x, axis=-1)
    x = x + _L0_attn_ref(xn, L0_attn_W_in, L0_attn_conv_w, L0_attn_conv_b, L0_attn_dt_bias, L0_attn_A_log, L0_attn_D_param, L0_attn_ln_gamma, L0_attn_ln_beta, L0_attn_W_gate, L0_attn_b_gate, L0_attn_W_out) + _L0_ffn_ref(xn, L0_ffn_shared_up, L0_ffn_shared_down, L0_ffn_routed_up, L0_ffn_routed_down, L0_ffn_router_w)
    xn = _layernorm(x, axis=-1)
    x = x + _L1_attn_ref(xn, L1_attn_Wq, L1_attn_bq, L1_attn_Wk, L1_attn_bk, L1_attn_Wv, L1_attn_bv, L1_attn_Wo, L1_attn_bo, L1_attn_g1, L1_attn_b1, L1_attn_W1, L1_attn_c1, L1_attn_W2, L1_attn_c2, L1_attn_g2, L1_attn_b2) + _L1_ffn_ref(xn, L1_ffn_gate_w, L1_ffn_gate_b, L1_ffn_w1, L1_ffn_b1, L1_ffn_w2, L1_ffn_b2)
    return x

_drawn_inputs = setup_inputs


def setup_inputs(seed=0):
    import zlib

    import numpy as np

    out = dict(_drawn_inputs(seed))
    spreads = {'L0_attn_conv_b': (0.0, 0.1),
     'L0_attn_D_param': (1.0, 0.2),
     'L0_attn_ln_gamma': (1.0, 0.2),
     'L0_attn_ln_beta': (0.0, 0.1),
     'L0_attn_b_gate': (0.0, 0.418),
     'L1_attn_bq': (0.0, 0.8),
     'L1_attn_bk': (0.0, 0.8),
     'L1_attn_bv': (0.0, 0.1),
     'L1_attn_bo': (0.0, 0.1),
     'L1_attn_g1': (1.0, 0.2),
     'L1_attn_b1': (0.0, 0.1),
     'L1_attn_c1': (0.0, 0.323),
     'L1_attn_c2': (0.0, 0.1),
     'L1_attn_g2': (1.0, 0.2),
     'L1_attn_b2': (0.0, 0.1)}
    factors = {'L0_attn_A_log': 7.231, 'L1_ffn_b1': 5.808, 'L1_ffn_b2': 4.597}
    for name, (base, spread) in spreads.items():
        noise = np.random.default_rng([zlib.crc32(name.encode()), seed]).standard_normal(out[name].shape)
        drawn = base * np.exp(spread * noise) if base else spread * noise
        out[name] = jnp.asarray(drawn.astype(out[name].dtype))
    for name, factor in factors.items():
        out[name] = (out[name] * factor).astype(out[name].dtype)
    return out
```

```python
from contextlib import ExitStack

import numpy as np

import concourse.bass as bass
from concourse import mybir

F32 = mybir.dt.float32
BF16 = mybir.dt.bfloat16
ALU = mybir.AluOpType
ACT = mybir.ActivationFunctionType
AXX = mybir.AxisListType.X

P = 128
BATCH, SEQ = 8, 512
TILES = SEQ // P
NT = BATCH * TILES
EPS = 1e-5
HEADS, HDIM, NSTATE, INNER, TAPS = 8, 32, 16, 256, 4
EXP0, TOP0, EDIM0 = 16, 4, 64
UPS = (2 + EXP0) * EDIM0 // P
AH, AHD, WIN = 16, 8, 32
BLOCKS = SEQ // WIN
GROUPS = 4
KEYS = 3 * WIN
FFN = 512
EXP1, EDIM1 = 8, 512

W0 = [("w_small0", HEADS + EXP0), ("w_up0", UPS * P), ("w_down0", UPS * P), ("w_zx", 4 * P),
      ("w_xbc", 3 * P), ("w_out", 4 * P), ("w_gate", 4 * P)]
C0 = [("conv_w", 3 * TAPS), ("conv_b", 3), ("gamma", 2), ("beta", 2), ("b_gate", 2)]
R0 = [("dt_bias", HEADS), ("a_log", HEADS), ("d_param", HEADS)]
W1 = [("w_small1", EXP1), ("wq", P), ("wk", P), ("wv", P), ("wo", P), ("w_f1", FFN), ("w_f2", FFN)]
C1 = [("bq", 1), ("bk", 1), ("bv", 1), ("c1", FFN // P)]
R1 = [("gate_b", EXP1), ("bo", P), ("g1", P), ("b1", P), ("c2", P), ("g2", P), ("b2", P)]


def columns(layout):
    at, out = 0, {}
    for name, width in layout:
        out[name] = (at, at + width)
        at += width
    return out, at


def wait(eng, sem, value):
    if isinstance(value, int) and value <= 0:
        return
    eng.wait_ge(sem, value)


def live(n, c, lag):
    return not isinstance(n, int) or 0 <= n * TILES + c - lag < NT


def back(n, c, lag):
    return n + (c - lag) // TILES, (c - lag) % TILES


def over_sequences(eng, body):
    body(0)
    with eng.Fori(1, BATCH) as n:
        body(n)


class Core:

    def __init__(self, nc, ctx):
        self.nc, self.ctx = nc, ctx

    def sb(self, name, shape, dt=F32):
        t = self.ctx.enter_context(self.nc.sbuf_tensor(name, shape, dt))
        return t

    def sem(self, name):
        return self.ctx.enter_context(self.nc.semaphore(name))


def norm_phase(nc, core, tag, x, x_loaded, w_small, n_small, n_exp, bias_row, logits, top8, xn_tokens):
    with ExitStack() as ctx:
        sb = lambda name, shape, dt=F32: ctx.enter_context(nc.sbuf_tensor(tag + name, shape, dt))
        sem = lambda name: ctx.enter_context(nc.semaphore(tag + name))
        stats = sb("stats", [P, TILES, 6])
        mean_var = sb("mean_var", [P, TILES, 2])
        var_eps = sb("var_eps", [P, TILES])
        rstd = sb("rstd", [P, TILES])
        xn = sb("xn", [P, TILES, P])
        xnT_tile = sb("xnT_tile", [P, TILES, P])
        small = sb("small", [P, TILES, n_small])
        top = sb("top", [P, TILES, 8])
        stats_done, mv_done, vareps_done, rstd_done = sem("stats_done"), sem("mv_done"), sem("vareps_done"), sem("rstd_done")
        xn_done, turned, xnT_done, small_mm, small_done, top_done = (
            sem("xn_done"), sem("turned"), sem("xnT_done"), sem("small_mm"), sem("small_done"), sem("top_done"))
        ps_turn = [core.bank[0], core.bank[1]]
        evac = 3 if xn_tokens is not None else 2
        ps_small = [core.bank[2], core.bank[3]]

        with nc.Block() as block:
            @block.vector
            def _(dve):
                def statistics(n):
                    for c in range(TILES):
                        if x_loaded is not None and c == 0:
                            if isinstance(n, int):
                                dve.wait_ge(x_loaded[0], 16)
                            else:
                                dve.wait_ge(x_loaded[1], 16 * (BATCH - 1))
                        nc.vector.bn_stats(stats[:, c, :], x[:, bass.ds((n * TILES + c) * P, P)]).then_inc(stats_done, 1)
                    dve.wait_ge(stats_done, TILES * n + TILES)
                    nc.vector.memset(core.spare[:, 0:1], 0.0)
                    for c in range(TILES):
                        nc.vector.bn_aggr(mean_var[:, c, :], stats[:, c, :]).then_inc(mv_done, 1)

                def normalise(n):
                    dve.wait_ge(rstd_done, n + 1)
                    for c in range(TILES):
                        t = n * TILES + c
                        wait(dve, turned, t - TILES + 1)
                        if xn_tokens is not None:
                            wait(dve, xnT_done, 3 * (t - TILES + 1))
                        nc.vector.tensor_scalar(xn[:, c, :], x[:, bass.ds(t * P, P)], mean_var[:, c, 0:1],
                                                rstd[:, c:c + 1], ALU.subtract, ALU.mult).then_inc(xn_done, 1)

                def router(n):
                    for c in range(TILES):
                        t = n * TILES + c
                        dve.wait_ge(small_mm, t + 1)
                        if bias_row is None:
                            nc.vector.tensor_copy(small[:, c, :], ps_small[c % 2][:, 0:n_small]).then_inc(small_done, 1)
                        else:
                            nc.vector.tensor_tensor(small[:, c, :], ps_small[c % 2][:, 0:n_small], bias_row,
                                                    ALU.add).then_inc(small_done, 1)
                    dve.wait_ge(small_done, TILES * n + TILES)
                    nc.vector.memset(core.spare[:, 0:1], 0.0)
                    for c in range(TILES):
                        nc.vector.max(top[:, c, :], small[:, c, 0:n_exp]).then_inc(top_done, 1)
                    dve.wait_ge(top_done, TILES * n + TILES)
                    nc.vector.tensor_copy(logits[:, bass.ds(n * TILES, TILES), :], small[:, :, :])
                    nc.vector.tensor_copy(top8[:, bass.ds(n * TILES, TILES), :], top[:, :, :])

                def sequence(n):
                    statistics(n)
                    if live(n, 0, 1):
                        router(n - 1)
                    normalise(n)
                dve.wait_ge(core.params_in, core.params_count)
                over_sequences(dve, sequence)
                router(BATCH - 1)

            @block.gpsimd
            def _(pool):
                def sequence(n):
                    pool.wait_ge(mv_done, TILES * n + TILES)
                    wait(pool, xn_done, TILES * n)
                    nc.gpsimd.tensor_tensor(var_eps[:, :], mean_var[:, :, 1], core.eps[:, 0:TILES], ALU.add).then_inc(vareps_done, 1)
                    pool.wait_ge(vareps_done, n + 1)
                    nc.gpsimd.tensor_tensor(rstd[:, :], var_eps[:, :], core.minus_half[:, 0:TILES], ALU.pow).then_inc(rstd_done, 1)
                pool.wait_ge(core.params_in, core.params_count)
                over_sequences(pool, sequence)

            @block.tensor
            def _(pe):
                def turn(n, c):
                    t = n * TILES + c
                    pe.wait_ge(xn_done, t + 1)
                    wait(pe, xnT_done, evac * (t - 1))
                    nc.tensor.transpose(ps_turn[c % 2][:, 0:P], xn[:, c, :], core.ident[:, :]).then_inc(turned, 1)

                def small_product(n, c):
                    t = n * TILES + c
                    pe.wait_ge(xnT_done, evac * (t + 1))
                    wait(pe, small_done, t - 1)
                    nc.tensor.matmul(ps_small[c % 2][:, 0:n_small], xnT_tile[:, c, :], w_small,
                                     start=True, stop=True).then_inc(small_mm, 1)

                def sequence(n):
                    for c in range(TILES):
                        if live(n, c, 1):
                            small_product(*back(n, c, 1))
                        turn(n, c)
                pe.wait_ge(core.params_in, core.params_count)
                over_sequences(pe, sequence)
                small_product(BATCH - 1, TILES - 1)

            @block.scalar
            def _(act):
                def sequence(n):
                    for c in range(TILES):
                        t = n * TILES + c
                        act.wait_ge(turned, t + 1)
                        wait(act, small_mm, t - TILES + 1)
                        nc.scalar.activation(xnT_tile[:, c, :], ps_turn[c % 2][:, 0:P], ACT.Copy).then_inc(xnT_done, 1)
                        nc.scalar.activation(core.xnT[:, bass.ds(t * P, P)], ps_turn[c % 2][:, 0:P], ACT.Copy).then_inc(xnT_done, 1)
                        if xn_tokens is not None:
                            nc.scalar.activation(xn_tokens[:, bass.ds(t * P, P)], xn[:, c, :], ACT.Copy).then_inc(xnT_done, 1)
                over_sequences(act, sequence)


def routing0_phase(nc, core, logits, top8, dt_bias, a_log):
    with ExitStack() as ctx:
        sb = lambda name, shape, dt=F32: ctx.enter_context(nc.sbuf_tensor("r0_" + name, shape, dt))
        sem = lambda name: ctx.enter_context(nc.semaphore("r0_" + name))
        shifted = sb("shifted", [P, NT, EXP0])
        above = sb("above", [P, NT, EXP0])
        equal = sb("equal", [P, NT, EXP0])
        order = sb("order", [P, NT, EXP0])
        total = sb("total", [P, NT])
        n_above = sb("n_above", [P, NT])
        pre = sb("pre", [P, NT, HEADS])
        small_exp = sb("small_exp", [P, NT, HEADS])
        one_plus = sb("one_plus", [P, NT, HEADS])
        log_1p = sb("log_1p", [P, NT, HEADS])
        ratio = sb("ratio", [P, NT, HEADS])
        decay = sb("decay", [P, NT, HEADS])
        a_exp = sb("a_exp", [P, HEADS])
        dve_step, a_ready, act_ready, decay_ready, sums_ready, sums_copied = (
            sem("dve_step"), sem("a_ready"), sem("act_ready"), sem("decay_ready"), sem("sums_ready"), sem("sums_copied"))
        abs_done = sem("abs_done")
        E = [P, NT, EXP0]
        H = [P, NT, HEADS]
        lg = logits[:, :, 0:EXP0]
        largest = top8[:, :, 0:1].to_broadcast(E)
        fourth = top8[:, :, TOP0 - 1:TOP0].to_broadcast(E)
        flat = lambda t: t[:, :, :].rearrange("p t h -> p (t h)")

        with nc.Block() as block:
            @block.vector
            def _(dve):
                count = [0]

                def step(ins):
                    count[0] += 1
                    ins.then_inc(dve_step, 1)
                    dve.wait_ge(dve_step, count[0])
                step(nc.vector.tensor_tensor(pre[:, :, :], logits[:, :, EXP0:EXP0 + HEADS],
                                             dt_bias.unsqueeze(1).to_broadcast(H), ALU.add))
                step(nc.vector.tensor_tensor(shifted[:, :, :], lg, largest, ALU.subtract))
                step(nc.vector.tensor_tensor(above[:, :, :], lg, fourth, ALU.is_gt))
                step(nc.vector.tensor_tensor(equal[:, :, :], lg, fourth, ALU.is_equal))
                step(nc.vector.tensor_reduce(n_above[:, :], above[:, :, :], AXX, ALU.add))
                step(nc.vector.tensor_tensor_scan(flat(order), core.restart[:, 0:NT * EXP0], flat(equal), 0.0,
                                                  ALU.mult, ALU.add))
                step(nc.vector.tensor_tensor(order[:, :, :], order[:, :, :], n_above[:, :].unsqueeze(2).to_broadcast(E), ALU.add))
                step(nc.vector.scalar_tensor_tensor(flat(equal), flat(order), float(TOP0), flat(equal), ALU.is_le, ALU.mult))
                step(nc.vector.tensor_tensor(above[:, :, :], above[:, :, :], equal[:, :, :], ALU.add))
                dve.wait_ge(act_ready, 2)
                step(nc.vector.tensor_scalar(one_plus[:, :, :], small_exp[:, :, :], 1.0, None, ALU.add))
                dve.wait_ge(act_ready, 3)
                step(nc.vector.tensor_reduce(total[:, :], shifted[:, :, :], AXX, ALU.add))
                step(nc.vector.reciprocal(total[:, :], total[:, :]))
                step(nc.vector.tensor_tensor(shifted[:, :, :], shifted[:, :, :], total[:, :].unsqueeze(2).to_broadcast(E), ALU.mult))
                step(nc.vector.tensor_tensor(core.gates0[:, :, :], shifted[:, :, :], above[:, :, :], ALU.mult))
                step(nc.vector.tensor_scalar(ratio[:, :, :], one_plus[:, :, :], -1.0, None, ALU.add))
                step(nc.vector.scalar_tensor_tensor(flat(decay), flat(ratio), 0.0, flat(small_exp), ALU.is_equal, ALU.mult))
                step(nc.vector.tensor_scalar(ratio[:, :, :], ratio[:, :, :], 1e-30, None, ALU.max))
                step(nc.vector.reciprocal(ratio[:, :, :], ratio[:, :, :]))
                step(nc.vector.tensor_tensor(ratio[:, :, :], ratio[:, :, :], small_exp[:, :, :], ALU.mult))
                dve.wait_ge(act_ready, 4)
                step(nc.vector.tensor_tensor(log_1p[:, :, :], log_1p[:, :, :], ratio[:, :, :], ALU.mult))
                step(nc.vector.tensor_tensor(log_1p[:, :, :], log_1p[:, :, :], decay[:, :, :], ALU.add))
                step(nc.vector.scalar_tensor_tensor(flat(core.dt), flat(pre), 0.0, flat(log_1p), ALU.max, ALU.add))
                step(nc.vector.tensor_scalar(a_exp[:, :], a_exp[:, :], -1.0, None, ALU.mult))
                nc.vector.tensor_tensor(decay[:, :, :], core.dt[:, :, :], a_exp[:, :].unsqueeze(1).to_broadcast(H),
                                        ALU.mult).then_inc(decay_ready, 1)
                dve.wait_ge(sums_ready, 2)
                nc.vector.tensor_copy(flat(core.cum), core.bank[0][:, 0:NT * HEADS]).then_inc(sums_copied, 1)
                dve.wait_ge(sums_copied, 1)
                nc.vector.tensor_tensor(flat(core.w_end), core.bank[1][:, 0:NT * HEADS], flat(core.cum),
                                        ALU.subtract).then_inc(sums_copied, 1)
                dve.wait_ge(act_ready, 7)
                nc.vector.tensor_tensor(core.w_end[:, :, :], core.w_end[:, :, :], core.dt[:, :, :], ALU.mult)

            @block.scalar
            def _(act):
                act.wait_ge(dve_step, 1)
                nc.scalar.activation(one_plus[:, :, :], pre[:, :, :], ACT.Abs).then_inc(abs_done, 1)
                act.wait_ge(abs_done, 1)
                nc.scalar.activation(small_exp[:, :, :], one_plus[:, :, :], ACT.Exp, scale=-1.0).then_inc(act_ready, 1)
                nc.scalar.activation(a_exp[:, :], a_log, ACT.Exp).then_inc(act_ready, 1)
                act.wait_ge(dve_step, 2)
                nc.scalar.activation(shifted[:, :, :], shifted[:, :, :], ACT.Exp).then_inc(act_ready, 1)
                act.wait_ge(dve_step, 10)
                nc.scalar.activation(log_1p[:, :, :], one_plus[:, :, :], ACT.Ln).then_inc(act_ready, 1)
                act.wait_ge(sums_copied, 2)
                nc.scalar.activation(core.exp_cum[:, :, :], core.cum[:, :, :], ACT.Exp).then_inc(act_ready, 1)
                nc.scalar.activation(flat(core.exp_total), core.bank[1][:, 0:NT * HEADS], ACT.Exp).then_inc(act_ready, 1)
                nc.scalar.activation(core.w_end[:, :, :], core.w_end[:, :, :], ACT.Exp).then_inc(act_ready, 1)

            @block.tensor
            def _(pe):
                pe.wait_ge(decay_ready, 1)
                nc.tensor.matmul(core.bank[0][:, 0:NT * HEADS], core.upper[:, :], flat(decay), start=True, stop=True).then_inc(sums_ready, 1)
                nc.tensor.matmul(core.bank[1][:, 0:NT * HEADS], core.ones[:, :], flat(decay), start=True, stop=True).then_inc(sums_ready, 1)


def experts0_phase(nc, core, w_up, w_down):
    with ExitStack() as ctx:
        sb = lambda name, shape, dt=F32: ctx.enter_context(nc.sbuf_tensor("m0_" + name, shape, dt))
        sem = lambda name: ctx.enter_context(nc.semaphore("m0_" + name))
        hidden = sb("hidden", [P, 2, SEQ])
        gated = sb("gated", [P, UPS, SEQ])
        gates = sb("gates", [P, 2, TILES, P])
        up_done, gelu_done, gates_in, spread_done, gated_done, down_done, added = (
            sem("up_done"), sem("gelu_done"), sem("gates_in"), sem("spread_done"), sem("gated_done"),
            sem("down_done"), sem("added"))
        ps_up = core.bank[0:3]
        ps_spread = core.bank[3:5]
        ps_down = core.bank[5]
        ROUTED = UPS - 1

        with nc.Block() as block:
            @block.tensor
            def _(pe):
                def up(n, m):
                    wait(pe, gelu_done, n * UPS + m - 2)
                    nc.tensor.matmul(ps_up[m % 3][:, :], w_up[:, m * P:(m + 1) * P], core.xnT[:, bass.ds(n * SEQ, SEQ)],
                                     start=True, stop=True).then_inc(up_done, 1)

                def spread(n, m):
                    pe.wait_ge(gates_in, n * ROUTED + m)
                    wait(pe, gated_done, n * ROUTED + m - 2)
                    for c in range(TILES):
                        last = nc.tensor.transpose(ps_spread[(m - 1) % 2][:, c * P:(c + 1) * P],
                                                   gates[:, (m - 1) % 2, c, :], core.ident[:, :])
                    last.then_inc(spread_done, 1)

                def down(n, m):
                    if m == 0:
                        pe.wait_ge(gelu_done, n * UPS + 1)
                        wait(pe, added, n)
                    else:
                        pe.wait_ge(gated_done, n * ROUTED + m)
                    for c in range(TILES):
                        last = nc.tensor.matmul(ps_down[:, c * P:(c + 1) * P], gated[:, m, c * P:(c + 1) * P],
                                                w_down[:, m * P:(m + 1) * P], start=(m == 0 and c == 0),
                                                stop=(m == UPS - 1), skip_group_check=True)
                    last.then_inc(down_done, 1)

                def sequence(n):
                    for m in range(UPS):
                        up(n, m)
                        if m:
                            spread(n, m)
                        if m >= 2:
                            down(n, m - 2)
                        elif live(n, 0, 1):
                            down(n - 1, UPS + m - 2)
                over_sequences(pe, sequence)
                down(BATCH - 1, UPS - 2)
                down(BATCH - 1, UPS - 1)

            @block.scalar
            def _(act):
                def sequence(n):
                    for m in range(UPS):
                        act.wait_ge(up_done, n * UPS + m + 1)
                        if m == 0:
                            wait(act, down_done, (n - 1) * UPS + 1)
                            out = gated[:, 0, :]
                        else:
                            wait(act, gated_done, n * ROUTED + m - 2)
                            out = hidden[:, (m - 1) % 2, :]
                        nc.scalar.activation(out, ps_up[m % 3][:, :], ACT.Gelu).then_inc(gelu_done, 1)
                over_sequences(act, sequence)

            @block.gpsimd
            def _(pool):
                def sequence(n):
                    for m in range(1, UPS):
                        wait(pool, spread_done, n * ROUTED + m - 2)
                        nc.gpsimd.tensor_copy(
                            gates[:, (m - 1) % 2, :, :].rearrange("p c (e u) -> p c e u", e=2),
                            core.gates0[:, bass.ds(n * TILES, TILES), 2 * (m - 1):2 * m].unsqueeze(3).to_broadcast(
                                [P, TILES, 2, EDIM0])).then_inc(gates_in, 1)
                over_sequences(pool, sequence)

            @block.vector
            def _(dve):
                def add(n):
                    dve.wait_ge(down_done, (n + 1) * UPS)
                    here = core.x[:, bass.ds(n * SEQ, SEQ)]
                    nc.vector.tensor_tensor(here, ps_down[:, :], here, ALU.add).then_inc(added, 1)

                def sequence(n):
                    for m in range(1, UPS):
                        dve.wait_ge(gelu_done, n * UPS + m + 1)
                        dve.wait_ge(spread_done, n * ROUTED + m)
                        wait(dve, down_done, (n - 1) * UPS + m + 1)
                        nc.vector.tensor_tensor(gated[:, m, :], ps_spread[(m - 1) % 2][:, :], hidden[:, (m - 1) % 2, :],
                                                ALU.mult).then_inc(gated_done, 1)
                        if m == 1 and live(n, 0, 1):
                            add(n - 1)
                over_sequences(dve, sequence)
                add(BATCH - 1)


def skip_phase(nc, core, w_zx, w_out):
    with ExitStack() as ctx:
        sb = lambda name, shape, dt=F32: ctx.enter_context(nc.sbuf_tensor("sk_" + name, shape, dt))
        sem = lambda name: ctx.enter_context(nc.semaphore("sk_" + name))
        silu = sb("silu", [P, 2, SEQ])
        skip = sb("skip", [P, 2, SEQ])
        in_done, silu_done, skip_done, out_done, added = (
            sem("in_done"), sem("silu_done"), sem("skip_done"), sem("out_done"), sem("added"))
        ps_in = core.bank[0:4]
        ps_out = core.bank[4]
        with nc.Block() as block:
            @block.tensor
            def _(pe):
                def project(n):
                    for u in range(4):
                        k = u // 2
                        wait(pe, silu_done if u % 2 == 0 else skip_done, 2 * (n - 1) + k + 1)
                        nc.tensor.matmul(ps_in[u][:, :], w_zx[:, u * P:(u + 1) * P], core.xnT[:, bass.ds(n * SEQ, SEQ)],
                                         start=True, stop=True).then_inc(in_done, 1)

                def out(n):
                    pe.wait_ge(skip_done, 2 * n + 2)
                    wait(pe, added, n)
                    for k in range(2):
                        for c in range(TILES):
                            last = nc.tensor.matmul(ps_out[:, c * P:(c + 1) * P], skip[:, k, c * P:(c + 1) * P],
                                                    w_out[:, k * P:(k + 1) * P], start=(k == 0 and c == 0), stop=(k == 1),
                                                    skip_group_check=True)
                    last.then_inc(out_done, 1)

                def sequence(n):
                    project(n)
                    if live(n, 0, 1):
                        out(n - 1)
                over_sequences(pe, sequence)
                out(BATCH - 1)

            @block.scalar
            def _(act):
                def sequence(n):
                    for k in range(2):
                        act.wait_ge(in_done, 4 * n + 2 * k + 1)
                        wait(act, skip_done, 2 * (n - 1) + k + 1)
                        nc.scalar.activation(silu[:, k, :], ps_in[2 * k][:, :], ACT.Silu).then_inc(silu_done, 1)
                over_sequences(act, sequence)

            @block.vector
            def _(dve):
                def add(n):
                    dve.wait_ge(out_done, n + 1)
                    here = core.x[:, bass.ds(n * SEQ, SEQ)]
                    nc.vector.tensor_tensor(here, ps_out[:, :], here, ALU.add).then_inc(added, 1)

                def sequence(n):
                    wait(dve, out_done, n)
                    for k in range(2):
                        dve.wait_ge(silu_done, 2 * n + k + 1)
                        dve.wait_ge(in_done, 4 * n + 2 * k + 2)
                        nc.vector.tensor_tensor(skip[:, k, :], ps_in[2 * k + 1][:, :], silu[:, k, :], ALU.mult).then_inc(skip_done, 1)
                    if live(n, 0, 1):
                        add(n - 1)
                over_sequences(dve, sequence)
                add(BATCH - 1)


def conv_phase(nc, core, w_xbc, conv_w, conv_b):
    with ExitStack() as ctx:
        sb = lambda name, shape, dt=F32: ctx.enter_context(nc.sbuf_tensor("cv_" + name, shape, dt))
        sem = lambda name: ctx.enter_context(nc.semaphore("cv_" + name))
        PAD = TAPS - 1
        padded = sb("padded", [P, 3, PAD + SEQ])
        summed = sb("summed", [P, 3, SEQ])
        x_act = sb("x_act", [P, 2, SEQ])
        b_act = sb("b_act", [NSTATE, SEQ])
        ROWS = [P, P, 48]
        pads_zero, in_done, first_tap, taps_done, silu_done, turned, kept = (
            sem("pads_zero"), sem("in_done"), sem("first_tap"), sem("taps_done"), sem("silu_done"), sem("turned"), sem("kept"))
        ps_in = core.bank[0:3]
        ps_turn = core.bank[3:5]
        with nc.Block() as block:
            @block.tensor
            def _(pe):
                def project(n):
                    for m in range(3):
                        wait(pe, first_tap, 3 * (n - 1) + m + 1)
                        nc.tensor.matmul(ps_in[m][:, :], w_xbc[:, m * P:(m + 1) * P],
                                         core.xnT[:, bass.ds(n * SEQ, SEQ)], start=True, stop=True).then_inc(in_done, 1)

                def turn(n):
                    pe.wait_ge(silu_done, 3 * n + 3)
                    for c in range(TILES):
                        t = n * TILES + c
                        pe.wait_ge(kept, t + 1)
                        for k in range(2):
                            nc.tensor.transpose(ps_turn[c % 2][:, k * P:(k + 1) * P], x_act[:, k, c * P:(c + 1) * P], core.ident[:, :])
                        nc.tensor.transpose(ps_turn[c % 2][:, INNER:INNER + NSTATE], b_act[:, c * P:(c + 1) * P],
                                            core.ident[0:NSTATE, 0:NSTATE]).then_inc(turned, 1)

                def sequence(n):
                    project(n)
                    if live(n, 0, 1):
                        turn(n - 1)
                over_sequences(pe, sequence)
                turn(BATCH - 1)

            @block.scalar
            def _(act):
                def sequence(n):
                    for m in range(3):
                        r = ROWS[m]
                        act.wait_ge(in_done, 3 * n + m + 1)
                        wait(act, taps_done, 9 * (n - 1) + 3 * m + 3)
                        wait(act, silu_done, 3 * (n - 1) + m + 1)
                        nc.scalar.activation(padded[0:r, m, PAD:], ps_in[m][0:r, :], ACT.Copy)
                        nc.scalar.activation(summed[0:r, m, :], ps_in[m][0:r, :], ACT.Identity, bias=conv_b[0:r, m:m + 1],
                                             scale=conv_w[0:r, TAPS * m + PAD:TAPS * m + TAPS]).then_inc(first_tap, 1)
                    wait(act, turned, TILES * n)
                    for m in range(2):
                        act.wait_ge(taps_done, 9 * n + 3 * m + 3)
                        nc.scalar.activation(x_act[:, m, :], summed[:, m, :], ACT.Silu).then_inc(silu_done, 1)
                    act.wait_ge(taps_done, 9 * n + 9)
                    nc.scalar.activation(b_act[:, :], summed[0:NSTATE, 2, :], ACT.Silu)
                    nc.scalar.activation(core.b_rows[:, 0, bass.ds(n * SEQ, SEQ)], summed[0:NSTATE, 2, :], ACT.Silu)
                    nc.scalar.activation(core.b_rows[:, 1, bass.ds(n * SEQ, SEQ)], summed[32:32 + NSTATE, 2, :],
                                         ACT.Silu).then_inc(silu_done, 1)
                over_sequences(act, sequence)

            @block.vector
            def _(dve):
                dve.sem_inc(kept, 2)
                nc.vector.memset(padded[:, :, 0:PAD], 0.0).then_inc(pads_zero, 1)
                dve.wait_ge(pads_zero, 1)

                def keep(n):
                    for c in range(TILES):
                        t = n * TILES + c
                        dve.wait_ge(turned, t + 1)
                        nc.vector.tensor_copy(core.x_tokens[:, bass.ds(t, 1), :].rearrange("p o c -> p (o c)"),
                                              ps_turn[c % 2][:, 0:INNER + NSTATE]).then_inc(kept, 1)

                def sequence(n):
                    for m in range(3):
                        r = ROWS[m]
                        dve.wait_ge(first_tap, 3 * n + m + 1)
                        for k in range(PAD):
                            if k:
                                dve.wait_ge(taps_done, 9 * n + 3 * m + k)
                            nc.vector.scalar_tensor_tensor(summed[0:r, m, :], padded[0:r, m, k:k + SEQ],
                                                           conv_w[0:r, TAPS * m + k:TAPS * m + k + 1], summed[0:r, m, :],
                                                           ALU.mult, ALU.add).then_inc(taps_done, 1)
                    if live(n, 0, 1):
                        keep(n - 1)
                over_sequences(dve, sequence)
                keep(BATCH - 1)


def ssm_phase(nc, core, w_gate, w_out, gamma, beta, b_gate, d_param):
    with ExitStack() as ctx:
        sb = lambda name, shape, dt=F32: ctx.enter_context(nc.sbuf_tensor("ss_" + name, shape, dt))
        sem = lambda name: ctx.enter_context(nc.semaphore("ss_" + name))
        cum_local = sb("cum_local", [P, 2, HEADS])
        b_local = sb("b_local", [NSTATE, 2, P])
        c_local = sb("c_local", [NSTATE, 2, P])
        b_tokens = sb("b_tokens", [P, 2, NSTATE])
        x_dt = sb("x_dt", [P, 2, INNER])
        x_end = sb("x_end", [P, 2, INNER])
        x_d = sb("x_d", [P, 2, INNER])
        mix = sb("mix", [P, HEADS, P])
        bc = sb("bc", [P, P])
        weights = sb("weights", [P, HEADS, P])
        state = sb("state", [NSTATE, 2, INNER])
        y = sb("y", [P, 2, INNER])
        stats = sb("stats", [P, 2, 6])
        mean_var = sb("mean_var", [P, 2, 2])
        var_eps = sb("var_eps", [P, 2])
        rstd = sb("rstd", [P, 2])
        y_norm = sb("y_norm", [P, 2, INNER])
        yT = sb("yT", [P, 2, SEQ])
        tanh = sb("tanh", [P, 2, SEQ])
        half_bias = sb("half_bias", [P, 2])
        half_out = sb("half_out", [P, 2 * P])
        names = ("halves_ready local_ready spread_done diff_done exp_done weights_done bc_mm bc_done state_mm state_done "
                 "y_mm y_free y_done stats_done mv_done vareps_done rstd_done norm_done turned yT_done gate_mm tanh_done "
                 "gated_done out_done added inter_done scaled_done")
        s = type("Sems", (), {k: sem(k) for k in names.split()})
        ps_spread = core.bank[0:2]
        ps_bc, ps_state, ps_y, ps_turn = core.bank[2], core.bank[3], core.bank[4], core.bank[5]
        ps_gate = core.bank[6:8]
        ps_out = core.bank[6]
        HALF = HEADS // 2
        COPIES = 7
        tile = lambda n, c: n * TILES + c
        per_head = lambda t: t[:, :].unsqueeze(2)

        with nc.Block() as block:
            @block.gpsimd
            def _(pool):
                def prepare(n, c):
                    t = tile(n, c)
                    b = c % 2
                    columns_ = bass.ds(t * P, P)
                    of_tile = lambda a: a[:, bass.ds(t, 1), :].rearrange("p o h -> p (o h)")
                    heads = lambda a: a.unsqueeze(2).to_broadcast([P, HEADS, HDIM])
                    x_t = core.x_tokens[:, bass.ds(t, 1), 0:INNER].rearrange("p o (h d) -> p (o h) d", h=HEADS)
                    wait(pool, s.spread_done, 2 * (t - 1))
                    nc.gpsimd.tensor_copy(cum_local[:, b, :], of_tile(core.cum)).then_inc(s.local_ready, 1)
                    wait(pool, s.y_mm, t - 1)
                    wait(pool, s.y_done, t - 1)
                    nc.gpsimd.tensor_copy(b_local[:, b, :], core.b_rows[:, 0, columns_]).then_inc(s.local_ready, 1)
                    nc.gpsimd.tensor_copy(c_local[:, b, :], core.b_rows[:, 1, columns_]).then_inc(s.local_ready, 1)
                    nc.gpsimd.tensor_copy(b_tokens[:, b, :], core.x_tokens[:, bass.ds(t, 1), INNER:INNER + NSTATE].rearrange(
                        "p o c -> p (o c)")).then_inc(s.local_ready, 1)
                    nc.gpsimd.tensor_tensor(x_dt[:, b, :].rearrange("p (h d) -> p h d", h=HEADS), x_t,
                                            heads(of_tile(core.dt)), ALU.mult).then_inc(s.local_ready, 1)
                    nc.gpsimd.tensor_tensor(x_end[:, b, :].rearrange("p (h d) -> p h d", h=HEADS), x_t,
                                            heads(of_tile(core.w_end)), ALU.mult).then_inc(s.local_ready, 1)
                    nc.gpsimd.tensor_tensor(x_d[:, b, :].rearrange("p (h d) -> p h d", h=HEADS), x_t,
                                            heads(d_param), ALU.mult).then_inc(s.local_ready, 1)

                def root(n, c):
                    t = tile(n, c)
                    b = c % 2
                    pool.wait_ge(s.mv_done, t + 1)
                    nc.gpsimd.tensor_tensor(var_eps[:, b:b + 1], mean_var[:, b, 1:2], core.eps[:, 0:1], ALU.add).then_inc(s.vareps_done, 1)
                    wait(pool, s.norm_done, t - 1)
                    pool.wait_ge(s.vareps_done, t + 1)
                    nc.gpsimd.tensor_tensor(rstd[:, b:b + 1], var_eps[:, b:b + 1], core.minus_half[:, 0:1], ALU.pow).then_inc(s.rstd_done, 1)

                def steps(n):
                    for c in range(TILES):
                        if live(n, c, 0):
                            prepare(n, c)
                        if live(n, c, 2):
                            root(*back(n, c, 2))
                over_sequences(pool, steps)
                steps(BATCH)

            @block.tensor
            def _(pe):
                def chunk(n, c):
                    t = tile(n, c)
                    b = c % 2
                    pe.wait_ge(s.local_ready, COPIES * (t + 1))
                    for half in range(2):
                        wait(pe, s.diff_done, 2 * (t - 1) + half + 1)
                        for h in range(HALF):
                            last = nc.tensor.transpose(ps_spread[half][:, h * P:(h + 1) * P],
                                                       cum_local[:, b, half * HALF + h:half * HALF + h + 1].to_broadcast([P, P]),
                                                       core.ident[:, :])
                        last.then_inc(s.spread_done, 1)
                    wait(pe, s.bc_done, t)
                    nc.tensor.matmul(ps_bc[:, 0:P], b_local[:, b, :], c_local[:, b, :], start=True, stop=True).then_inc(s.bc_mm, 1)
                    if c < TILES - 1:
                        wait(pe, s.state_done, 3 * n + c)
                        nc.tensor.matmul(ps_state[0:NSTATE, 0:INNER], b_tokens[:, b, :], x_end[:, b, :],
                                         start=True, stop=True).then_inc(s.state_mm, 1)

                def outputs(n, c):
                    t = tile(n, c)
                    b = c % 2
                    pe.wait_ge(s.weights_done, 2 * t + 2)
                    wait(pe, s.y_free, t)
                    if c:
                        pe.wait_ge(s.state_done, 3 * n + c)
                        nc.tensor.matmul(ps_y[:, INNER:2 * INNER], c_local[:, b, :], state[:, b, :], start=True, stop=True)
                    for h in range(HEADS):
                        last = nc.tensor.matmul(ps_y[:, h * HDIM:(h + 1) * HDIM], weights[:, h, :],
                                                x_dt[:, b, h * HDIM:(h + 1) * HDIM], start=True, stop=True)
                    last.then_inc(s.y_mm, 1)

                def turn(n, c):
                    t = tile(n, c)
                    pe.wait_ge(s.norm_done, t + 1)
                    wait(pe, s.yT_done, 2 * t)
                    for k in range(2):
                        last = nc.tensor.transpose(ps_turn[:, k * P:(k + 1) * P], y_norm[:, c % 2, k * P:(k + 1) * P], core.ident[:, :])
                    last.then_inc(s.turned, 1)

                def gate(n):
                    pe.wait_ge(s.yT_done, 2 * TILES * (n + 1))
                    pe.wait_ge(s.added, n + 1)
                    for m in range(2):
                        for k in range(2):
                            last = nc.tensor.matmul(ps_gate[m][:, :], w_gate[:, (2 * k + m) * P:(2 * k + m + 1) * P], yT[:, k, :],
                                                    start=(k == 0), stop=(k == 1))
                        last.then_inc(s.gate_mm, 1)

                def out(n):
                    pe.wait_ge(s.gated_done, 2 * n + 2)
                    for k in range(2):
                        for c in range(TILES):
                            last = nc.tensor.matmul(ps_out[:, c * P:(c + 1) * P], tanh[:, k, c * P:(c + 1) * P],
                                                    half_out[:, k * P:(k + 1) * P], start=(k == 0 and c == 0), stop=(k == 1),
                                                    skip_group_check=True)
                    last.then_inc(s.out_done, 1)

                def steps(n):
                    for c in range(TILES):
                        if live(n, c, 0):
                            chunk(n, c)
                        ready = c == TILES - 1 and live(n, 0, 1)
                        if ready:
                            gate(n - 1)
                        if live(n, c, 1):
                            outputs(*back(n, c, 1))
                        if ready:
                            out(n - 1)
                        if live(n, c, 3):
                            turn(*back(n, c, 3))
                pe.sem_inc(s.out_done, 1)
                pe.wait_ge(s.halves_ready, 2)
                over_sequences(pe, steps)
                steps(BATCH)

            @block.scalar
            def _(act):
                def exponentials(n, c):
                    t = tile(n, c)
                    for half in range(2):
                        act.wait_ge(s.diff_done, 2 * t + half + 1)
                        here = mix[:, half * HALF:(half + 1) * HALF, :]
                        nc.scalar.activation(here, here, ACT.Exp).then_inc(s.exp_done, 1)

                def keep(n, c):
                    t = tile(n, c)
                    act.wait_ge(s.turned, t + 1)
                    if c == 0:
                        wait(act, s.gated_done, 2 * n)
                    for k in range(2):
                        nc.scalar.activation(yT[:, k, c * P:(c + 1) * P], ps_turn[:, k * P:(k + 1) * P], ACT.Identity,
                                             bias=beta[:, k:k + 1], scale=gamma[:, k:k + 1]).then_inc(s.yT_done, 1)

                def squash(n):
                    act.wait_ge(s.out_done, n + 1)
                    for m in range(2):
                        act.wait_ge(s.gate_mm, 2 * n + m + 1)
                        nc.scalar.activation(tanh[:, m, :], ps_gate[m][:, :], ACT.Tanh, bias=half_bias[:, m:m + 1],
                                             scale=0.5).then_inc(s.tanh_done, 1)

                def steps(n):
                    for c in range(TILES):
                        if live(n, c, 0):
                            exponentials(n, c)
                        if c == TILES - 1 and live(n, 0, 1):
                            squash(n - 1)
                        if live(n, c, 3):
                            keep(*back(n, c, 3))
                act.wait_ge(s.halves_ready, 2)
                over_sequences(act, steps)
                steps(BATCH)

            @block.vector
            def _(dve):
                dve.sem_inc(s.added, 1)
                nc.vector.tensor_scalar(half_bias[:, :], b_gate, 0.5, None, ALU.mult).then_inc(s.halves_ready, 1)
                nc.vector.tensor_scalar(half_out[:, :], w_out[:, 2 * P:4 * P], 0.5, None, ALU.mult).then_inc(s.halves_ready, 1)

                def differences(n, c):
                    t = tile(n, c)
                    for half in range(2):
                        wait(dve, s.weights_done, 2 * (t - 1) + half + 1)
                        dve.wait_ge(s.spread_done, 2 * t + half + 1)
                        here = core.cum[:, bass.ds(t, 1), half * HALF:(half + 1) * HALF].rearrange("p o h -> p (o h)")
                        nc.vector.tensor_tensor(mix[:, half * HALF:(half + 1) * HALF, :],
                                                ps_spread[half][:, :].rearrange("p (h t) -> p h t", h=HALF),
                                                here.unsqueeze(2).to_broadcast([P, HALF, P]), ALU.subtract).then_inc(s.diff_done, 1)
                    wait(dve, s.weights_done, 2 * t)
                    dve.wait_ge(s.bc_mm, t + 1)
                    nc.vector.tensor_tensor(bc[:, :], ps_bc[:, 0:P], core.upper[:, :], ALU.mult).then_inc(s.bc_done, 1)

                def update_state(n, c):
                    old, new = state[:, c % 2, :], state[:, (c + 1) % 2, :]
                    dve.wait_ge(s.state_mm, 3 * n + c + 1)
                    wait(dve, s.y_mm, tile(n, c))
                    if c == 0:
                        nc.vector.tensor_copy(new, ps_state[0:NSTATE, 0:INNER]).then_inc(s.state_done, 1)
                        return
                    fade = core.exp_total[0:NSTATE, bass.ds(tile(n, c), 1), :].rearrange("p o h -> p (o h)")
                    nc.vector.tensor_tensor(new.rearrange("p (h d) -> p h d", h=HEADS), old.rearrange("p (h d) -> p h d", h=HEADS),
                                            fade.unsqueeze(2).to_broadcast([NSTATE, HEADS, HDIM]), ALU.mult).then_inc(s.scaled_done, 1)
                    dve.wait_ge(s.scaled_done, 2 * n + c)
                    nc.vector.tensor_tensor(new, ps_state[0:NSTATE, 0:INNER], new, ALU.add).then_inc(s.state_done, 1)

                def finish(n, c):
                    t = tile(n, c)
                    b = c % 2
                    here = y[:, b, :]
                    wait(dve, s.norm_done, t - 1)
                    dve.wait_ge(s.y_mm, t + 1)
                    dve.wait_ge(s.local_ready, COPIES * (t + 1))
                    if c:
                        fade = core.exp_cum[:, bass.ds(t, 1), :].rearrange("p o h -> p (o h)")
                        nc.vector.tensor_tensor(here.rearrange("p (h d) -> p h d", h=HEADS),
                                                ps_y[:, INNER:2 * INNER].rearrange("p (h d) -> p h d", h=HEADS),
                                                fade.unsqueeze(2).to_broadcast([P, HEADS, HDIM]), ALU.mult).then_inc(s.inter_done, 1)
                        dve.wait_ge(s.inter_done, 6 * n + 2 * c - 1)
                        nc.vector.tensor_tensor(here, here, x_d[:, b, :], ALU.add).then_inc(s.inter_done, 1)
                        dve.wait_ge(s.inter_done, 6 * n + 2 * c)
                        nc.vector.tensor_tensor(here, ps_y[:, 0:INNER], here, ALU.add).then_inc(s.y_free, 1)
                    else:
                        nc.vector.tensor_tensor(here, ps_y[:, 0:INNER], x_d[:, b, :], ALU.add).then_inc(s.y_free, 1)
                    dve.wait_ge(s.y_free, t + 1)
                    nc.vector.bn_stats(stats[:, b, :], here).then_inc(s.y_done, 1)
                    dve.wait_ge(s.y_done, t + 1)
                    nc.vector.memset(core.spare[:, 0:1], 0.0)
                    nc.vector.bn_aggr(mean_var[:, b, :], stats[:, b, :]).then_inc(s.mv_done, 1)

                def weigh(n, c):
                    t = tile(n, c)
                    dve.wait_ge(s.bc_done, t + 1)
                    wait(dve, s.y_mm, t)
                    for half in range(2):
                        dve.wait_ge(s.exp_done, 2 * t + half + 1)
                        nc.vector.scalar_tensor_tensor(weights[:, half * HALF:(half + 1) * HALF, :],
                                                       mix[:, half * HALF:(half + 1) * HALF, :], 1.0,
                                                       bc[:, :].unsqueeze(1).to_broadcast([P, HALF, P]),
                                                       ALU.min, ALU.mult).then_inc(s.weights_done, 1)

                def normalise(n, c):
                    t = tile(n, c)
                    b = c % 2
                    dve.wait_ge(s.rstd_done, t + 1)
                    wait(dve, s.turned, t - 1)
                    nc.vector.tensor_scalar(y_norm[:, b, :], y[:, b, :], mean_var[:, b, 0:1], rstd[:, b:b + 1],
                                            ALU.subtract, ALU.mult).then_inc(s.norm_done, 1)

                def apply_gate(n):
                    for m in range(2):
                        dve.wait_ge(s.tanh_done, 2 * n + m + 1)
                        nc.vector.scalar_tensor_tensor(tanh[:, m, :], tanh[:, m, :], 1.0, yT[:, m, :],
                                                       ALU.add, ALU.mult).then_inc(s.gated_done, 1)

                def add(n):
                    dve.wait_ge(s.out_done, n + 2)
                    here = core.x[:, bass.ds(n * SEQ, SEQ)]
                    nc.vector.tensor_tensor(here, ps_out[:, :], here, ALU.add).then_inc(s.added, 1)

                def steps(n):
                    for c in range(TILES):
                        if live(n, c, 0):
                            differences(n, c)
                            if c < TILES - 1:
                                update_state(n, c)
                        ready = c == TILES - 1 and live(n, 0, 1)
                        if ready:
                            apply_gate(n - 1)
                        if live(n, c, 1):
                            finish(*back(n, c, 1))
                        if live(n, c, 0):
                            weigh(n, c)
                        if live(n, c, 2):
                            normalise(*back(n, c, 2))
                        if ready:
                            add(n - 1)
                dve.wait_ge(s.halves_ready, 2)
                over_sequences(dve, steps)
                steps(BATCH)


def attention_phase(nc, core, wq, wk, wv, bq, bk, bv, head_mask, bf_consts):
    with ExitStack() as ctx:
        sb = lambda name, shape, dt=F32: ctx.enter_context(nc.sbuf_tensor("at_" + name, shape, dt))
        sem = lambda name: ctx.enter_context(nc.semaphore("at_" + name))
        STEPS = TILES * GROUPS
        BT = P // WIN
        x_win = sb("x_win", [P, WIN + SEQ + WIN])
        kT = sb("kT", [P, WIN + SEQ + WIN])
        q_spread = sb("q_spread", [P, BLOCKS, GROUPS, WIN])
        v_ones = sb("v_ones", [KEYS, 2, BT, AH, AHD + 1])
        probs = sb("probs", [P, 2, BT, KEYS])
        probsT = sb("probsT", [KEYS, 2, BT * P])
        largest = sb("largest", [P, 2, BT])
        inverse = sb("inverse", [P, 2, 2 * BT, GROUPS])
        attended = sb("attended", [WIN, BT, P])
        repeat = sb("repeat", [P, P], BF16)
        band = sb("band", [P, 3, BT * KEYS], BF16)
        names = ("set_up consts_cast x_ready k_mm k_done q_mm q_done v_mm v_done score_mm max_done diff_done exp_done turned copied "
                 "pv_mm inverse_done attended_done final_mm final_done")
        s = type("Sems", (), {k: sem(k) for k in names.split()})
        ps_score = core.bank[0:2]
        ps_turn = core.bank[2:4]
        ps_out = core.banks[:, 4:6, :]
        ps_k, ps_q = core.bank[6], core.bank[7]
        OUTW = GROUPS * (AHD + 1)

        def back16(n, u, lag):
            return n + (u - lag) // STEPS, (u - lag) % STEPS

        def alive(n, u, lag):
            return not isinstance(n, int) or 0 <= n * STEPS + u - lag < BATCH * STEPS

        with nc.Block() as block:
            @block.gpsimd
            def _(pool):
                nc.gpsimd.memset(x_win[:, :], 0.0).then_inc(s.set_up, 1)
                nc.gpsimd.memset(kT[:, :], 0.0).then_inc(s.set_up, 1)
                nc.gpsimd.memset(v_ones[:, :, :, :, :], 1.0).then_inc(s.set_up, 1)
                pool.wait_ge(s.set_up, 3)

                def window(n):
                    wait(pool, s.v_mm, TILES * n)
                    nc.gpsimd.tensor_copy(x_win[:, WIN:WIN + SEQ], core.xnT[:, bass.ds(n * SEQ, SEQ)]).then_inc(s.x_ready, 1)
                over_sequences(pool, window)

            @block.tensor
            def _(pe):
                def project(n):
                    pe.wait_ge(s.x_ready, n + 1)
                    wait(pe, s.final_done, TILES * n - 1)
                    nc.tensor.matmul(ps_k[:, :], wk, x_win[:, WIN:WIN + SEQ], start=True, stop=True).then_inc(s.k_mm, 1)
                    wait(pe, s.v_done, TILES * n)
                    nc.tensor.matmul(ps_q[:, :], wq, x_win[:, WIN:WIN + SEQ], start=True, stop=True).then_inc(s.q_mm, 1)

                def values(n, j):
                    if j == 0:
                        pe.wait_ge(s.q_done, n + 1)
                    wait(pe, s.v_done, TILES * n + j)
                    for b in range(BT):
                        at = (j * BT + b) * WIN
                        last = nc.tensor.matmul(ps_q[0:KEYS, b * P:(b + 1) * P], x_win[:, at:at + KEYS], wv, start=True, stop=True)
                    last.then_inc(s.v_mm, 1)

                def scores(n, u):
                    j, g = u // GROUPS, u % GROUPS
                    bank = ps_score[u % 2]
                    rows = slice(WIN * g, WIN * g + WIN)
                    if u == 0:
                        pe.wait_ge(s.k_done, n + 1)
                        pe.wait_ge(s.q_done, n + 1)
                    wait(pe, s.diff_done, n * STEPS + u - 1)
                    which = 0 if j == 0 else 2 if j == TILES - 1 else 1
                    nc.tensor.matmul(bank[:, 0:BT * KEYS], repeat[rows, :], band[rows, which, :], start=True, stop=False,
                                     skip_group_check=True)
                    for b in range(BT):
                        blk = j * BT + b
                        last = nc.tensor.matmul(bank[:, b * KEYS:(b + 1) * KEYS],
                                                q_spread[rows, blk, :, :].rearrange("p h q -> p (h q)"),
                                                kT[rows, blk * WIN:blk * WIN + KEYS], start=False, stop=True, skip_group_check=True)
                    last.then_inc(s.score_mm, 1)

                def turn(n, u):
                    t = n * STEPS + u
                    pe.wait_ge(s.exp_done, t + 1)
                    wait(pe, s.copied, t - 1)
                    for b in range(BT):
                        last = nc.tensor.transpose(ps_turn[u % 2][0:KEYS, b * P:(b + 1) * P], probs[:, u % 2, b, :], core.ident[:, :])
                    last.then_inc(s.turned, 1)

                def weigh_values(n, u):
                    t = n * STEPS + u
                    j, g = u // GROUPS, u % GROUPS
                    pe.wait_ge(s.copied, t + 1)
                    if g == 0:
                        pe.wait_ge(s.v_done, TILES * n + j + 1)
                        wait(pe, s.attended_done, 8 * (TILES * n + j))
                    for b in range(BT):
                        at = ((g % 2) * BT + b) * OUTW
                        last = nc.tensor.matmul(ps_out[:, g // 2, at:at + OUTW], probsT[:, u % 2, b * P:(b + 1) * P],
                                                v_ones[:, j % 2, b, GROUPS * g:GROUPS * (g + 1), :].rearrange("k h d -> k (h d)"),
                                                start=True, stop=True)
                    last.then_inc(s.pv_mm, 1)

                def turn_back(n, j, after_k):
                    t = TILES * n + j
                    pe.wait_ge(s.attended_done, 8 * (t + 1))
                    wait(pe, s.final_done, t)
                    if after_k:
                        pe.wait_ge(s.k_done, n + 2)
                    nc.tensor.matmul(ps_k[:, 511:512], repeat[:, :], repeat[:, 0:1], start=True, stop=True)
                    for b in range(BT):
                        last = nc.tensor.transpose(ps_k[:, b * WIN:(b + 1) * WIN], attended[:, b, :], core.ident[0:WIN, 0:WIN])
                    last.then_inc(s.final_mm, 1)

                def steps(n):
                    for u in range(STEPS):
                        now = alive(n, u, 0)
                        if now and u == 0:
                            project(n)
                        if now and u % GROUPS == 0:
                            values(n, u // GROUPS)
                        if now:
                            scores(n, u)
                        if alive(n, u, 1):
                            turn(*back16(n, u, 1))
                        if alive(n, u, 2):
                            weigh_values(*back16(n, u, 2))
                        if u % GROUPS == GROUPS - 1 and alive(n, u, 4):
                            m, v = back16(n, u, 4)
                            turn_back(m, v // GROUPS, now and v == STEPS - 1)
                pe.wait_ge(s.set_up, 3)
                pe.wait_ge(s.consts_cast, 2)
                over_sequences(pe, steps)
                steps(BATCH)

            @block.scalar
            def _(act):
                def keys(n):
                    act.wait_ge(s.k_mm, n + 1)
                    wait(act, s.score_mm, STEPS * n)
                    nc.scalar.activation(kT[:, WIN:WIN + SEQ], ps_k[:, :], ACT.Identity, bias=bk).then_inc(s.k_done, 1)

                def values(n, j):
                    t = TILES * n + j
                    act.wait_ge(s.v_mm, t + 1)
                    wait(act, s.pv_mm, GROUPS * (t - 1))
                    nc.scalar.activation(v_ones[:, j % 2, :, :, 0:AHD].rearrange("k b h d -> k (b h) d"),
                                         ps_q[0:KEYS, :].rearrange("k (a d) -> k a d", d=AHD), ACT.Copy).then_inc(s.v_done, 1)

                def exponential(n, u):
                    act.wait_ge(s.diff_done, n * STEPS + u + 1)
                    here = probs[:, u % 2, :, :]
                    nc.scalar.activation(here, here, ACT.Exp).then_inc(s.exp_done, 1)

                def copy(n, u):
                    t = n * STEPS + u
                    act.wait_ge(s.turned, t + 1)
                    wait(act, s.pv_mm, t - 1)
                    nc.scalar.activation(probsT[:, u % 2, :], ps_turn[u % 2][0:KEYS, :], ACT.Copy).then_inc(s.copied, 1)

                def final(n, j):
                    t = TILES * n + j
                    act.wait_ge(s.final_mm, t + 1)
                    nc.scalar.activation(core.xnT[:, bass.ds(t * P, P)], ps_k[:, 0:P], ACT.Identity, bias=bv).then_inc(s.final_done, 1)

                def steps(n):
                    for u in range(STEPS):
                        now = alive(n, u, 0)
                        if now and u == 0:
                            keys(n)
                        if now and u % GROUPS == 0:
                            values(n, u // GROUPS)
                        if now:
                            exponential(n, u)
                        if alive(n, u, 1):
                            copy(*back16(n, u, 1))
                        if u % GROUPS == GROUPS - 1 and alive(n, u, 4):
                            m, v = back16(n, u, 4)
                            final(m, v // GROUPS)
                act.wait_ge(s.set_up, 3)
                over_sequences(act, steps)
                steps(BATCH)

            @block.vector
            def _(dve):
                dve.wait_ge(core.params1_in, core.params1_count)
                nc.vector.tensor_copy(repeat[:, :], bf_consts[:, 0:P]).then_inc(s.consts_cast, 1)
                nc.vector.tensor_copy(band[:, :, :], bf_consts[:, P:].rearrange("p (v k) -> p v k", v=3)).then_inc(s.consts_cast, 1)

                def queries(n):
                    dve.wait_ge(s.q_mm, n + 1)
                    wait(dve, s.score_mm, STEPS * n)
                    for h in range(GROUPS):
                        last = nc.vector.tensor_scalar(q_spread[:, :, h, :], ps_q[:, :].rearrange("p (b q) -> p b q", q=WIN),
                                                       bq, head_mask[:, h:h + 1], ALU.add, ALU.mult)
                    last.then_inc(s.q_done, 1)

                def differences(n, u):
                    t = n * STEPS + u
                    bank = ps_score[u % 2][:, 0:BT * KEYS].rearrange("p (b k) -> p b k", k=KEYS)
                    dve.wait_ge(s.score_mm, t + 1)
                    wait(dve, s.diff_done, t - 1)
                    nc.vector.tensor_reduce(largest[:, u % 2, :], bank, AXX, ALU.max).then_inc(s.max_done, 1)
                    dve.wait_ge(s.max_done, t + 1)
                    wait(dve, s.turned, t - 1)
                    nc.vector.tensor_tensor(probs[:, u % 2, :, :], bank,
                                            largest[:, u % 2, :].unsqueeze(2).to_broadcast([P, BT, KEYS]),
                                            ALU.subtract).then_inc(s.diff_done, 1)

                def divide(n, j):
                    t = TILES * n + j
                    outs = ps_out[:, :, 0:2 * BT * OUTW].rearrange("p e (a h d) -> p e a h d", h=GROUPS, d=AHD + 1)
                    dve.wait_ge(s.pv_mm, GROUPS * (t + 1))
                    wait(dve, s.attended_done, 8 * t)
                    for e in range(2):
                        nc.vector.reciprocal(inverse[:, e, :, :], outs[:, e, :, :, AHD]).then_inc(s.inverse_done, 1)
                    dve.wait_ge(s.inverse_done, 2 * (t + 1))
                    wait(dve, s.final_mm, t)
                    for h in range(GROUPS):
                        rows = slice(WIN * h, WIN * h + WIN)
                        for e in range(2):
                            to = attended[:, :, :].rearrange("q b (g h d) -> q g b h d", g=GROUPS, h=GROUPS)
                            nc.vector.tensor_tensor(
                                to[:, 2 * e:2 * e + 2, :, h, :],
                                outs[rows, e, :, h, 0:AHD].rearrange("q (g b) d -> q g b d", g=2),
                                inverse[rows, e, :, h].rearrange("q (g b) -> q g b", g=2).unsqueeze(3).to_broadcast(
                                    [WIN, 2, BT, AHD]), ALU.mult).then_inc(s.attended_done, 1)

                def steps(n):
                    for u in range(STEPS):
                        now = alive(n, u, 0)
                        if now and u == 0:
                            queries(n)
                        if now:
                            differences(n, u)
                        if u % GROUPS == 2 and alive(n, u, 3):
                            m, v = back16(n, u, 3)
                            divide(m, v // GROUPS)
                over_sequences(dve, steps)
                steps(BATCH)


def mlp_phase(nc, core, wo, w_f1, w_f2, c1, bo, g1, b1, c2, g2, b2):
    with ExitStack() as ctx:
        sb = lambda name, shape, dt=F32: ctx.enter_context(nc.sbuf_tensor("ml_" + name, shape, dt))
        sem = lambda name: ctx.enter_context(nc.semaphore("ml_" + name))
        HID = FFN // P
        ALL = [P, TILES, P]
        aT = sb("aT", [P, SEQ])
        base = sb("base", ALL)
        raw = [sb("raw0", ALL), sb("raw1", ALL)]
        stats = [sb("stats0", [P, TILES, 6]), sb("stats1", [P, TILES, 6])]
        mean_var = [sb("mv0", [P, TILES, 2]), sb("mv1", [P, TILES, 2])]
        var_eps = [sb("ve0", [P, TILES]), sb("ve1", [P, TILES])]
        rstd = [sb("rstd0", [P, TILES]), sb("rstd1", [P, TILES])]
        h = sb("h", ALL)
        h_c2 = sb("h_c2", ALL)
        hT = sb("hT", [P, SEQ])
        hidden = sb("hidden", [P, HID, SEQ])
        names = "a_ready base_part base_ready wo_mm h_part h_done h_c2_done turned hT_done f1_mm gelu_done f2_mm tail_part added"
        s = type("Sems", (), {k: sem(k) for k in names.split()})
        raw_done, stats_done, mv_done, vareps_done, rstd_done, norm_done = (
            [sem(f"{k}{i}") for i in range(2)] for k in ("raw_done", "stats_done", "mv_done", "vareps_done", "rstd_done", "norm_done"))
        ps_wo, ps_turn, ps_f2 = core.bank[0], core.bank[1], core.bank[2]
        ps_f1 = core.bank[3:5]
        row = lambda r: r.unsqueeze(1).to_broadcast(ALL)
        tiles = lambda bank: bank[:, :].rearrange("p (c d) -> p c d", c=TILES)
        here = lambda t, n: t[:, bass.ds(n * SEQ, SEQ)].rearrange("p (c d) -> p c d", c=TILES)

        with nc.Block() as block:
            @block.gpsimd
            def _(pool):
                def inputs(n):
                    wait(pool, s.wo_mm, n)
                    nc.gpsimd.tensor_copy(aT[:, :], core.xnT[:, bass.ds(n * SEQ, SEQ)]).then_inc(s.a_ready, 1)
                    wait(pool, raw_done[0], n)
                    nc.gpsimd.tensor_copy(base[:, :, :], here(core.xn2, n)).then_inc(s.base_part, 1)
                    pool.wait_ge(s.base_part, n + 1)
                    nc.gpsimd.tensor_tensor(base[:, :, :], base[:, :, :], row(bo), ALU.add).then_inc(s.base_ready, 1)

                def root(n, i):
                    pool.wait_ge(mv_done[i], TILES * (n + 1))
                    nc.gpsimd.tensor_tensor(var_eps[i][:, :], mean_var[i][:, :, 1], core.eps[:, 0:TILES], ALU.add).then_inc(vareps_done[i], 1)
                    pool.wait_ge(vareps_done[i], n + 1)
                    nc.gpsimd.tensor_tensor(rstd[i][:, :], var_eps[i][:, :], core.minus_half[:, 0:TILES], ALU.pow).then_inc(rstd_done[i], 1)

                def scale_h(n):
                    pool.wait_ge(norm_done[0], TILES * (n + 1))
                    wait(pool, s.turned, n)
                    wait(pool, s.h_c2_done, n)
                    nc.gpsimd.tensor_tensor(h[:, :, :], raw[0][:, :, :], row(g1), ALU.mult).then_inc(s.h_part, 1)
                    pool.wait_ge(s.h_part, n + 1)
                    nc.gpsimd.tensor_tensor(h[:, :, :], h[:, :, :], row(b1), ALU.add).then_inc(s.h_done, 1)
                    pool.wait_ge(s.h_done, n + 1)
                    if live(n, 0, 1):
                        pool.wait_ge(raw_done[1], n + 1)
                    nc.gpsimd.tensor_tensor(h_c2[:, :, :], h[:, :, :], row(c2), ALU.add).then_inc(s.h_c2_done, 1)

                def finish(n):
                    pool.wait_ge(norm_done[1], TILES * (n + 1))
                    r = raw[1][:, :, :]
                    nc.gpsimd.tensor_tensor(r, r, row(g2), ALU.mult).then_inc(s.tail_part, 1)
                    pool.wait_ge(s.tail_part, 2 * n + 1)
                    nc.gpsimd.tensor_tensor(r, r, row(b2), ALU.add).then_inc(s.tail_part, 1)

                def steps(n):
                    if live(n, 0, 0):
                        inputs(n)
                        root(n, 0)
                        scale_h(n)
                    if live(n, 0, 1):
                        root(n - 1, 1)
                        finish(n - 1)
                over_sequences(pool, steps)
                steps(BATCH)

            @block.tensor
            def _(pe):
                def project(n):
                    pe.wait_ge(s.a_ready, n + 1)
                    wait(pe, raw_done[0], n)
                    for c in range(TILES):
                        last = nc.tensor.matmul(ps_wo[:, c * P:(c + 1) * P], aT[:, c * P:(c + 1) * P], wo, start=True, stop=True)
                    last.then_inc(s.wo_mm, 1)

                def mlp(n):
                    pe.wait_ge(s.h_done, n + 1)
                    for c in range(TILES):
                        last = nc.tensor.transpose(ps_turn[:, c * P:(c + 1) * P], h[:, c, :], core.ident[:, :])
                    last.then_inc(s.turned, 1)
                    pe.wait_ge(s.hT_done, n + 1)
                    for m in range(HID):
                        if m >= 2:
                            pe.wait_ge(s.gelu_done, HID * n + m - 1)
                        nc.tensor.matmul(ps_f1[m % 2][:, :], w_f1[:, m * P:(m + 1) * P], hT[:, :], start=True, stop=True).then_inc(s.f1_mm, 1)
                    if not isinstance(n, int) or n:
                        pe.wait_ge(raw_done[1], n + 1)
                    for m in range(HID):
                        pe.wait_ge(s.gelu_done, HID * n + m + 1)
                        for c in range(TILES):
                            last = nc.tensor.matmul(ps_f2[:, c * P:(c + 1) * P], hidden[:, m, c * P:(c + 1) * P],
                                                    w_f2[:, m * P:(m + 1) * P], start=(m == 0 and c == 0), stop=(m == HID - 1),
                                                    skip_group_check=True)
                    last.then_inc(s.f2_mm, 1)

                def steps(n):
                    if live(n, 0, 0):
                        project(n)
                    if live(n, 0, 1):
                        mlp(n - 1)
                over_sequences(pe, steps)
                steps(BATCH)

            @block.scalar
            def _(act):
                def steps(n):
                    act.wait_ge(s.turned, n + 1)
                    nc.scalar.activation(hT[:, :], ps_turn[:, :], ACT.Copy).then_inc(s.hT_done, 1)
                    wait(act, s.f2_mm, n)
                    for m in range(HID):
                        act.wait_ge(s.f1_mm, HID * n + m + 1)
                        nc.scalar.activation(hidden[:, m, :], ps_f1[m % 2][:, :], ACT.Gelu_apprx_tanh,
                                             bias=c1[:, m:m + 1]).then_inc(s.gelu_done, 1)
                over_sequences(act, steps)

            @block.vector
            def _(dve):
                dve.sem_inc(raw_done[1], 1)

                def statistics(n, i):
                    for c in range(TILES):
                        nc.vector.bn_stats(stats[i][:, c, :], raw[i][:, c, :]).then_inc(stats_done[i], 1)
                    dve.wait_ge(stats_done[i], TILES * (n + 1))
                    nc.vector.memset(core.spare[:, 0:1], 0.0)
                    for c in range(TILES):
                        nc.vector.bn_aggr(mean_var[i][:, c, :], stats[i][:, c, :]).then_inc(mv_done[i], 1)

                def normalise(n, i):
                    dve.wait_ge(rstd_done[i], n + 1)
                    for c in range(TILES):
                        nc.vector.tensor_scalar(raw[i][:, c, :], raw[i][:, c, :], mean_var[i][:, c, 0:1], rstd[i][:, c:c + 1],
                                                ALU.subtract, ALU.mult).then_inc(norm_done[i], 1)

                def first(n):
                    dve.wait_ge(s.wo_mm, n + 1)
                    dve.wait_ge(s.base_ready, n + 1)
                    wait(dve, s.h_part, n)
                    nc.vector.tensor_tensor(raw[0][:, :, :], tiles(ps_wo), base[:, :, :], ALU.add).then_inc(raw_done[0], 1)
                    dve.wait_ge(raw_done[0], n + 1)
                    statistics(n, 0)
                    normalise(n, 0)

                def second(n):
                    dve.wait_ge(s.f2_mm, n + 1)
                    dve.wait_ge(s.h_c2_done, n + 1)
                    nc.vector.tensor_tensor(raw[1][:, :, :], tiles(ps_f2), h_c2[:, :, :], ALU.add).then_inc(raw_done[1], 1)
                    dve.wait_ge(raw_done[1], n + 2)
                    statistics(n, 1)
                    normalise(n, 1)
                    dve.wait_ge(s.tail_part, 2 * n + 2)
                    nc.vector.tensor_tensor(here(core.x, n), here(core.x, n), raw[1][:, :, :], ALU.add).then_inc(s.added, 1)
                    dve.wait_ge(s.added, n + 1)

                def steps(n):
                    if live(n, 0, 0):
                        first(n)
                    if live(n, 0, 1):
                        second(n - 1)
                over_sequences(dve, steps)
                steps(BATCH)


def layer1(nc, core, ins, last_phase):
    with ExitStack() as layer:
        lsb = lambda name, shape, dt=F32: layer.enter_context(nc.sbuf_tensor(name, shape, dt))
        lsem = lambda name: layer.enter_context(nc.semaphore(name))
        at_w1, n_w1 = columns(W1)
        at_c1, n_c1 = columns(C1)
        at_r1, n_r1 = columns(R1)
        w1 = lsb("w1", [P, n_w1])
        c1 = lsb("c1", [P, n_c1 + GROUPS])
        r1 = lsb("r1", [P, n_r1])
        bf_consts = lsb("bf_consts", [P, P + 3 * (P // WIN) * KEYS])
        core.xn2 = lsb("xn2", [P, NT * P])
        logits = lsb("logits1", [P, NT, EXP1])
        top8 = lsb("top1", [P, NT, 8])
        core.params1_in, core.params1_count = lsem("params1_in"), 64
        W = lambda name: w1[:, at_w1[name][0]:at_w1[name][1]]
        C = lambda name: c1[:, at_c1[name][0]:at_c1[name][1]]
        R = lambda name: r1[:, at_r1[name][0]:at_r1[name][1]]
        with nc.Block() as block:
            @block.sync
            def _(sp):
                sp.dma_start(w1[:, :], ins["w1"]).then_inc(core.params1_in, 16)
                sp.dma_start(c1[:, :], ins["c1"]).then_inc(core.params1_in, 16)
                sp.dma_start(r1[:, :], ins["r1"].partition_broadcast(P)).then_inc(core.params1_in, 16)
                sp.dma_start(bf_consts[:, :], ins["bf_consts"]).then_inc(core.params1_in, 16)
                sp.wait_ge(core.params1_in, 64)
        norm_phase(nc, core, "n1_", core.x, None, W("w_small1"), EXP1, EXP1, R("gate_b"), logits, top8, core.xn2)
        attention_phase(nc, core, W("wq"), W("wk"), W("wv"), C("bq"), C("bk"), C("bv"), c1[:, n_c1:n_c1 + GROUPS], bf_consts)
        mlp_phase(nc, core, W("wo"), W("w_f1"), W("w_f2"), C("c1"), R("bo"), R("g1"), R("b1"), R("c2"), R("g2"), R("b2"))
        if last_phase >= 6:
            experts1(nc, core, ins, layer, logits, top8)


def layer1_arrays(a, pack, slices):
    channel = np.arange(P)
    query, key = channel % WIN, np.arange(KEYS)
    band = (key[None, :] >= query[:, None]) & (key[None, :] <= query[:, None] + 2 * WIN)
    blocks = np.stack([band & (key >= WIN), band, band, band, band & (key < 2 * WIN)], 0)
    variants = [blocks[[0, 1, 1, 1]], blocks[[1, 1, 1, 1]], blocks[[1, 1, 1, 4]]]
    masks = np.stack([np.where(v, 0.0, -1e30).transpose(1, 0, 2).reshape(P, -1) for v in variants], 1).reshape(P, -1)
    head_mask = ((channel[:, None] // AHD) % GROUPS == np.arange(GROUPS)) / np.sqrt(AHD)
    repeat = (query[:, None] == query[None, :])
    arrays = {
        "w1": pack(W1, {"w_small1": a["L1_ffn_gate_w"].T, "wq": a["L1_attn_Wq"], "wk": a["L1_attn_Wk"], "wv": a["L1_attn_Wv"],
                        "wo": a["L1_attn_Wo"], "w_f1": a["L1_attn_W1"], "w_f2": slices(a["L1_attn_W2"])}),
        "c1": np.concatenate([pack(C1, {"bq": a["L1_attn_bq"][:, None], "bk": a["L1_attn_bk"][:, None], "bv": a["L1_attn_bv"][:, None],
                                        "c1": a["L1_attn_c1"].reshape(-1, P).T}), head_mask.astype(np.float32)], 1),
        "r1": np.concatenate([a["L1_ffn_gate_b"], a["L1_attn_bo"], a["L1_attn_g1"], a["L1_attn_b1"], a["L1_attn_c2"],
                              a["L1_attn_g2"], a["L1_attn_b2"]]),
        "bf_consts": np.concatenate([repeat, masks], 1).astype(np.float32),
    }
    arrays.update(experts1_arrays(a))
    return arrays


SLOTS = NT + EXP1 - 1
HID1 = EDIM1 // P
RING = 3


def places_phase(nc, core, logits, top8):
    with ExitStack() as ctx:
        sb = lambda name, shape, dt=F32: ctx.enter_context(nc.sbuf_tensor("pl_" + name, shape, dt))
        sem = lambda name: ctx.enter_context(nc.semaphore("pl_" + name))
        E = [P, NT, EXP1]
        chosen = sb("chosen", E)
        order = sb("order", E)
        counts = sb("counts", [P, EXP1, NT])
        before = sb("before", [P, EXP1, NT])
        over = sb("over", [P, EXP1, NT])
        tiles_of = sb("tiles_of", [P, EXP1])
        tiles_to = sb("tiles_to", [P, EXP1])
        start = sb("start", [P, EXP1])
        passed = sb("passed", [P, SLOTS, EXP1])
        slot_e = sb("slot_e", [P, SLOTS])
        place = sb("place", [P, NT])
        dve_step, chosen_done, counted = sem("dve_step"), sem("chosen_done"), sem("counted")
        flat = lambda t: t[:, :, :].rearrange("p a b -> p (a b)")
        with nc.Block() as block:
            @block.tensor
            def _(pe):
                pe.wait_ge(chosen_done, 1)
                nc.tensor.matmul(core.bank[0][:, 0:NT * EXP1], core.strict, flat(chosen), start=True, stop=True).then_inc(counted, 1)
                nc.tensor.matmul(core.bank[1][:, 0:NT * EXP1], core.ones, flat(chosen), start=True, stop=True).then_inc(counted, 1)

            @block.vector
            def _(dve):
                count = [0]

                def step(ins):
                    count[0] += 1
                    ins.then_inc(dve_step, 1)
                    dve.wait_ge(dve_step, count[0])
                tt = nc.vector.tensor_tensor
                scan = lambda out, keep, data: step(nc.vector.tensor_tensor_scan(out, keep, data, 0.0, ALU.mult, ALU.add))
                step(tt(chosen[:, :, :], logits[:, :, :], top8[:, :, 0:1].to_broadcast(E), ALU.is_equal))
                scan(flat(order), core.restart8, flat(chosen))
                nc.vector.scalar_tensor_tensor(flat(chosen), flat(order), 1.0, flat(chosen), ALU.is_le, ALU.mult).then_inc(chosen_done, 1)
                dve.wait_ge(counted, 2)
                step(nc.vector.tensor_copy(counts[:, :, :], core.bank[1][:, 0:NT * EXP1].rearrange("p (t e) -> p e t", e=EXP1)))
                scan(flat(before), core.restart32, flat(counts))
                step(tt(over[:, :, :], before[:, :, NT - 1:NT].to_broadcast([P, EXP1, NT]),
                        core.multiples.unsqueeze(1).to_broadcast([P, EXP1, NT]), ALU.is_gt))
                step(nc.vector.tensor_reduce(tiles_of[:, :], over[:, :, :], AXX, ALU.add))
                step(tt(before[:, :, :], before[:, :, :], counts[:, :, :], ALU.subtract))
                scan(tiles_to[:, :], core.ones[:, 0:EXP1], tiles_of[:, :])
                step(tt(start[:, :], tiles_to[:, :], tiles_of[:, :], ALU.subtract))
                step(nc.vector.tensor_scalar(start[:, :], start[:, :], float(P), None, ALU.mult))
                step(tt(before[:, :, :], before[:, :, :], start[:, :].unsqueeze(2).to_broadcast([P, EXP1, NT]), ALU.add))
                step(tt(order[:, :, :], core.bank[0][:, 0:NT * EXP1].rearrange("p (t e) -> p t e", e=EXP1),
                        before[:, :, :].rearrange("p e t -> p t e"), ALU.add))
                step(tt(order[:, :, :], order[:, :, :], chosen[:, :, :], ALU.mult))
                step(nc.vector.tensor_reduce(place[:, :], order[:, :, :], AXX, ALU.add))
                step(nc.vector.tensor_copy(core.place[:, :], place[:, :]))
                step(tt(passed[:, :, :], core.slot_numbers.unsqueeze(2).to_broadcast([P, SLOTS, EXP1]),
                        tiles_to[:, :].unsqueeze(1).to_broadcast([P, SLOTS, EXP1]), ALU.is_ge))
                step(nc.vector.tensor_reduce(slot_e[:, :], passed[:, :, :], AXX, ALU.add))
                step(nc.vector.tensor_scalar(slot_e[:, :], slot_e[:, :], float(EXP1 - 1), None, ALU.min))
                step(nc.vector.tensor_copy(core.slot_expert[:, :], slot_e[:, :]))


def scatter_phase(nc, core, sorted_x):
    with ExitStack() as ctx:
        scattered = ctx.enter_context(nc.semaphore("scattered"))
        with nc.Block() as block:
            @block.gpsimd
            def _(pool):
                pool.wait_ge(core.cleared, 16)
                for t in range(NT):
                    nc.gpsimd.indirect_dma_start(
                        out=sorted_x, out_offset=bass.IndirectOffsetOnAxis(ap=core.place[:, t:t + 1], axis=0),
                        in_=core.xn2[:, t * P:(t + 1) * P], in_offset=None).then_inc(scattered, 16)
                pool.wait_ge(scattered, 16 * NT)


def experts1_phase(nc, core, sorted_x, sorted_y, w_up, w_down, b_up, b_down):
    with ExitStack() as ctx:
        sb = lambda name, shape, dt=F32: ctx.enter_context(nc.sbuf_tensor("e1_" + name, shape, dt))
        sem = lambda name: ctx.enter_context(nc.semaphore("e1_" + name))
        x = sb("x", [P, RING, P])
        xT = sb("xT", [P, RING, P])
        up = sb("up", [P, RING, EDIM1])
        hT = sb("hT", [P, RING, EDIM1])
        y = sb("y", [P, RING, P])
        names = "x_turned xT_done up_mm up_done up_turned hT_done down_mm y_done"
        s = type("Sems", (), {k: sem(k) for k in names.split()})
        x_in = [sem(f"x_in{u}") for u in range(RING)]
        y_out = [sem(f"y_out{u}") for u in range(RING)]
        ps_x, ps_up, ps_h, ps_y = core.bank[0], core.bank[1:4], core.bank[4:7], core.bank[7]
        ROUNDS = SLOTS // RING
        expert_of = lambda eng, slot: eng.value_load(core.slot_expert[0:1, bass.ds(slot, 1)], min_val=0, max_val=EXP1 - 1)

        def going(r, u, lag):
            return not isinstance(r, int) or 0 <= r * RING + u - lag < SLOTS

        def rounds(eng, body):
            body(0)
            body(1)
            with eng.Fori(2, ROUNDS) as r:
                body(r)

        with nc.Block() as block:
            @block.sync
            def _(sp):
                def steps(r):
                    for u in range(RING):
                        if going(r, u, 0):
                            slot = r * RING + u
                            wait(sp, s.x_turned, slot - RING + 1)
                            sp.dma_start(x[:, u, :], sorted_x[bass.ds(slot * P, P), :]).then_inc(x_in[u], 16)
                        if going(r, u, RING):
                            slot = (r - 1) * RING + u
                            sp.wait_ge(s.y_done, slot + 2)
                            sp.dma_start(sorted_y[bass.ds(slot * P, P), :], y[:, u, :]).then_inc(y_out[u], 16)
                rounds(sp, steps)
                steps(ROUNDS)
                for u in range(RING):
                    sp.wait_ge(y_out[u], 16 * ROUNDS)

            @block.tensor
            def _(pe):
                def turn(r, u):
                    slot = r * RING + u
                    pe.wait_ge(x_in[u], 16 * (r + 1))
                    wait(pe, s.xT_done, slot)
                    nc.tensor.transpose(ps_x[:, 0:P], x[:, u, :], core.ident).then_inc(s.x_turned, 1)

                def widen(r, u):
                    slot = r * RING + u
                    e = expert_of(pe, slot)
                    pe.wait_ge(s.xT_done, slot + 1)
                    wait(pe, s.up_done, slot - RING + 1)
                    nc.tensor.matmul(ps_up[u][:, :], xT[:, u, :], w_up[:, bass.ds(e * EDIM1, EDIM1)], start=True, stop=True).then_inc(s.up_mm, 1)

                def turn_up(r, u):
                    slot = r * RING + u
                    pe.wait_ge(s.up_done, slot + 1)
                    wait(pe, s.hT_done, slot - RING + 1)
                    for k in range(HID1):
                        last = nc.tensor.transpose(ps_h[u][:, k * P:(k + 1) * P], up[:, u, k * P:(k + 1) * P], core.ident)
                    last.then_inc(s.up_turned, 1)

                def narrow(r, u):
                    slot = r * RING + u
                    e = expert_of(pe, slot)
                    pe.wait_ge(s.hT_done, slot + 1)
                    if not isinstance(slot, int) or slot:
                        pe.wait_ge(s.y_done, slot + 1)
                    for k in range(HID1):
                        last = nc.tensor.matmul(ps_y[:, 0:P], hT[:, u, k * P:(k + 1) * P], w_down[:, bass.ds((e * HID1 + k) * P, P)],
                                                start=(k == 0), stop=(k == HID1 - 1))
                    last.then_inc(s.down_mm, 1)

                def steps(r):
                    for u in range(RING):
                        for lag, what in ((0, turn), (1, widen), (2, turn_up), (3, narrow)):
                            if going(r, u, lag):
                                what(r + (u - lag) // RING, (u - lag) % RING)
                rounds(pe, steps)
                steps(ROUNDS)

            @block.scalar
            def _(act):
                def steps(r):
                    for u in range(RING):
                        if going(r, u, 0):
                            slot = r * RING + u
                            act.wait_ge(s.x_turned, slot + 1)
                            wait(act, s.up_mm, slot - RING + 1)
                            nc.scalar.activation(xT[:, u, :], ps_x[:, 0:P], ACT.Copy).then_inc(s.xT_done, 1)
                        if going(r, u, 2):
                            q, v = r + (u - 2) // RING, (u - 2) % RING
                            slot = q * RING + v
                            act.wait_ge(s.up_turned, slot + 1)
                            wait(act, s.down_mm, slot - RING + 1)
                            nc.scalar.activation(hT[:, v, :], ps_h[v][:, :], ACT.Relu).then_inc(s.hT_done, 1)
                rounds(act, steps)
                steps(ROUNDS)

            @block.vector
            def _(dve):
                dve.sem_inc(s.y_done, 1)

                def bias_up(r, u):
                    slot = r * RING + u
                    e = expert_of(dve, slot)
                    dve.wait_ge(s.up_mm, slot + 1)
                    wait(dve, s.up_turned, slot - RING + 1)
                    nc.vector.tensor_tensor(up[:, u, :], ps_up[u][:, :], b_up[:, bass.ds(e * EDIM1, EDIM1)], ALU.add).then_inc(s.up_done, 1)

                def bias_down(r, u):
                    slot = r * RING + u
                    e = expert_of(dve, slot)
                    dve.wait_ge(s.down_mm, slot + 1)
                    if not isinstance(r, int) or r:
                        wait(dve, y_out[u], 16 * r)
                    nc.vector.tensor_tensor(y[:, u, :], ps_y[:, 0:P], b_down[:, bass.ds(e * P, P)], ALU.add).then_inc(s.y_done, 1)

                def steps(r):
                    for u in range(RING):
                        if going(r, u, 1):
                            bias_up(r + (u - 1) // RING, (u - 1) % RING)
                        if going(r, u, 3):
                            bias_down(r - 1, u)
                rounds(dve, steps)
                steps(ROUNDS)


def gather_phase(nc, core, sorted_y):
    with ExitStack() as ctx:
        gathered = [ctx.enter_context(nc.semaphore(f"gathered{n}")) for n in range(BATCH)]
        with nc.Block() as block:
            @block.gpsimd
            def _(pool):
                for t in range(NT):
                    nc.gpsimd.indirect_dma_start(
                        out=core.xn2[:, t * P:(t + 1) * P], out_offset=None, in_=sorted_y,
                        in_offset=bass.IndirectOffsetOnAxis(ap=core.place[:, t:t + 1], axis=0)).then_inc(gathered[t // TILES], 16)

            @block.vector
            def _(dve):
                for n in range(BATCH):
                    here = slice(n * SEQ, (n + 1) * SEQ)
                    dve.wait_ge(gathered[n], 16 * TILES)
                    nc.vector.tensor_tensor(core.x[:, here], core.x[:, here], core.xn2[:, here], ALU.add)


def experts1(nc, core, ins, layer, logits, top8):
    lsb = lambda name, shape, dt=F32: layer.enter_context(nc.sbuf_tensor(name, shape, dt))
    w_up = lsb("w_up1", [P, EXP1 * EDIM1])
    w_down = lsb("w_down1", [P, EXP1 * EDIM1])
    b_up = lsb("b_up1", [P, EXP1 * EDIM1])
    b_down = lsb("b_down1", [P, EXP1 * P])
    more = lsb("more_consts", [P, P + 3 * NT * EXP1 + SLOTS])
    zeros = lsb("zeros", [P, P])
    core.place = lsb("place", [P, NT], mybir.dt.uint32)
    core.slot_expert = lsb("slot_expert", [P, SLOTS], mybir.dt.int32)
    loaded, zero_set = layer.enter_context(nc.semaphore("experts_in")), layer.enter_context(nc.semaphore("zero_set"))
    core.cleared = layer.enter_context(nc.semaphore("cleared"))
    sorted_x = nc.dram_tensor("sorted_x", (SLOTS * P, P), F32, kind="Internal").ap()
    sorted_y = nc.dram_tensor("sorted_y", (SLOTS * P, P), F32, kind="Internal").ap()
    with nc.Block() as block:
        @block.vector
        def _(dve):
            nc.vector.memset(zeros[:, :], 0.0).then_inc(zero_set, 1)

        @block.sync
        def _(sp):
            sp.dma_start(more[:, :], ins["more_consts"]).then_inc(loaded, 16)
            sp.wait_ge(zero_set, 1)
            sp.dma_start(sorted_x.rearrange("(s p) d -> p s d", p=P), zeros[:, :].unsqueeze(1).to_broadcast([P, SLOTS, P])).then_inc(core.cleared, 16)
            sp.dma_start(w_up[:, :], ins["w_up1"]).then_inc(loaded, 16)
            sp.dma_start(w_down[:, :], ins["w_down1"]).then_inc(loaded, 16)
            sp.dma_start(b_up[:, :], ins["b_up1"].partition_broadcast(P)).then_inc(loaded, 16)
            sp.dma_start(b_down[:, :], ins["b_down1"].partition_broadcast(P)).then_inc(loaded, 16)
            sp.wait_ge(loaded, 80)
    core.strict = more[:, 0:P]
    width = NT * EXP1
    core.restart8 = more[:, P:P + width]
    core.restart32 = more[:, P + width:P + 2 * width]
    core.multiples = more[:, P + 2 * width:P + 2 * width + NT]
    core.slot_numbers = more[:, P + 3 * width:P + 3 * width + SLOTS]
    places_phase(nc, core, logits, top8)
    scatter_phase(nc, core, sorted_x)
    experts1_phase(nc, core, sorted_x, sorted_y, w_up, w_down, b_up, b_down)
    gather_phase(nc, core, sorted_y)


def experts1_arrays(a):
    row = lambda v, n: np.broadcast_to(np.asarray(v, np.float32), (P, n))
    width = NT * EXP1
    multiples = np.zeros(width)
    multiples[:NT] = np.arange(NT) * P
    return {
        "more_consts": np.concatenate([np.triu(np.ones((P, P)), 1), row(np.arange(width) % EXP1 != 0, width),
                                       row(np.arange(width) % NT != 0, width), row(multiples, width), row(np.arange(SLOTS), SLOTS)],
                                      1).astype(np.float32),
        "w_up1": a["L1_ffn_w1"].transpose(2, 0, 1).reshape(P, -1),
        "w_down1": a["L1_ffn_w2"].transpose(0, 2, 1).reshape(EXP1 * HID1, P, P).transpose(1, 0, 2).reshape(P, -1),
        "b_up1": a["L1_ffn_b1"].reshape(-1),
        "b_down1": a["L1_ffn_b2"].reshape(-1),
    }


LAST_PHASE = 6


def build(nc, ins, out, last_phase=99):
    with ExitStack() as ctx:
        core = Core(nc, ctx)
        sb, sem = core.sb, core.sem
        core.banks = ctx.enter_context(nc.psum_tensor("banks", [P, 8, 512], F32))
        core.bank = [core.banks[:, i, :] for i in range(8)]
        core.x = sb("x", [P, NT * P])
        core.xnT = sb("xnT", [P, NT * P])
        at_w0, n_w0 = columns(W0)
        at_c0, n_c0 = columns(C0)
        at_r0, n_r0 = columns(R0)
        w0 = sb("w0", [P, n_w0])
        c0 = sb("c0", [P, n_c0])
        r0 = sb("r0", [P, n_r0])
        consts = sb("consts", [P, 4 * P])
        core.ident, core.upper, core.ones = consts[:, 0:P], consts[:, P:2 * P], consts[:, 2 * P:3 * P]
        core.minus_half, core.eps = consts[:, 3 * P:3 * P + 64], consts[:, 3 * P + 64:4 * P]
        core.spare = sb("spare", [P, 1])
        core.restart = sb("restart", [P, NT * EXP0])
        x_in = [sem("x_in_first"), sem("x_in_rest")]
        core.params_in, out_done = sem("params_in"), sem("out_done")
        core.params_count = 16 * 5
        W = lambda name: w0[:, at_w0[name][0]:at_w0[name][1]]
        C = lambda name: c0[:, at_c0[name][0]:at_c0[name][1]]
        R = lambda name: r0[:, at_r0[name][0]:at_r0[name][1]]
        x_rows = ins["x"].rearrange("b (c p) d -> p (b c) d", p=P)
        out_rows = out.rearrange("b (c p) d -> p (b c) d", p=P)

        def load_x(sp, n):
            sp.dma_start(core.x[:, n * SEQ:(n + 1) * SEQ].rearrange("p (c d) -> p c d", d=P),
                         x_rows[:, n * TILES:(n + 1) * TILES, :]).then_inc(x_in[min(n, 1)], 16)

        with nc.Block() as block:
            @block.sync
            def _(sp):
                load_x(sp, 0)
                sp.dma_start(consts[:, :], ins["consts"]).then_inc(core.params_in, 16)
                sp.dma_start(core.restart[:, :], ins["restart"]).then_inc(core.params_in, 16)
                sp.dma_start(c0[:, :], ins["c0"]).then_inc(core.params_in, 16)
                sp.dma_start(r0[:, :], ins["r0"].partition_broadcast(P)).then_inc(core.params_in, 16)
                sp.dma_start(w0[:, :], ins["w0"]).then_inc(core.params_in, 16)
                for n in range(1, BATCH):
                    load_x(sp, n)

        with ExitStack() as layer:
            lsb = lambda name, shape, dt=F32: layer.enter_context(nc.sbuf_tensor(name, shape, dt))
            core.gates0 = lsb("gates0", [P, NT, EXP0])
            core.dt = lsb("dt", [P, NT, HEADS])
            core.cum = lsb("cum", [P, NT, HEADS])
            core.exp_cum = lsb("exp_cum", [P, NT, HEADS])
            core.exp_total = lsb("exp_total", [P, NT, HEADS])
            core.w_end = lsb("w_end", [P, NT, HEADS])
            with ExitStack() as routing:
                logits = routing.enter_context(nc.sbuf_tensor("logits0", [P, NT, EXP0 + HEADS], F32))
                top8 = routing.enter_context(nc.sbuf_tensor("top0", [P, NT, 8], F32))
                norm_phase(nc, core, "n0_", core.x, x_in, W("w_small0"), EXP0 + HEADS, EXP0, None, logits, top8, None)
                routing0_phase(nc, core, logits, top8, R("dt_bias"), R("a_log"))
            if last_phase >= 1:
                experts0_phase(nc, core, W("w_up0"), W("w_down0"))
            if last_phase >= 2:
                skip_phase(nc, core, W("w_zx"), W("w_out"))
            if last_phase >= 3:
                core.x_tokens = lsb("x_tokens", [P, NT, INNER + NSTATE])
                core.b_rows = lsb("b_rows", [NSTATE, 2, NT * P])
                conv_phase(nc, core, W("w_xbc"), C("conv_w"), C("conv_b"))
                ssm_phase(nc, core, W("w_gate"), W("w_out"), C("gamma"), C("beta"), C("b_gate"), R("d_param"))
        if last_phase >= 4:
            layer1(nc, core, ins, last_phase)

        with nc.Block() as block:
            @block.sync
            def _(sp):
                for n in range(BATCH):
                    sp.dma_start(out_rows[:, n * TILES:(n + 1) * TILES, :],
                                 core.x[:, n * SEQ:(n + 1) * SEQ].rearrange("p (c d) -> p c d", d=P)).then_inc(out_done, 16)
                sp.wait_ge(out_done, 16 * BATCH)


def kernel(**inputs):
    import concourse.bacc as bacc
    from concourse.bass_utils import run_bass_kernel_spmd

    a = {k: np.asarray(v) for k, v in inputs.items()}

    def pack(layout, parts):
        cols, width = columns(layout)
        packed = np.zeros((P, width), np.float32)
        for name, value in parts.items():
            packed[:value.shape[0], cols[name][0]:cols[name][0] + value.shape[1]] = value
        return packed

    def slices(m):
        return m.reshape(-1, P, m.shape[1]).transpose(1, 0, 2).reshape(P, -1)

    w_in = a["L0_attn_W_in"].T
    xbc = w_in[:, 3 * INNER:]
    conv = a["L0_attn_conv_w"][:, 0, :]
    zero = np.zeros((P, 16), np.float32)
    third = lambda m: np.concatenate([m[256:272], zero[:16, :m.shape[1]], m[272:288]])
    arrays = {
        "x": a["L0_attn_u"],
        "w0": pack(W0, {
            "w_small0": np.concatenate([a["L0_ffn_router_w"].T, w_in[:, -HEADS:]], 1),
            "w_up0": np.concatenate([a["L0_ffn_shared_up"].reshape(-1, P), a["L0_ffn_routed_up"].reshape(-1, P)]).T,
            "w_down0": slices(np.concatenate([a["L0_ffn_shared_down"].transpose(0, 2, 1).reshape(-1, P),
                                              a["L0_ffn_routed_down"].transpose(0, 2, 1).reshape(-1, P)])),
            "w_zx": np.concatenate([w_in[:, 0:128], w_in[:, 256:384], w_in[:, 128:256], w_in[:, 384:512]], 1),
            "w_xbc": np.concatenate([xbc[:, 0:272], zero, xbc[:, 272:288]], 1),
            "w_out": slices(a["L0_attn_W_out"].T),
            "w_gate": slices(a["L0_attn_W_gate"].T)}),
        "c0": pack(C0, {
            "conv_w": np.concatenate([conv[0:128], conv[128:256], np.concatenate([third(conv), np.zeros((80, 4), np.float32)])], 1),
            "conv_b": np.stack([a["L0_attn_conv_b"][0:128], a["L0_attn_conv_b"][128:256],
                                np.concatenate([third(a["L0_attn_conv_b"][:, None])[:, 0], np.zeros(80, np.float32)])], 1),
            "gamma": a["L0_attn_ln_gamma"].reshape(2, P).T, "beta": a["L0_attn_ln_beta"].reshape(2, P).T,
            "b_gate": a["L0_attn_b_gate"].reshape(2, P).T}),
        "r0": np.concatenate([a["L0_attn_dt_bias"], a["L0_attn_A_log"], a["L0_attn_D_param"]]),
        "consts": np.concatenate([np.eye(P), np.triu(np.ones((P, P))), np.ones((P, P)), np.full((P, 64), -0.5), np.full((P, 64), EPS)], 1).astype(np.float32),
        "restart": np.broadcast_to((np.arange(NT * EXP0) % EXP0 != 0).astype(np.float32), (P, NT * EXP0)).copy(),
    }
    arrays.update(layer1_arrays(a, pack, slices))
    nc = bacc.Bacc("TRN2", target_bir_lowering=False, num_devices=1)
    arrays = {f"in_{k}": np.ascontiguousarray(v) for k, v in arrays.items()}
    ins = {k[3:]: nc.dram_tensor(k, v.shape, mybir.dt.from_np(v.dtype), kind="ExternalInput").ap() for k, v in arrays.items()}
    out = nc.dram_tensor("out", (BATCH, SEQ, P), F32, kind="ExternalOutput").ap()
    build(nc, ins, out, LAST_PHASE)
    result = run_bass_kernel_spmd(nc, [arrays], core_ids=[0])
    return result.results[0]["out"]
```

```python
from contextlib import ExitStack

import numpy as np

import concourse.bass as bass
from concourse import mybir

F32 = mybir.dt.float32
BF16 = mybir.dt.bfloat16
ALU = mybir.AluOpType
ACT = mybir.ActivationFunctionType
AXX = mybir.AxisListType.X

P = 128
BATCH, SEQ = 8, 512
TILES = SEQ // P
NT = BATCH * TILES
EPS = 1e-5
HEADS, HDIM, NSTATE, INNER, TAPS = 8, 32, 16, 256, 4
EXP0, TOP0, EDIM0 = 16, 4, 64
UPS = (2 + EXP0) * EDIM0 // P
AH, AHD, WIN = 16, 8, 32
BLOCKS = SEQ // WIN
GROUPS = 4
KEYS = 3 * WIN
FFN = 512
EXP1, EDIM1 = 8, 512

W0 = [("w_small0", HEADS + EXP0), ("w_up0", UPS * P), ("w_down0", UPS * P), ("w_zx", 4 * P),
      ("w_xbc", 3 * P), ("w_out", 4 * P), ("w_gate", 4 * P)]
C0 = [("conv_w", 3 * TAPS), ("conv_b", 3), ("gamma", 2), ("beta", 2), ("b_gate", 2)]
R0 = [("dt_bias", HEADS), ("a_log", HEADS), ("d_param", HEADS)]
W1 = [("w_small1", EXP1), ("wq", P), ("wk", P), ("wv", P), ("wo", P), ("w_f1", FFN), ("w_f2", FFN)]
C1 = [("bq", 1), ("bk", 1), ("bv", 1), ("c1", FFN // P)]
R1 = [("gate_b", EXP1), ("bo", P), ("g1", P), ("b1", P), ("c2", P), ("g2", P), ("b2", P)]


def columns(layout):
    at, out = 0, {}
    for name, width in layout:
        out[name] = (at, at + width)
        at += width
    return out, at


def wait(eng, sem, value):
    if isinstance(value, int) and value <= 0:
        return
    eng.wait_ge(sem, value)


def live(n, c, lag):
    return not isinstance(n, int) or 0 <= n * TILES + c - lag < NT


def back(n, c, lag):
    return n + (c - lag) // TILES, (c - lag) % TILES


def over_sequences(eng, body):
    body(0)
    with eng.Fori(1, BATCH) as n:
        body(n)


class Core:

    def __init__(self, nc, ctx):
        self.nc, self.ctx = nc, ctx

    def sb(self, name, shape, dt=F32):
        t = self.ctx.enter_context(self.nc.sbuf_tensor(name, shape, dt))
        return t

    def sem(self, name):
        return self.ctx.enter_context(self.nc.semaphore(name))


def norm_phase(nc, core, tag, x, x_loaded, w_small, n_small, n_exp, bias_row, logits, top8, xn_tokens):
    with ExitStack() as ctx:
        sb = lambda name, shape, dt=F32: ctx.enter_context(nc.sbuf_tensor(tag + name, shape, dt))
        sem = lambda name: ctx.enter_context(nc.semaphore(tag + name))
        stats = sb("stats", [P, TILES, 6])
        mean_var = sb("mean_var", [P, TILES, 2])
        var_eps = sb("var_eps", [P, TILES])
        rstd = sb("rstd", [P, TILES])
        xn = sb("xn", [P, TILES, P])
        xnT_tile = sb("xnT_tile", [P, TILES, P])
        small = sb("small", [P, TILES, n_small])
        top = sb("top", [P, TILES, 8])
        stats_done, mv_done, vareps_done, rstd_done = sem("stats_done"), sem("mv_done"), sem("vareps_done"), sem("rstd_done")
        xn_done, turned, xnT_done, small_mm, small_done, top_done = (
            sem("xn_done"), sem("turned"), sem("xnT_done"), sem("small_mm"), sem("small_done"), sem("top_done"))
        ps_turn = [core.bank[0], core.bank[1]]
        evac = 3 if xn_tokens is not None else 2
        ps_small = [core.bank[2], core.bank[3]]

        with nc.Block() as block:
            @block.vector
            def _(dve):
                def statistics(n):
                    for c in range(TILES):
                        if x_loaded is not None and c == 0:
                            if isinstance(n, int):
                                dve.wait_ge(x_loaded[0], 16)
                            else:
                                dve.wait_ge(x_loaded[1], 16 * (BATCH - 1))
                        nc.vector.bn_stats(stats[:, c, :], x[:, bass.ds((n * TILES + c) * P, P)]).then_inc(stats_done, 1)
                    dve.wait_ge(stats_done, TILES * n + TILES)
                    nc.vector.memset(core.spare[:, 0:1], 0.0)
                    for c in range(TILES):
                        nc.vector.bn_aggr(mean_var[:, c, :], stats[:, c, :]).then_inc(mv_done, 1)

                def normalise(n):
                    dve.wait_ge(rstd_done, n + 1)
                    for c in range(TILES):
                        t = n * TILES + c
                        wait(dve, turned, t - TILES + 1)
                        if xn_tokens is not None:
                            wait(dve, xnT_done, 3 * (t - TILES + 1))
                        nc.vector.tensor_scalar(xn[:, c, :], x[:, bass.ds(t * P, P)], mean_var[:, c, 0:1],
                                                rstd[:, c:c + 1], ALU.subtract, ALU.mult).then_inc(xn_done, 1)

                def router(n):
                    for c in range(TILES):
                        t = n * TILES + c
                        dve.wait_ge(small_mm, t + 1)
                        if bias_row is None:
                            nc.vector.tensor_copy(small[:, c, :], ps_small[c % 2][:, 0:n_small]).then_inc(small_done, 1)
                        else:
                            nc.vector.tensor_tensor(small[:, c, :], ps_small[c % 2][:, 0:n_small], bias_row,
                                                    ALU.add).then_inc(small_done, 1)
                    dve.wait_ge(small_done, TILES * n + TILES)
                    nc.vector.memset(core.spare[:, 0:1], 0.0)
                    for c in range(TILES):
                        nc.vector.max(top[:, c, :], small[:, c, 0:n_exp]).then_inc(top_done, 1)
                    dve.wait_ge(top_done, TILES * n + TILES)
                    nc.vector.tensor_copy(logits[:, bass.ds(n * TILES, TILES), :], small[:, :, :])
                    nc.vector.tensor_copy(top8[:, bass.ds(n * TILES, TILES), :], top[:, :, :])

                def sequence(n):
                    statistics(n)
                    if live(n, 0, 1):
                        router(n - 1)
                    normalise(n)
                dve.wait_ge(core.params_in, core.params_count)
                over_sequences(dve, sequence)
                router(BATCH - 1)

            @block.gpsimd
            def _(pool):
                def sequence(n):
                    pool.wait_ge(mv_done, TILES * n + TILES)
                    wait(pool, xn_done, TILES * n)
                    nc.gpsimd.tensor_tensor(var_eps[:, :], mean_var[:, :, 1], core.eps[:, 0:TILES], ALU.add).then_inc(vareps_done, 1)
                    pool.wait_ge(vareps_done, n + 1)
                    nc.gpsimd.tensor_tensor(rstd[:, :], var_eps[:, :], core.minus_half[:, 0:TILES], ALU.pow).then_inc(rstd_done, 1)
                pool.wait_ge(core.params_in, core.params_count)
                over_sequences(pool, sequence)

            @block.tensor
            def _(pe):
                def turn(n, c):
                    t = n * TILES + c
                    pe.wait_ge(xn_done, t + 1)
                    wait(pe, xnT_done, evac * (t - 1))
                    nc.tensor.transpose(ps_turn[c % 2][:, 0:P], xn[:, c, :], core.ident[:, :]).then_inc(turned, 1)

                def small_product(n, c):
                    t = n * TILES + c
                    pe.wait_ge(xnT_done, evac * (t + 1))
                    wait(pe, small_done, t - 1)
                    nc.tensor.matmul(ps_small[c % 2][:, 0:n_small], xnT_tile[:, c, :], w_small,
                                     start=True, stop=True).then_inc(small_mm, 1)

                def sequence(n):
                    for c in range(TILES):
                        if live(n, c, 1):
                            small_product(*back(n, c, 1))
                        turn(n, c)
                pe.wait_ge(core.params_in, core.params_count)
                over_sequences(pe, sequence)
                small_product(BATCH - 1, TILES - 1)

            @block.scalar
            def _(act):
                def sequence(n):
                    for c in range(TILES):
                        t = n * TILES + c
                        act.wait_ge(turned, t + 1)
                        wait(act, small_mm, t - TILES + 1)
                        nc.scalar.activation(xnT_tile[:, c, :], ps_turn[c % 2][:, 0:P], ACT.Copy).then_inc(xnT_done, 1)
                        nc.scalar.activation(core.xnT[:, bass.ds(t * P, P)], ps_turn[c % 2][:, 0:P], ACT.Copy).then_inc(xnT_done, 1)
                        if xn_tokens is not None:
                            nc.scalar.activation(xn_tokens[:, bass.ds(t * P, P)], xn[:, c, :], ACT.Copy).then_inc(xnT_done, 1)
                over_sequences(act, sequence)


def routing0_phase(nc, core, logits, top8, dt_bias, a_log):
    with ExitStack() as ctx:
        sb = lambda name, shape, dt=F32: ctx.enter_context(nc.sbuf_tensor("r0_" + name, shape, dt))
        sem = lambda name: ctx.enter_context(nc.semaphore("r0_" + name))
        shifted = sb("shifted", [P, NT, EXP0])
        above = sb("above", [P, NT, EXP0])
        equal = sb("equal", [P, NT, EXP0])
        order = sb("order", [P, NT, EXP0])
        total = sb("total", [P, NT])
        n_above = sb("n_above", [P, NT])
        pre = sb("pre", [P, NT, HEADS])
        small_exp = sb("small_exp", [P, NT, HEADS])
        one_plus = sb("one_plus", [P, NT, HEADS])
        log_1p = sb("log_1p", [P, NT, HEADS])
        ratio = sb("ratio", [P, NT, HEADS])
        decay = sb("decay", [P, NT, HEADS])
        a_exp = sb("a_exp", [P, HEADS])
        dve_step, a_ready, act_ready, decay_ready, sums_ready, sums_copied = (
            sem("dve_step"), sem("a_ready"), sem("act_ready"), sem("decay_ready"), sem("sums_ready"), sem("sums_copied"))
        abs_done = sem("abs_done")
        E = [P, NT, EXP0]
        H = [P, NT, HEADS]
        lg = logits[:, :, 0:EXP0]
        largest = top8[:, :, 0:1].to_broadcast(E)
        fourth = top8[:, :, TOP0 - 1:TOP0].to_broadcast(E)
        flat = lambda t: t[:, :, :].rearrange("p t h -> p (t h)")

        with nc.Block() as block:
            @block.vector
            def _(dve):
                count = [0]

                def step(ins):
                    count[0] += 1
                    ins.then_inc(dve_step, 1)
                    dve.wait_ge(dve_step, count[0])
                step(nc.vector.tensor_tensor(pre[:, :, :], logits[:, :, EXP0:EXP0 + HEADS],
                                             dt_bias.unsqueeze(1).to_broadcast(H), ALU.add))
                step(nc.vector.tensor_tensor(shifted[:, :, :], lg, largest, ALU.subtract))
                step(nc.vector.tensor_tensor(above[:, :, :], lg, fourth, ALU.is_gt))
                step(nc.vector.tensor_tensor(equal[:, :, :], lg, fourth, ALU.is_equal))
                step(nc.vector.tensor_reduce(n_above[:, :], above[:, :, :], AXX, ALU.add))
                step(nc.vector.tensor_tensor_scan(flat(order), core.restart[:, 0:NT * EXP0], flat(equal), 0.0,
                                                  ALU.mult, ALU.add))
                step(nc.vector.tensor_tensor(order[:, :, :], order[:, :, :], n_above[:, :].unsqueeze(2).to_broadcast(E), ALU.add))
                step(nc.vector.scalar_tensor_tensor(flat(equal), flat(order), float(TOP0), flat(equal), ALU.is_le, ALU.mult))
                step(nc.vector.tensor_tensor(above[:, :, :], above[:, :, :], equal[:, :, :], ALU.add))
                dve.wait_ge(act_ready, 2)
                step(nc.vector.tensor_scalar(one_plus[:, :, :], small_exp[:, :, :], 1.0, None, ALU.add))
                dve.wait_ge(act_ready, 3)
                step(nc.vector.tensor_reduce(total[:, :], shifted[:, :, :], AXX, ALU.add))
                step(nc.vector.reciprocal(total[:, :], total[:, :]))
                step(nc.vector.tensor_tensor(shifted[:, :, :], shifted[:, :, :], total[:, :].unsqueeze(2).to_broadcast(E), ALU.mult))
                step(nc.vector.tensor_tensor(core.gates0[:, :, :], shifted[:, :, :], above[:, :, :], ALU.mult))
                step(nc.vector.tensor_scalar(ratio[:, :, :], one_plus[:, :, :], -1.0, None, ALU.add))
                step(nc.vector.scalar_tensor_tensor(flat(decay), flat(ratio), 0.0, flat(small_exp), ALU.is_equal, ALU.mult))
                step(nc.vector.tensor_scalar(ratio[:, :, :], ratio[:, :, :], 1e-30, None, ALU.max))
                step(nc.vector.reciprocal(ratio[:, :, :], ratio[:, :, :]))
                step(nc.vector.tensor_tensor(ratio[:, :, :], ratio[:, :, :], small_exp[:, :, :], ALU.mult))
                dve.wait_ge(act_ready, 4)
                step(nc.vector.tensor_tensor(log_1p[:, :, :], log_1p[:, :, :], ratio[:, :, :], ALU.mult))
                step(nc.vector.tensor_tensor(log_1p[:, :, :], log_1p[:, :, :], decay[:, :, :], ALU.add))
                step(nc.vector.scalar_tensor_tensor(flat(core.dt), flat(pre), 0.0, flat(log_1p), ALU.max, ALU.add))
                step(nc.vector.tensor_scalar(a_exp[:, :], a_exp[:, :], -1.0, None, ALU.mult))
                nc.vector.tensor_tensor(decay[:, :, :], core.dt[:, :, :], a_exp[:, :].unsqueeze(1).to_broadcast(H),
                                        ALU.mult).then_inc(decay_ready, 1)
                dve.wait_ge(sums_ready, 2)
                nc.vector.tensor_copy(flat(core.cum), core.bank[0][:, 0:NT * HEADS]).then_inc(sums_copied, 1)
                dve.wait_ge(sums_copied, 1)
                nc.vector.tensor_tensor(flat(core.w_end), core.bank[1][:, 0:NT * HEADS], flat(core.cum),
                                        ALU.subtract).then_inc(sums_copied, 1)
                dve.wait_ge(act_ready, 7)
                nc.vector.tensor_tensor(core.w_end[:, :, :], core.w_end[:, :, :], core.dt[:, :, :], ALU.mult)

            @block.scalar
            def _(act):
                act.wait_ge(dve_step, 1)
                nc.scalar.activation(one_plus[:, :, :], pre[:, :, :], ACT.Abs).then_inc(abs_done, 1)
                act.wait_ge(abs_done, 1)
                nc.scalar.activation(small_exp[:, :, :], one_plus[:, :, :], ACT.Exp, scale=-1.0).then_inc(act_ready, 1)
                nc.scalar.activation(a_exp[:, :], a_log, ACT.Exp).then_inc(act_ready, 1)
                act.wait_ge(dve_step, 2)
                nc.scalar.activation(shifted[:, :, :], shifted[:, :, :], ACT.Exp).then_inc(act_ready, 1)
                act.wait_ge(dve_step, 10)
                nc.scalar.activation(log_1p[:, :, :], one_plus[:, :, :], ACT.Ln).then_inc(act_ready, 1)
                act.wait_ge(sums_copied, 2)
                nc.scalar.activation(core.exp_cum[:, :, :], core.cum[:, :, :], ACT.Exp).then_inc(act_ready, 1)
                nc.scalar.activation(flat(core.exp_total), core.bank[1][:, 0:NT * HEADS], ACT.Exp).then_inc(act_ready, 1)
                nc.scalar.activation(core.w_end[:, :, :], core.w_end[:, :, :], ACT.Exp).then_inc(act_ready, 1)

            @block.tensor
            def _(pe):
                pe.wait_ge(decay_ready, 1)
                nc.tensor.matmul(core.bank[0][:, 0:NT * HEADS], core.upper[:, :], flat(decay), start=True, stop=True).then_inc(sums_ready, 1)
                nc.tensor.matmul(core.bank[1][:, 0:NT * HEADS], core.ones[:, :], flat(decay), start=True, stop=True).then_inc(sums_ready, 1)


def experts0_phase(nc, core, w_up, w_down):
    with ExitStack() as ctx:
        sb = lambda name, shape, dt=F32: ctx.enter_context(nc.sbuf_tensor("m0_" + name, shape, dt))
        sem = lambda name: ctx.enter_context(nc.semaphore("m0_" + name))
        hidden = sb("hidden", [P, 2, SEQ])
        gated = sb("gated", [P, UPS, SEQ])
        gates = sb("gates", [P, 2, TILES, P])
        up_done, gelu_done, gates_in, spread_done, gated_done, down_done, added = (
            sem("up_done"), sem("gelu_done"), sem("gates_in"), sem("spread_done"), sem("gated_done"),
            sem("down_done"), sem("added"))
        ps_up = core.bank[0:3]
        ps_spread = core.bank[3:5]
        ps_down = core.bank[5]
        ROUTED = UPS - 1

        with nc.Block() as block:
            @block.tensor
            def _(pe):
                def up(n, m):
                    wait(pe, gelu_done, n * UPS + m - 2)
                    nc.tensor.matmul(ps_up[m % 3][:, :], w_up[:, m * P:(m + 1) * P], core.xnT[:, bass.ds(n * SEQ, SEQ)],
                                     start=True, stop=True).then_inc(up_done, 1)

                def spread(n, m):
                    pe.wait_ge(gates_in, n * ROUTED + m)
                    wait(pe, gated_done, n * ROUTED + m - 2)
                    for c in range(TILES):
                        last = nc.tensor.transpose(ps_spread[(m - 1) % 2][:, c * P:(c + 1) * P],
                                                   gates[:, (m - 1) % 2, c, :], core.ident[:, :])
                    last.then_inc(spread_done, 1)

                def down(n, m):
                    if m == 0:
                        pe.wait_ge(gelu_done, n * UPS + 1)
                        wait(pe, added, n)
                    else:
                        pe.wait_ge(gated_done, n * ROUTED + m)
                    for c in range(TILES):
                        last = nc.tensor.matmul(ps_down[:, c * P:(c + 1) * P], gated[:, m, c * P:(c + 1) * P],
                                                w_down[:, m * P:(m + 1) * P], start=(m == 0 and c == 0),
                                                stop=(m == UPS - 1), skip_group_check=True)
                    last.then_inc(down_done, 1)

                def sequence(n):
                    for m in range(UPS):
                        up(n, m)
                        if m:
                            spread(n, m)
                        if m >= 2:
                            down(n, m - 2)
                        elif live(n, 0, 1):
                            down(n - 1, UPS + m - 2)
                over_sequences(pe, sequence)
                down(BATCH - 1, UPS - 2)
                down(BATCH - 1, UPS - 1)

            @block.scalar
            def _(act):
                def sequence(n):
                    for m in range(UPS):
                        act.wait_ge(up_done, n * UPS + m + 1)
                        if m == 0:
                            wait(act, down_done, (n - 1) * UPS + 1)
                            out = gated[:, 0, :]
                        else:
                            wait(act, gated_done, n * ROUTED + m - 2)
                            out = hidden[:, (m - 1) % 2, :]
                        nc.scalar.activation(out, ps_up[m % 3][:, :], ACT.Gelu).then_inc(gelu_done, 1)
                over_sequences(act, sequence)

            @block.gpsimd
            def _(pool):
                def sequence(n):
                    for m in range(1, UPS):
                        wait(pool, spread_done, n * ROUTED + m - 2)
                        nc.gpsimd.tensor_copy(
                            gates[:, (m - 1) % 2, :, :].rearrange("p c (e u) -> p c e u", e=2),
                            core.gates0[:, bass.ds(n * TILES, TILES), 2 * (m - 1):2 * m].unsqueeze(3).to_broadcast(
                                [P, TILES, 2, EDIM0])).then_inc(gates_in, 1)
                over_sequences(pool, sequence)

            @block.vector
            def _(dve):
                def add(n):
                    dve.wait_ge(down_done, (n + 1) * UPS)
                    here = core.x[:, bass.ds(n * SEQ, SEQ)]
                    nc.vector.tensor_tensor(here, ps_down[:, :], here, ALU.add).then_inc(added, 1)

                def sequence(n):
                    for m in range(1, UPS):
                        dve.wait_ge(gelu_done, n * UPS + m + 1)
                        dve.wait_ge(spread_done, n * ROUTED + m)
                        wait(dve, down_done, (n - 1) * UPS + m + 1)
                        nc.vector.tensor_tensor(gated[:, m, :], ps_spread[(m - 1) % 2][:, :], hidden[:, (m - 1) % 2, :],
                                                ALU.mult).then_inc(gated_done, 1)
                        if m == 1 and live(n, 0, 1):
                            add(n - 1)
                over_sequences(dve, sequence)
                add(BATCH - 1)


def skip_phase(nc, core, w_zx, w_out):
    with ExitStack() as ctx:
        sb = lambda name, shape, dt=F32: ctx.enter_context(nc.sbuf_tensor("sk_" + name, shape, dt))
        sem = lambda name: ctx.enter_context(nc.semaphore("sk_" + name))
        silu = sb("silu", [P, 2, SEQ])
        skip = sb("skip", [P, 2, SEQ])
        in_done, silu_done, skip_done, out_done, added = (
            sem("in_done"), sem("silu_done"), sem("skip_done"), sem("out_done"), sem("added"))
        ps_in = core.bank[0:4]
        ps_out = core.bank[4]
        with nc.Block() as block:
            @block.tensor
            def _(pe):
                def project(n):
                    for u in range(4):
                        k = u // 2
                        wait(pe, silu_done if u % 2 == 0 else skip_done, 2 * (n - 1) + k + 1)
                        nc.tensor.matmul(ps_in[u][:, :], w_zx[:, u * P:(u + 1) * P], core.xnT[:, bass.ds(n * SEQ, SEQ)],
                                         start=True, stop=True).then_inc(in_done, 1)

                def out(n):
                    pe.wait_ge(skip_done, 2 * n + 2)
                    wait(pe, added, n)
                    for k in range(2):
                        for c in range(TILES):
                            last = nc.tensor.matmul(ps_out[:, c * P:(c + 1) * P], skip[:, k, c * P:(c + 1) * P],
                                                    w_out[:, k * P:(k + 1) * P], start=(k == 0 and c == 0), stop=(k == 1),
                                                    skip_group_check=True)
                    last.then_inc(out_done, 1)

                def sequence(n):
                    project(n)
                    if live(n, 0, 1):
                        out(n - 1)
                over_sequences(pe, sequence)
                out(BATCH - 1)

            @block.scalar
            def _(act):
                def sequence(n):
                    for k in range(2):
                        act.wait_ge(in_done, 4 * n + 2 * k + 1)
                        wait(act, skip_done, 2 * (n - 1) + k + 1)
                        nc.scalar.activation(silu[:, k, :], ps_in[2 * k][:, :], ACT.Silu).then_inc(silu_done, 1)
                over_sequences(act, sequence)

            @block.vector
            def _(dve):
                def add(n):
                    dve.wait_ge(out_done, n + 1)
                    here = core.x[:, bass.ds(n * SEQ, SEQ)]
                    nc.vector.tensor_tensor(here, ps_out[:, :], here, ALU.add).then_inc(added, 1)

                def sequence(n):
                    wait(dve, out_done, n)
                    for k in range(2):
                        dve.wait_ge(silu_done, 2 * n + k + 1)
                        dve.wait_ge(in_done, 4 * n + 2 * k + 2)
                        nc.vector.tensor_tensor(skip[:, k, :], ps_in[2 * k + 1][:, :], silu[:, k, :], ALU.mult).then_inc(skip_done, 1)
                    if live(n, 0, 1):
                        add(n - 1)
                over_sequences(dve, sequence)
                add(BATCH - 1)


def conv_phase(nc, core, w_xbc, conv_w, conv_b):
    with ExitStack() as ctx:
        sb = lambda name, shape, dt=F32: ctx.enter_context(nc.sbuf_tensor("cv_" + name, shape, dt))
        sem = lambda name: ctx.enter_context(nc.semaphore("cv_" + name))
        PAD = TAPS - 1
        padded = sb("padded", [P, 3, PAD + SEQ])
        summed = sb("summed", [P, 3, SEQ])
        x_act = sb("x_act", [P, 2, SEQ])
        b_act = sb("b_act", [NSTATE, SEQ])
        ROWS = [P, P, 48]
        pads_zero, in_done, first_tap, taps_done, silu_done, turned, kept = (
            sem("pads_zero"), sem("in_done"), sem("first_tap"), sem("taps_done"), sem("silu_done"), sem("turned"), sem("kept"))
        ps_in = core.bank[0:3]
        ps_turn = core.bank[3:5]
        with nc.Block() as block:
            @block.tensor
            def _(pe):
                def project(n):
                    for m in range(3):
                        wait(pe, first_tap, 3 * (n - 1) + m + 1)
                        nc.tensor.matmul(ps_in[m][:, :], w_xbc[:, m * P:(m + 1) * P],
                                         core.xnT[:, bass.ds(n * SEQ, SEQ)], start=True, stop=True).then_inc(in_done, 1)

                def turn(n):
                    pe.wait_ge(silu_done, 3 * n + 3)
                    for c in range(TILES):
                        t = n * TILES + c
                        pe.wait_ge(kept, t + 1)
                        for k in range(2):
                            nc.tensor.transpose(ps_turn[c % 2][:, k * P:(k + 1) * P], x_act[:, k, c * P:(c + 1) * P], core.ident[:, :])
                        nc.tensor.transpose(ps_turn[c % 2][:, INNER:INNER + NSTATE], b_act[:, c * P:(c + 1) * P],
                                            core.ident[0:NSTATE, 0:NSTATE]).then_inc(turned, 1)

                def sequence(n):
                    project(n)
                    if live(n, 0, 1):
                        turn(n - 1)
                over_sequences(pe, sequence)
                turn(BATCH - 1)

            @block.scalar
            def _(act):
                def sequence(n):
                    for m in range(3):
                        r = ROWS[m]
                        act.wait_ge(in_done, 3 * n + m + 1)
                        wait(act, taps_done, 9 * (n - 1) + 3 * m + 3)
                        wait(act, silu_done, 3 * (n - 1) + m + 1)
                        nc.scalar.activation(padded[0:r, m, PAD:], ps_in[m][0:r, :], ACT.Copy)
                        nc.scalar.activation(summed[0:r, m, :], ps_in[m][0:r, :], ACT.Identity, bias=conv_b[0:r, m:m + 1],
                                             scale=conv_w[0:r, TAPS * m + PAD:TAPS * m + TAPS]).then_inc(first_tap, 1)
                    wait(act, turned, TILES * n)
                    for m in range(2):
                        act.wait_ge(taps_done, 9 * n + 3 * m + 3)
                        nc.scalar.activation(x_act[:, m, :], summed[:, m, :], ACT.Silu).then_inc(silu_done, 1)
                    act.wait_ge(taps_done, 9 * n + 9)
                    nc.scalar.activation(b_act[:, :], summed[0:NSTATE, 2, :], ACT.Silu)
                    nc.scalar.activation(core.b_rows[:, 0, bass.ds(n * SEQ, SEQ)], summed[0:NSTATE, 2, :], ACT.Silu)
                    nc.scalar.activation(core.b_rows[:, 1, bass.ds(n * SEQ, SEQ)], summed[32:32 + NSTATE, 2, :],
                                         ACT.Silu).then_inc(silu_done, 1)
                over_sequences(act, sequence)

            @block.vector
            def _(dve):
                dve.sem_inc(kept, 2)
                nc.vector.memset(padded[:, :, 0:PAD], 0.0).then_inc(pads_zero, 1)
                dve.wait_ge(pads_zero, 1)

                def keep(n):
                    for c in range(TILES):
                        t = n * TILES + c
                        dve.wait_ge(turned, t + 1)
                        nc.vector.tensor_copy(core.x_tokens[:, bass.ds(t, 1), :].rearrange("p o c -> p (o c)"),
                                              ps_turn[c % 2][:, 0:INNER + NSTATE]).then_inc(kept, 1)

                def sequence(n):
                    for m in range(3):
                        r = ROWS[m]
                        dve.wait_ge(first_tap, 3 * n + m + 1)
                        for k in range(PAD):
                            if k:
                                dve.wait_ge(taps_done, 9 * n + 3 * m + k)
                            nc.vector.scalar_tensor_tensor(summed[0:r, m, :], padded[0:r, m, k:k + SEQ],
                                                           conv_w[0:r, TAPS * m + k:TAPS * m + k + 1], summed[0:r, m, :],
                                                           ALU.mult, ALU.add).then_inc(taps_done, 1)
                    if live(n, 0, 1):
                        keep(n - 1)
                over_sequences(dve, sequence)
                keep(BATCH - 1)


def ssm_phase(nc, core, w_gate, w_out, gamma, beta, b_gate, d_param):
    with ExitStack() as ctx:
        sb = lambda name, shape, dt=F32: ctx.enter_context(nc.sbuf_tensor("ss_" + name, shape, dt))
        sem = lambda name: ctx.enter_context(nc.semaphore("ss_" + name))
        cum_local = sb("cum_local", [P, 2, HEADS])
        b_local = sb("b_local", [NSTATE, 2, P])
        c_local = sb("c_local", [NSTATE, 2, P])
        b_tokens = sb("b_tokens", [P, 2, NSTATE])
        x_dt = sb("x_dt", [P, 2, INNER])
        x_end = sb("x_end", [P, 2, INNER])
        x_d = sb("x_d", [P, 2, INNER])
        mix = sb("mix", [P, HEADS, P])
        bc = sb("bc", [P, P])
        weights = sb("weights", [P, HEADS, P])
        state = sb("state", [NSTATE, 2, INNER])
        y = sb("y", [P, 2, INNER])
        stats = sb("stats", [P, 2, 6])
        mean_var = sb("mean_var", [P, 2, 2])
        var_eps = sb("var_eps", [P, 2])
        rstd = sb("rstd", [P, 2])
        y_norm = sb("y_norm", [P, 2, INNER])
        yT = sb("yT", [P, 2, SEQ])
        tanh = sb("tanh", [P, 2, SEQ])
        half_bias = sb("half_bias", [P, 2])
        half_out = sb("half_out", [P, 2 * P])
        names = ("halves_ready local_ready spread_done diff_done exp_done weights_done bc_mm bc_done state_mm state_done "
                 "y_mm y_free y_done stats_done mv_done vareps_done rstd_done norm_done turned yT_done gate_mm tanh_done "
                 "gated_done out_done added inter_done scaled_done")
        s = type("Sems", (), {k: sem(k) for k in names.split()})
        ps_spread = core.bank[0:2]
        ps_bc, ps_state, ps_y, ps_turn = core.bank[2], core.bank[3], core.bank[4], core.bank[5]
        ps_gate = core.bank[6:8]
        ps_out = core.bank[6]
        HALF = HEADS // 2
        COPIES = 7
        tile = lambda n, c: n * TILES + c
        per_head = lambda t: t[:, :].unsqueeze(2)

        with nc.Block() as block:
            @block.gpsimd
            def _(pool):
                def prepare(n, c):
                    t = tile(n, c)
                    b = c % 2
                    columns_ = bass.ds(t * P, P)
                    of_tile = lambda a: a[:, bass.ds(t, 1), :].rearrange("p o h -> p (o h)")
                    heads = lambda a: a.unsqueeze(2).to_broadcast([P, HEADS, HDIM])
                    x_t = core.x_tokens[:, bass.ds(t, 1), 0:INNER].rearrange("p o (h d) -> p (o h) d", h=HEADS)
                    wait(pool, s.spread_done, 2 * (t - 1))
                    nc.gpsimd.tensor_copy(cum_local[:, b, :], of_tile(core.cum)).then_inc(s.local_ready, 1)
                    wait(pool, s.y_mm, t - 1)
                    wait(pool, s.y_done, t - 1)
                    nc.gpsimd.tensor_copy(b_local[:, b, :], core.b_rows[:, 0, columns_]).then_inc(s.local_ready, 1)
                    nc.gpsimd.tensor_copy(c_local[:, b, :], core.b_rows[:, 1, columns_]).then_inc(s.local_ready, 1)
                    nc.gpsimd.tensor_copy(b_tokens[:, b, :], core.x_tokens[:, bass.ds(t, 1), INNER:INNER + NSTATE].rearrange(
                        "p o c -> p (o c)")).then_inc(s.local_ready, 1)
                    nc.gpsimd.tensor_tensor(x_dt[:, b, :].rearrange("p (h d) -> p h d", h=HEADS), x_t,
                                            heads(of_tile(core.dt)), ALU.mult).then_inc(s.local_ready, 1)
                    nc.gpsimd.tensor_tensor(x_end[:, b, :].rearrange("p (h d) -> p h d", h=HEADS), x_t,
                                            heads(of_tile(core.w_end)), ALU.mult).then_inc(s.local_ready, 1)
                    nc.gpsimd.tensor_tensor(x_d[:, b, :].rearrange("p (h d) -> p h d", h=HEADS), x_t,
                                            heads(d_param), ALU.mult).then_inc(s.local_ready, 1)

                def root(n, c):
                    t = tile(n, c)
                    b = c % 2
                    pool.wait_ge(s.mv_done, t + 1)
                    nc.gpsimd.tensor_tensor(var_eps[:, b:b + 1], mean_var[:, b, 1:2], core.eps[:, 0:1], ALU.add).then_inc(s.vareps_done, 1)
                    wait(pool, s.norm_done, t - 1)
                    pool.wait_ge(s.vareps_done, t + 1)
                    nc.gpsimd.tensor_tensor(rstd[:, b:b + 1], var_eps[:, b:b + 1], core.minus_half[:, 0:1], ALU.pow).then_inc(s.rstd_done, 1)

                def steps(n):
                    for c in range(TILES):
                        if live(n, c, 0):
                            prepare(n, c)
                        if live(n, c, 2):
                            root(*back(n, c, 2))
                over_sequences(pool, steps)
                steps(BATCH)

            @block.tensor
            def _(pe):
                def chunk(n, c):
                    t = tile(n, c)
                    b = c % 2
                    pe.wait_ge(s.local_ready, COPIES * (t + 1))
                    for half in range(2):
                        wait(pe, s.diff_done, 2 * (t - 1) + half + 1)
                        for h in range(HALF):
                            last = nc.tensor.transpose(ps_spread[half][:, h * P:(h + 1) * P],
                                                       cum_local[:, b, half * HALF + h:half * HALF + h + 1].to_broadcast([P, P]),
                                                       core.ident[:, :])
                        last.then_inc(s.spread_done, 1)
                    wait(pe, s.bc_done, t)
                    nc.tensor.matmul(ps_bc[:, 0:P], b_local[:, b, :], c_local[:, b, :], start=True, stop=True).then_inc(s.bc_mm, 1)
                    if c < TILES - 1:
                        wait(pe, s.state_done, 3 * n + c)
                        nc.tensor.matmul(ps_state[0:NSTATE, 0:INNER], b_tokens[:, b, :], x_end[:, b, :],
                                         start=True, stop=True).then_inc(s.state_mm, 1)

                def outputs(n, c):
                    t = tile(n, c)
                    b = c % 2
                    pe.wait_ge(s.weights_done, 2 * t + 2)
                    wait(pe, s.y_free, t)
                    if c:
                        pe.wait_ge(s.state_done, 3 * n + c)
                        nc.tensor.matmul(ps_y[:, INNER:2 * INNER], c_local[:, b, :], state[:, b, :], start=True, stop=True)
                    for h in range(HEADS):
                        last = nc.tensor.matmul(ps_y[:, h * HDIM:(h + 1) * HDIM], weights[:, h, :],
                                                x_dt[:, b, h * HDIM:(h + 1) * HDIM], start=True, stop=True)
                    last.then_inc(s.y_mm, 1)

                def turn(n, c):
                    t = tile(n, c)
                    pe.wait_ge(s.norm_done, t + 1)
                    wait(pe, s.yT_done, 2 * t)
                    for k in range(2):
                        last = nc.tensor.transpose(ps_turn[:, k * P:(k + 1) * P], y_norm[:, c % 2, k * P:(k + 1) * P], core.ident[:, :])
                    last.then_inc(s.turned, 1)

                def gate(n):
                    pe.wait_ge(s.yT_done, 2 * TILES * (n + 1))
                    pe.wait_ge(s.added, n + 1)
                    for m in range(2):
                        for k in range(2):
                            last = nc.tensor.matmul(ps_gate[m][:, :], w_gate[:, (2 * k + m) * P:(2 * k + m + 1) * P], yT[:, k, :],
                                                    start=(k == 0), stop=(k == 1))
                        last.then_inc(s.gate_mm, 1)

                def out(n):
                    pe.wait_ge(s.gated_done, 2 * n + 2)
                    for k in range(2):
                        for c in range(TILES):
                            last = nc.tensor.matmul(ps_out[:, c * P:(c + 1) * P], tanh[:, k, c * P:(c + 1) * P],
                                                    half_out[:, k * P:(k + 1) * P], start=(k == 0 and c == 0), stop=(k == 1),
                                                    skip_group_check=True)
                    last.then_inc(s.out_done, 1)

                def steps(n):
                    for c in range(TILES):
                        if live(n, c, 0):
                            chunk(n, c)
                        ready = c == TILES - 1 and live(n, 0, 1)
                        if ready:
                            gate(n - 1)
                        if live(n, c, 1):
                            outputs(*back(n, c, 1))
                        if ready:
                            out(n - 1)
                        if live(n, c, 3):
                            turn(*back(n, c, 3))
                pe.sem_inc(s.out_done, 1)
                pe.wait_ge(s.halves_ready, 2)
                over_sequences(pe, steps)
                steps(BATCH)

            @block.scalar
            def _(act):
                def exponentials(n, c):
                    t = tile(n, c)
                    for half in range(2):
                        act.wait_ge(s.diff_done, 2 * t + half + 1)
                        here = mix[:, half * HALF:(half + 1) * HALF, :]
                        nc.scalar.activation(here, here, ACT.Exp).then_inc(s.exp_done, 1)

                def keep(n, c):
                    t = tile(n, c)
                    act.wait_ge(s.turned, t + 1)
                    if c == 0:
                        wait(act, s.gated_done, 2 * n)
                    for k in range(2):
                        nc.scalar.activation(yT[:, k, c * P:(c + 1) * P], ps_turn[:, k * P:(k + 1) * P], ACT.Identity,
                                             bias=beta[:, k:k + 1], scale=gamma[:, k:k + 1]).then_inc(s.yT_done, 1)

                def squash(n):
                    act.wait_ge(s.out_done, n + 1)
                    for m in range(2):
                        act.wait_ge(s.gate_mm, 2 * n + m + 1)
                        nc.scalar.activation(tanh[:, m, :], ps_gate[m][:, :], ACT.Tanh, bias=half_bias[:, m:m + 1],
                                             scale=0.5).then_inc(s.tanh_done, 1)

                def steps(n):
                    for c in range(TILES):
                        if live(n, c, 0):
                            exponentials(n, c)
                        if c == TILES - 1 and live(n, 0, 1):
                            squash(n - 1)
                        if live(n, c, 3):
                            keep(*back(n, c, 3))
                act.wait_ge(s.halves_ready, 2)
                over_sequences(act, steps)
                steps(BATCH)

            @block.vector
            def _(dve):
                dve.sem_inc(s.added, 1)
                nc.vector.tensor_scalar(half_bias[:, :], b_gate, 0.5, None, ALU.mult).then_inc(s.halves_ready, 1)
                nc.vector.tensor_scalar(half_out[:, :], w_out[:, 2 * P:4 * P], 0.5, None, ALU.mult).then_inc(s.halves_ready, 1)

                def differences(n, c):
                    t = tile(n, c)
                    for half in range(2):
                        wait(dve, s.weights_done, 2 * (t - 1) + half + 1)
                        dve.wait_ge(s.spread_done, 2 * t + half + 1)
                        here = core.cum[:, bass.ds(t, 1), half * HALF:(half + 1) * HALF].rearrange("p o h -> p (o h)")
                        nc.vector.tensor_tensor(mix[:, half * HALF:(half + 1) * HALF, :],
                                                ps_spread[half][:, :].rearrange("p (h t) -> p h t", h=HALF),
                                                here.unsqueeze(2).to_broadcast([P, HALF, P]), ALU.subtract).then_inc(s.diff_done, 1)
                    wait(dve, s.weights_done, 2 * t)
                    dve.wait_ge(s.bc_mm, t + 1)
                    nc.vector.tensor_tensor(bc[:, :], ps_bc[:, 0:P], core.upper[:, :], ALU.mult).then_inc(s.bc_done, 1)

                def update_state(n, c):
                    old, new = state[:, c % 2, :], state[:, (c + 1) % 2, :]
                    dve.wait_ge(s.state_mm, 3 * n + c + 1)
                    wait(dve, s.y_mm, tile(n, c))
                    if c == 0:
                        nc.vector.tensor_copy(new, ps_state[0:NSTATE, 0:INNER]).then_inc(s.state_done, 1)
                        return
                    fade = core.exp_total[0:NSTATE, bass.ds(tile(n, c), 1), :].rearrange("p o h -> p (o h)")
                    nc.vector.tensor_tensor(new.rearrange("p (h d) -> p h d", h=HEADS), old.rearrange("p (h d) -> p h d", h=HEADS),
                                            fade.unsqueeze(2).to_broadcast([NSTATE, HEADS, HDIM]), ALU.mult).then_inc(s.scaled_done, 1)
                    dve.wait_ge(s.scaled_done, 2 * n + c)
                    nc.vector.tensor_tensor(new, ps_state[0:NSTATE, 0:INNER], new, ALU.add).then_inc(s.state_done, 1)

                def finish(n, c):
                    t = tile(n, c)
                    b = c % 2
                    here = y[:, b, :]
                    wait(dve, s.norm_done, t - 1)
                    dve.wait_ge(s.y_mm, t + 1)
                    dve.wait_ge(s.local_ready, COPIES * (t + 1))
                    if c:
                        fade = core.exp_cum[:, bass.ds(t, 1), :].rearrange("p o h -> p (o h)")
                        nc.vector.tensor_tensor(here.rearrange("p (h d) -> p h d", h=HEADS),
                                                ps_y[:, INNER:2 * INNER].rearrange("p (h d) -> p h d", h=HEADS),
                                                fade.unsqueeze(2).to_broadcast([P, HEADS, HDIM]), ALU.mult).then_inc(s.inter_done, 1)
                        dve.wait_ge(s.inter_done, 6 * n + 2 * c - 1)
                        nc.vector.tensor_tensor(here, here, x_d[:, b, :], ALU.add).then_inc(s.inter_done, 1)
                        dve.wait_ge(s.inter_done, 6 * n + 2 * c)
                        nc.vector.tensor_tensor(here, ps_y[:, 0:INNER], here, ALU.add).then_inc(s.y_free, 1)
                    else:
                        nc.vector.tensor_tensor(here, ps_y[:, 0:INNER], x_d[:, b, :], ALU.add).then_inc(s.y_free, 1)
                    dve.wait_ge(s.y_free, t + 1)
                    nc.vector.bn_stats(stats[:, b, :], here).then_inc(s.y_done, 1)
                    dve.wait_ge(s.y_done, t + 1)
                    nc.vector.memset(core.spare[:, 0:1], 0.0)
                    nc.vector.bn_aggr(mean_var[:, b, :], stats[:, b, :]).then_inc(s.mv_done, 1)

                def weigh(n, c):
                    t = tile(n, c)
                    dve.wait_ge(s.bc_done, t + 1)
                    wait(dve, s.y_mm, t)
                    for half in range(2):
                        dve.wait_ge(s.exp_done, 2 * t + half + 1)
                        nc.vector.scalar_tensor_tensor(weights[:, half * HALF:(half + 1) * HALF, :],
                                                       mix[:, half * HALF:(half + 1) * HALF, :], 1.0,
                                                       bc[:, :].unsqueeze(1).to_broadcast([P, HALF, P]),
                                                       ALU.min, ALU.mult).then_inc(s.weights_done, 1)

                def normalise(n, c):
                    t = tile(n, c)
                    b = c % 2
                    dve.wait_ge(s.rstd_done, t + 1)
                    wait(dve, s.turned, t - 1)
                    nc.vector.tensor_scalar(y_norm[:, b, :], y[:, b, :], mean_var[:, b, 0:1], rstd[:, b:b + 1],
                                            ALU.subtract, ALU.mult).then_inc(s.norm_done, 1)

                def apply_gate(n):
                    for m in range(2):
                        dve.wait_ge(s.tanh_done, 2 * n + m + 1)
                        nc.vector.scalar_tensor_tensor(tanh[:, m, :], tanh[:, m, :], 1.0, yT[:, m, :],
                                                       ALU.add, ALU.mult).then_inc(s.gated_done, 1)

                def add(n):
                    dve.wait_ge(s.out_done, n + 2)
                    here = core.x[:, bass.ds(n * SEQ, SEQ)]
                    nc.vector.tensor_tensor(here, ps_out[:, :], here, ALU.add).then_inc(s.added, 1)

                def steps(n):
                    for c in range(TILES):
                        if live(n, c, 0):
                            differences(n, c)
                            if c < TILES - 1:
                                update_state(n, c)
                        ready = c == TILES - 1 and live(n, 0, 1)
                        if ready:
                            apply_gate(n - 1)
                        if live(n, c, 1):
                            finish(*back(n, c, 1))
                        if live(n, c, 0):
                            weigh(n, c)
                        if live(n, c, 2):
                            normalise(*back(n, c, 2))
                        if ready:
                            add(n - 1)
                dve.wait_ge(s.halves_ready, 2)
                over_sequences(dve, steps)
                steps(BATCH)


def attention_phase(nc, core, wq, wk, wv, bq, bk, bv, head_mask, same_head, one_hot, key_mask):
    with ExitStack() as ctx:
        sb = lambda name, shape, dt=F32: ctx.enter_context(nc.sbuf_tensor("at_" + name, shape, dt))
        sem = lambda name: ctx.enter_context(nc.semaphore("at_" + name))
        STEPS = TILES * GROUPS
        BT = P // WIN
        RING = 4
        VALUES, VALUES_OUT, SCORES, TURN, WEIGH, PACK, DIVIDE, FINAL = 5, 6, 8, 10, 12, 16, 17, 18
        x_rep = sb("x_rep", [P, BLOCKS, GROUPS, WIN])
        kT = sb("kT", [P, GROUPS, WIN + SEQ + WIN])
        q_rows = sb("q_rows", [P, 2, P])
        q_spread = sb("q_spread", [P, GROUPS, BLOCKS, GROUPS, WIN])
        v_ones = sb("v_ones", [P, BLOCKS * GROUPS, 2 * WIN])
        probs = sb("probs", [P, RING, BT * KEYS])
        probsT = sb("probsT", [P, RING, 3 * BT, WIN])
        largest = sb("largest", [P, RING, BT])
        packed = sb("packed", [P, 2, 2, P])
        inverse = sb("inverse", [P, P])
        attended = sb("attended", [P, 2, P])
        names = ("keys_in cleared set_up x_ready kq_mm k_done q_rows_done q_done v_mm v_done score_mm max_done diff_done exp_done turned "
                 "pv_mm packed_done inverse_done attended_done final_done")
        s = type("Sems", (), {k: sem(k) for k in names.split()})
        ps_score = core.bank[0:RING]
        ps_out = core.bank[4:6]
        ps_kq, ps_v = core.bank[6], core.bank[7]

        def step_back(n, u, lag):
            return n + (u - lag) // STEPS, (u - lag) % STEPS

        def alive(n, u, lag):
            return not isinstance(n, int) or 0 <= n * STEPS + u - lag < BATCH * STEPS

        def one_hot_rows(copy, g):
            others = [r for r in range(GROUPS) if r != g]
            for which, r in enumerate(others):
                rows, blocks = slice(WIN * r, WIN * r + WIN), len(range(which, BLOCKS, 3))
                for h in range(GROUPS):
                    last = copy(q_spread[rows, g, which:BLOCKS:3, h, :], one_hot[rows, :].unsqueeze(1).to_broadcast([WIN, blocks, WIN]))
            last.then_inc(s.set_up, 1)

        def tile_due(n, u, lag):
            if (u - lag) % GROUPS or not alive(n, u, lag):
                return None
            m, v = step_back(n, u, lag)
            return m, v // GROUPS

        def step_due(n, u, lag):
            return step_back(n, u, lag) if alive(n, u, lag) else None

        with nc.Block() as block:
            @block.gpsimd
            def _(pool):
                half = q_spread[:, 2:4, :, :, :]
                nc.gpsimd.memset(half.rearrange("p g b h q -> p (g b h q)"), 0.0).then_inc(s.cleared, 1)

                def repeat_tokens(n, j):
                    t = TILES * n + j
                    wait(pool, s.v_mm, t - TILES + 1 if isinstance(n, int) else TILES * (n - 1) + j + 1)
                    wait(pool, s.q_done, GROUPS * (t - 1))
                    nc.gpsimd.tensor_copy(x_rep[:, j * BT:(j + 1) * BT, :, :],
                                          core.xnT[:, bass.ds(t * P, P)].rearrange("p (b q) -> p b q", q=WIN)
                                          .unsqueeze(2).to_broadcast([P, BT, GROUPS, WIN])).then_inc(s.x_ready, 1)

                def spread_queries(n, j):
                    pool.wait_ge(s.q_rows_done, TILES * n + j + 1)
                    wait(pool, s.score_mm, STEPS * n + GROUPS * (j - 3))
                    pool.wait_ge(s.x_ready, min(TILES * n + j + 2, NT) if isinstance(n, int) else TILES * n + j + 2)
                    for g in range(GROUPS):
                        rows = slice(WIN * g, WIN * g + WIN)
                        all_heads = [WIN, BT, GROUPS, WIN]
                        wait(pool, s.q_done, GROUPS * (TILES * n + j) + g)
                        nc.gpsimd.tensor_tensor(
                            q_spread[rows, g, j * BT:(j + 1) * BT, :, :],
                            q_rows[rows, j % 2, :].rearrange("p (b q) -> p b q", q=WIN).unsqueeze(2).to_broadcast(all_heads),
                            head_mask[rows, :].unsqueeze(1).unsqueeze(3).to_broadcast(all_heads), ALU.mult).then_inc(s.q_done, 1)

                SENDING = 4
                A_TILE = NT // (SENDING * TILES)

                def steps(n):
                    for j in range(TILES):
                        if live(n, j, 0):
                            repeat_tokens(n, j)
                        if live(n, j, 1):
                            if isinstance(n, int) and n == 0 and j == 1:
                                pool.wait_ge(s.set_up, 5)
                            if isinstance(n, int):
                                pool.wait_ge(core.scattered, 16 * A_TILE * (n * TILES + j))
                            spread_queries(*back(n, j, 1))
                        if isinstance(n, int) and n < SENDING:
                            if n == 0 and j == 0:
                                pool.wait_ge(core.cleared, 16)
                            wait(pool, s.q_done, GROUPS * (n * TILES + j))
                            for i in range(A_TILE):
                                scatter_tile(nc, core, (n * TILES + j) * A_TILE + i)
                for n in range(SENDING):
                    steps(n)
                pool.wait_ge(core.scattered, 16 * NT)
                with pool.Fori(SENDING, BATCH) as n:
                    steps(n)
                spread_queries(BATCH - 1, TILES - 1)

            @block.sync
            def _(sp):
                sp.dma_start(kT[:, :, :].rearrange("p g k -> p (g k)"), key_mask).then_inc(s.keys_in, 16)

            @block.tensor
            def _(pe):
                def keys_queries(n, j):
                    t = TILES * n + j
                    pe.wait_ge(s.x_ready, t + 1)
                    wait(pe, s.q_rows_done, t)
                    tokens = x_rep[:, j * BT:(j + 1) * BT, 0, :]
                    nc.tensor.matmul(ps_kq[:, 0:P], wk, tokens, start=True, stop=True)
                    nc.tensor.matmul(ps_kq[:, P:2 * P], wq, tokens, start=True, stop=True).then_inc(s.kq_mm, 1)

                def values(n, j):
                    wait(pe, s.v_done, TILES * n + j)
                    for b in range(BT):
                        last = nc.tensor.matmul(ps_v[:, b * P:(b + 1) * P], x_rep[:, j * BT + b, :, :].rearrange("p r k -> p (r k)"),
                                                wv, start=True, stop=True)
                    last.then_inc(s.v_mm, 1)

                def scores(n, u):
                    j, g = u // GROUPS, u % GROUPS
                    t = n * STEPS + u
                    bank = ps_score[u % RING]
                    if g == 0:
                        pe.wait_ge(s.q_done, GROUPS * (TILES * n + j + 1))
                        pe.wait_ge(s.k_done, TILES * n + j + (1 if j == TILES - 1 else 2))
                    wait(pe, s.diff_done, t - RING + 1)
                    for b in range(BT):
                        blk = j * BT + b
                        last = nc.tensor.matmul(bank[:, b * KEYS:(b + 1) * KEYS],
                                                q_spread[:, g, blk, :, :].rearrange("p h q -> p (h q)"),
                                                kT[:, g, blk * WIN:blk * WIN + KEYS], start=True, stop=True)
                    last.then_inc(s.score_mm, 1)

                def weigh_values(n, u):
                    t = n * STEPS + u
                    j, g = u // GROUPS, u % GROUPS
                    if g == 0:
                        pe.wait_ge(s.v_done, TILES * n + j + (1 if j == TILES - 1 else 2))
                        wait(pe, s.packed_done, TILES * n + j - 1)
                    pe.wait_ge(s.turned, t + 1)
                    half = slice(64 * (g % 2), 64 * (g % 2) + 64)
                    first = g < 2
                    for d in range(-1, BT + 1):
                        c = j * BT + d
                        if not 0 <= c < BLOCKS:
                            continue
                        b0, b1 = max(0, d - 1), min(BT - 1, d + 1)
                        nb, at = b1 - b0 + 1, b0 * 3 + d + 1 - b0
                        last = nc.tensor.matmul(ps_out[j % 2][half, (g // 2) * P + b0 * WIN:(g // 2) * P + (b1 + 1) * WIN],
                                                v_ones[:, c * GROUPS + g, :], probsT[:, u % RING, at:at + 2 * nb - 1:2, :],
                                                start=first, stop=True, skip_group_check=True)
                        first = False
                    last.then_inc(s.pv_mm, 1)

                def steps(n):
                    for u in range(STEPS):
                        if tile := tile_due(n, u, 0):
                            keys_queries(*tile)
                        if tile := tile_due(n, u, VALUES):
                            values(*tile)
                        if step := step_due(n, u, SCORES):
                            scores(*step)
                        if step := step_due(n, u, WEIGH):
                            weigh_values(*step)
                pe.wait_ge(s.set_up, 5)
                over_sequences(pe, steps)
                steps(BATCH)

            @block.scalar
            def _(act):
                def keys_queries(n, j):
                    t = TILES * n + j
                    act.wait_ge(s.kq_mm, t + 1)
                    wait(act, s.score_mm, STEPS * n + GROUPS * (j - 2))
                    for g in range(GROUPS):
                        rows = slice(WIN * g, WIN * g + WIN)
                        last = nc.scalar.activation(kT[rows, g, WIN + j * P:WIN + (j + 1) * P], ps_kq[rows, 0:P], ACT.Identity, bias=bk[rows, :])
                    last.then_inc(s.k_done, 1)
                    wait(act, s.q_done, GROUPS * (t - 1))
                    nc.scalar.activation(q_rows[:, j % 2, :], ps_kq[:, P:2 * P], ACT.Identity, bias=bq).then_inc(s.q_rows_done, 1)

                def exponential(n, u):
                    act.wait_ge(s.diff_done, n * STEPS + u + 1)
                    here = probs[:, u % RING, :]
                    nc.scalar.activation(here, here, ACT.Exp).then_inc(s.exp_done, 1)

                def pack(n, j):
                    t = TILES * n + j
                    act.wait_ge(s.pv_mm, GROUPS * (t + 1))
                    if live(n, j, 1):
                        act.wait_ge(s.attended_done, t)
                    for g in range(GROUPS):
                        for what in range(2):
                            at = 64 * (g % 2) + WIN * what
                            last = nc.scalar.activation(packed[WIN * g:WIN * (g + 1), j % 2, what, :],
                                                        ps_out[j % 2][at:at + WIN, (g // 2) * P:(g // 2 + 1) * P], ACT.Copy)
                    last.then_inc(s.packed_done, 1)

                def final(n, j):
                    t = TILES * n + j
                    act.wait_ge(s.attended_done, t + 2)
                    nc.scalar.activation(core.xnT[:, bass.ds(t * P, P)], attended[:, j % 2, :], ACT.Identity, bias=bv).then_inc(s.final_done, 1)

                def steps(n):
                    for u in range(STEPS):
                        if tile := tile_due(n, u, 0):
                            keys_queries(*tile)
                        if step := step_due(n, u, SCORES):
                            exponential(*step)
                        if tile := tile_due(n, u, PACK):
                            pack(*tile)
                        if tile := tile_due(n, u, FINAL):
                            final(*tile)
                act.sem_inc(s.final_done, 1)
                act.wait_ge(s.keys_in, 16)
                act.wait_ge(s.cleared, 2)
                for g in (2, 3):
                    one_hot_rows(nc.scalar.copy, g)
                over_sequences(act, steps)
                steps(BATCH)

            @block.vector
            def _(dve):
                dve.wait_ge(core.params1_in, core.params1_count)
                nc.vector.memset(q_spread[:, 0:2, :, :, :].rearrange("p g b h q -> p (g b h q)"), 0.0).then_inc(s.cleared, 1)
                dve.wait_ge(s.cleared, 2)
                for g in (0, 1):
                    one_hot_rows(nc.vector.tensor_copy, g)
                heads = same_head.unsqueeze(1)
                dve.sem_inc(s.attended_done, 1)
                nc.vector.tensor_copy(v_ones[:, :, WIN:], heads.to_broadcast([P, BLOCKS * GROUPS, WIN])).then_inc(s.set_up, 1)

                def values(n, j):
                    t = TILES * n + j
                    dve.wait_ge(s.v_mm, t + 1)
                    wait(dve, s.pv_mm, STEPS * n + GROUPS * (j - 2))
                    nc.vector.tensor_tensor(v_ones[:, j * STEPS:(j + 1) * STEPS, 0:WIN], ps_v[:, :].rearrange("k (a d) -> k a d", d=WIN),
                                            heads.to_broadcast([P, STEPS, WIN]), ALU.mult).then_inc(s.v_done, 1)

                def maximum(n, u):
                    t = n * STEPS + u
                    dve.wait_ge(s.score_mm, t + 1)
                    wait(dve, s.diff_done, t - RING + 1)
                    nc.vector.tensor_reduce(largest[:, u % RING, :], ps_score[u % RING][:, 0:BT * KEYS].rearrange("p (b k) -> p b k", k=KEYS),
                                            AXX, ALU.max).then_inc(s.max_done, 1)

                def differences(n, u):
                    t = n * STEPS + u
                    dve.wait_ge(s.max_done, t + 1)
                    wait(dve, s.turned, t - RING + 1)
                    nc.vector.tensor_tensor(probs[:, u % RING, :].rearrange("p (b k) -> p b k", k=KEYS),
                                            ps_score[u % RING][:, 0:BT * KEYS].rearrange("p (b k) -> p b k", k=KEYS),
                                            largest[:, u % RING, :].unsqueeze(2).to_broadcast([P, BT, KEYS]),
                                            ALU.subtract).then_inc(s.diff_done, 1)

                def turn(n, u):
                    t = n * STEPS + u
                    dve.wait_ge(s.exp_done, t + 1)
                    wait(dve, s.pv_mm, t - RING + 1)
                    nc.vector.transpose(probsT[:, u % RING, :, :].rearrange("p a q -> p (a q)"), probs[:, u % RING, :]).then_inc(s.turned, 1)

                def divide(n, j):
                    t = TILES * n + j
                    dve.wait_ge(s.packed_done, t + 1)
                    dve.wait_ge(s.attended_done, t + 1)
                    nc.vector.reciprocal(inverse[:, :], packed[:, j % 2, 1, :]).then_inc(s.inverse_done, 1)
                    dve.wait_ge(s.inverse_done, t + 1)
                    wait(dve, s.final_done, t)
                    nc.vector.tensor_tensor(attended[:, j % 2, :], packed[:, j % 2, 0, :], inverse[:, :], ALU.mult).then_inc(s.attended_done, 1)

                def steps(n):
                    for u in range(STEPS):
                        if tile := tile_due(n, u, VALUES_OUT):
                            values(*tile)
                        if step := step_due(n, u, SCORES):
                            maximum(*step)
                        if step := step_due(n, u, TURN):
                            turn(*step)
                        if step := step_due(n, u, SCORES):
                            differences(*step)
                        if tile := tile_due(n, u, DIVIDE):
                            divide(*tile)
                over_sequences(dve, steps)
                steps(BATCH)


def mlp_phase(nc, core, wo, w_f1, w_f2, c1, bo, g1, b1, c2, g2, b2):
    with ExitStack() as ctx:
        sb = lambda name, shape, dt=F32: ctx.enter_context(nc.sbuf_tensor("ml_" + name, shape, dt))
        sem = lambda name: ctx.enter_context(nc.semaphore("ml_" + name))
        HID = FFN // P
        ALL = [P, TILES, P]
        aT = sb("aT", [P, SEQ])
        base = sb("base", ALL)
        raw = [sb("raw0", ALL), sb("raw1", ALL)]
        stats = [sb("stats0", [P, TILES, 6]), sb("stats1", [P, TILES, 6])]
        mean_var = [sb("mv0", [P, TILES, 2]), sb("mv1", [P, TILES, 2])]
        var_eps = [sb("ve0", [P, TILES]), sb("ve1", [P, TILES])]
        rstd = [sb("rstd0", [P, TILES]), sb("rstd1", [P, TILES])]
        h = sb("h", ALL)
        h_c2 = sb("h_c2", ALL)
        hT = sb("hT", [P, SEQ])
        hidden = sb("hidden", [P, HID, SEQ])
        names = "a_ready base_part base_ready wo_mm h_part h_done h_c2_done turned hT_done f1_mm gelu_done f2_mm tail_part added"
        s = type("Sems", (), {k: sem(k) for k in names.split()})
        raw_done, stats_done, mv_done, vareps_done, rstd_done, norm_done = (
            [sem(f"{k}{i}") for i in range(2)] for k in ("raw_done", "stats_done", "mv_done", "vareps_done", "rstd_done", "norm_done"))
        ps_wo, ps_turn, ps_f2 = core.bank[0], core.bank[1], core.bank[2]
        ps_f1 = core.bank[3:5]
        row = lambda r: r.unsqueeze(1).to_broadcast(ALL)
        tiles = lambda bank: bank[:, :].rearrange("p (c d) -> p c d", c=TILES)
        here = lambda t, n: t[:, bass.ds(n * SEQ, SEQ)].rearrange("p (c d) -> p c d", c=TILES)

        with nc.Block() as block:
            @block.gpsimd
            def _(pool):
                def inputs(n):
                    wait(pool, s.wo_mm, n)
                    nc.gpsimd.tensor_copy(aT[:, :], core.xnT[:, bass.ds(n * SEQ, SEQ)]).then_inc(s.a_ready, 1)
                    wait(pool, raw_done[0], n)
                    nc.gpsimd.tensor_copy(base[:, :, :], here(core.xn2, n)).then_inc(s.base_part, 1)
                    pool.wait_ge(s.base_part, n + 1)
                    nc.gpsimd.tensor_tensor(base[:, :, :], base[:, :, :], row(bo), ALU.add).then_inc(s.base_ready, 1)

                def root(n, i):
                    pool.wait_ge(mv_done[i], TILES * (n + 1))
                    nc.gpsimd.tensor_tensor(var_eps[i][:, :], mean_var[i][:, :, 1], core.eps[:, 0:TILES], ALU.add).then_inc(vareps_done[i], 1)
                    pool.wait_ge(vareps_done[i], n + 1)
                    nc.gpsimd.tensor_tensor(rstd[i][:, :], var_eps[i][:, :], core.minus_half[:, 0:TILES], ALU.pow).then_inc(rstd_done[i], 1)

                def scale_h(n):
                    pool.wait_ge(norm_done[0], TILES * (n + 1))
                    wait(pool, s.turned, n)
                    wait(pool, s.h_c2_done, n)
                    nc.gpsimd.tensor_tensor(h[:, :, :], raw[0][:, :, :], row(g1), ALU.mult).then_inc(s.h_part, 1)
                    pool.wait_ge(s.h_part, n + 1)
                    nc.gpsimd.tensor_tensor(h[:, :, :], h[:, :, :], row(b1), ALU.add).then_inc(s.h_done, 1)
                    pool.wait_ge(s.h_done, n + 1)
                    if live(n, 0, 1):
                        pool.wait_ge(raw_done[1], n + 1)
                    nc.gpsimd.tensor_tensor(h_c2[:, :, :], h[:, :, :], row(c2), ALU.add).then_inc(s.h_c2_done, 1)

                def finish(n):
                    pool.wait_ge(norm_done[1], TILES * (n + 1))
                    r = raw[1][:, :, :]
                    nc.gpsimd.tensor_tensor(r, r, row(g2), ALU.mult).then_inc(s.tail_part, 1)
                    pool.wait_ge(s.tail_part, 2 * n + 1)
                    nc.gpsimd.tensor_tensor(r, r, row(b2), ALU.add).then_inc(s.tail_part, 1)

                def steps(n):
                    if live(n, 0, 0):
                        inputs(n)
                        root(n, 0)
                        scale_h(n)
                    if live(n, 0, 1):
                        root(n - 1, 1)
                        finish(n - 1)
                over_sequences(pool, steps)
                steps(BATCH)

            @block.tensor
            def _(pe):
                def project(n):
                    pe.wait_ge(s.a_ready, n + 1)
                    wait(pe, raw_done[0], n)
                    for c in range(TILES):
                        last = nc.tensor.matmul(ps_wo[:, c * P:(c + 1) * P], aT[:, c * P:(c + 1) * P], wo, start=True, stop=True)
                    last.then_inc(s.wo_mm, 1)

                def mlp(n):
                    pe.wait_ge(s.h_done, n + 1)
                    for c in range(TILES):
                        last = nc.tensor.transpose(ps_turn[:, c * P:(c + 1) * P], h[:, c, :], core.ident[:, :])
                    last.then_inc(s.turned, 1)
                    pe.wait_ge(s.hT_done, n + 1)
                    for m in range(HID):
                        if m >= 2:
                            pe.wait_ge(s.gelu_done, HID * n + m - 1)
                        nc.tensor.matmul(ps_f1[m % 2][:, :], w_f1[:, m * P:(m + 1) * P], hT[:, :], start=True, stop=True).then_inc(s.f1_mm, 1)
                    if not isinstance(n, int) or n:
                        pe.wait_ge(raw_done[1], n + 1)
                    for m in range(HID):
                        pe.wait_ge(s.gelu_done, HID * n + m + 1)
                        for c in range(TILES):
                            last = nc.tensor.matmul(ps_f2[:, c * P:(c + 1) * P], hidden[:, m, c * P:(c + 1) * P],
                                                    w_f2[:, m * P:(m + 1) * P], start=(m == 0 and c == 0), stop=(m == HID - 1),
                                                    skip_group_check=True)
                    last.then_inc(s.f2_mm, 1)

                def steps(n):
                    if live(n, 0, 0):
                        project(n)
                    if live(n, 0, 1):
                        mlp(n - 1)
                over_sequences(pe, steps)
                steps(BATCH)

            @block.scalar
            def _(act):
                def steps(n):
                    act.wait_ge(s.turned, n + 1)
                    nc.scalar.activation(hT[:, :], ps_turn[:, :], ACT.Copy).then_inc(s.hT_done, 1)
                    wait(act, s.f2_mm, n)
                    for m in range(HID):
                        act.wait_ge(s.f1_mm, HID * n + m + 1)
                        nc.scalar.activation(hidden[:, m, :], ps_f1[m % 2][:, :], ACT.Gelu_apprx_tanh,
                                             bias=c1[:, m:m + 1]).then_inc(s.gelu_done, 1)
                over_sequences(act, steps)

            @block.vector
            def _(dve):
                dve.sem_inc(raw_done[1], 1)

                def statistics(n, i):
                    for c in range(TILES):
                        nc.vector.bn_stats(stats[i][:, c, :], raw[i][:, c, :]).then_inc(stats_done[i], 1)
                    dve.wait_ge(stats_done[i], TILES * (n + 1))
                    nc.vector.memset(core.spare[:, 0:1], 0.0)
                    for c in range(TILES):
                        nc.vector.bn_aggr(mean_var[i][:, c, :], stats[i][:, c, :]).then_inc(mv_done[i], 1)

                def normalise(n, i):
                    dve.wait_ge(rstd_done[i], n + 1)
                    for c in range(TILES):
                        nc.vector.tensor_scalar(raw[i][:, c, :], raw[i][:, c, :], mean_var[i][:, c, 0:1], rstd[i][:, c:c + 1],
                                                ALU.subtract, ALU.mult).then_inc(norm_done[i], 1)

                def first(n):
                    dve.wait_ge(s.wo_mm, n + 1)
                    dve.wait_ge(s.base_ready, n + 1)
                    wait(dve, s.h_part, n)
                    nc.vector.tensor_tensor(raw[0][:, :, :], tiles(ps_wo), base[:, :, :], ALU.add).then_inc(raw_done[0], 1)
                    dve.wait_ge(raw_done[0], n + 1)
                    statistics(n, 0)
                    normalise(n, 0)

                def second(n):
                    dve.wait_ge(s.f2_mm, n + 1)
                    dve.wait_ge(s.h_c2_done, n + 1)
                    nc.vector.tensor_tensor(raw[1][:, :, :], tiles(ps_f2), h_c2[:, :, :], ALU.add).then_inc(raw_done[1], 1)
                    dve.wait_ge(raw_done[1], n + 2)
                    statistics(n, 1)
                    normalise(n, 1)
                    dve.wait_ge(s.tail_part, 2 * n + 2)
                    nc.vector.tensor_tensor(here(core.x, n), here(core.x, n), raw[1][:, :, :], ALU.add).then_inc(s.added, 1)
                    dve.wait_ge(s.added, n + 1)

                def steps(n):
                    if live(n, 0, 0):
                        first(n)
                    if live(n, 0, 1):
                        second(n - 1)
                over_sequences(dve, steps)
                steps(BATCH)


def layer1(nc, core, ins, out_rows):
    with ExitStack() as layer:
        lsb = lambda name, shape, dt=F32: layer.enter_context(nc.sbuf_tensor(name, shape, dt))
        lsem = lambda name: layer.enter_context(nc.semaphore(name))
        at_w1, n_w1 = columns(W1)
        at_c1, n_c1 = columns(C1)
        at_r1, n_r1 = columns(R1)
        w1 = lsb("w1", [P, n_w1])
        c1 = lsb("c1", [P, n_c1 + GROUPS + 2 * WIN])
        r1 = lsb("r1", [P, n_r1])
        core.xn2 = lsb("xn2", [P, NT * P])
        logits = lsb("logits1", [P, NT, EXP1])
        top8 = lsb("top1", [P, NT, 8])
        core.params1_in, core.params1_count = lsem("params1_in"), 48
        W = lambda name: w1[:, at_w1[name][0]:at_w1[name][1]]
        C = lambda name: c1[:, at_c1[name][0]:at_c1[name][1]]
        R = lambda name: r1[:, at_r1[name][0]:at_r1[name][1]]
        with nc.Block() as block:
            @block.sync
            def _(sp):
                sp.dma_start(w1[:, :], ins["w1"]).then_inc(core.params1_in, 16)
                sp.dma_start(c1[:, :], ins["c1"]).then_inc(core.params1_in, 16)
                sp.dma_start(r1[:, :], ins["r1"].partition_broadcast(P)).then_inc(core.params1_in, 16)
                sp.wait_ge(core.params1_in, 48)
        routing1(nc, core, ins, layer, logits, top8)
        norm_phase(nc, core, "n1_", core.x, None, W("w_small1"), EXP1, EXP1, R("gate_b"), logits, top8, core.xn2)
        places_phase(nc, core, logits, top8)
        attention_phase(nc, core, W("wq"), W("wk"), W("wv"), C("bq"), C("bk"), C("bv"), c1[:, n_c1:n_c1 + GROUPS],
                        c1[:, n_c1 + GROUPS:n_c1 + GROUPS + WIN], c1[:, n_c1 + GROUPS + WIN:], ins["key_mask"])
        experts1_load(nc, core, ins, layer)
        mlp_phase(nc, core, W("wo"), W("w_f1"), W("w_f2"), C("c1"), R("bo"), R("g1"), R("b1"), R("c2"), R("g2"), R("b2"))
        experts1_phase(nc, core, core.sorted_x, core.sorted_y, *core.expert_weights)
        gather_phase(nc, core, out_rows)


def layer1_arrays(a, pack, slices):
    channel = np.arange(P)
    query, key = np.arange(WIN)[:, None], np.arange(WIN)[None, :]
    key_mask = np.zeros((GROUPS, WIN, GROUPS, BLOCKS + 2, WIN), np.float32)
    for g in range(GROUPS):
        for which, r in enumerate([r for r in range(GROUPS) if r != g]):
            for blk in range(which, BLOCKS, 3):
                key_mask[r, :, g, blk] = np.where((key >= query) & (blk > 0), 0.0, -1e30)
                key_mask[r, :, g, blk + 2] = np.where((key <= query) & (blk < BLOCKS - 1), 0.0, -1e30)
    head_mask = ((channel[:, None] // AHD) % GROUPS == np.arange(GROUPS)) / np.sqrt(AHD)
    one_hot = channel[:, None] % WIN == np.arange(WIN)
    same_head = channel[:, None] // WIN == np.arange(WIN) // AHD
    arrays = {
        "w1": pack(W1, {"w_small1": a["L1_ffn_gate_w"].T, "wq": a["L1_attn_Wq"], "wk": a["L1_attn_Wk"], "wv": a["L1_attn_Wv"],
                        "wo": a["L1_attn_Wo"], "w_f1": a["L1_attn_W1"], "w_f2": slices(a["L1_attn_W2"])}),
        "c1": np.concatenate([pack(C1, {"bq": a["L1_attn_bq"][:, None], "bk": a["L1_attn_bk"][:, None], "bv": a["L1_attn_bv"][:, None],
                                        "c1": a["L1_attn_c1"].reshape(-1, P).T}), head_mask.astype(np.float32),
                              same_head.astype(np.float32), one_hot.astype(np.float32)], 1),
        "r1": np.concatenate([a["L1_ffn_gate_b"], a["L1_attn_bo"], a["L1_attn_g1"], a["L1_attn_b1"], a["L1_attn_c2"],
                              a["L1_attn_g2"], a["L1_attn_b2"]]),
        "key_mask": key_mask.reshape(P, -1),
    }
    arrays.update(experts1_arrays(a))
    return arrays


SLOTS = NT + EXP1 - 1
HID1 = EDIM1 // P
RING = 3


def places_phase(nc, core, logits, top8):
    with ExitStack() as ctx:
        sb = lambda name, shape, dt=F32: ctx.enter_context(nc.sbuf_tensor("pl_" + name, shape, dt))
        sem = lambda name: ctx.enter_context(nc.semaphore("pl_" + name))
        E = [P, NT, EXP1]
        chosen = sb("chosen", E)
        order = sb("order", E)
        counts = sb("counts", [P, EXP1, NT])
        before = sb("before", [P, EXP1, NT])
        over = sb("over", [P, EXP1, NT])
        tiles_of = sb("tiles_of", [P, EXP1])
        tiles_to = sb("tiles_to", [P, EXP1])
        start = sb("start", [P, EXP1])
        passed = sb("passed", [P, SLOTS, EXP1])
        slot_e = sb("slot_e", [P, SLOTS])
        place = sb("place", [P, NT])
        dve_step, chosen_done, counted = sem("dve_step"), sem("chosen_done"), sem("counted")
        flat = lambda t: t[:, :, :].rearrange("p a b -> p (a b)")
        with nc.Block() as block:
            @block.tensor
            def _(pe):
                pe.wait_ge(core.more_in, 16)
                pe.wait_ge(chosen_done, 1)
                nc.tensor.matmul(core.bank[0][:, 0:NT * EXP1], core.strict, flat(chosen), start=True, stop=True).then_inc(counted, 1)
                nc.tensor.matmul(core.bank[1][:, 0:NT * EXP1], core.ones, flat(chosen), start=True, stop=True).then_inc(counted, 1)

            @block.vector
            def _(dve):
                count = [0]

                def step(ins):
                    count[0] += 1
                    ins.then_inc(dve_step, 1)
                    dve.wait_ge(dve_step, count[0])
                tt = nc.vector.tensor_tensor
                dve.wait_ge(core.more_in, 16)
                scan = lambda out, keep, data: step(nc.vector.tensor_tensor_scan(out, keep, data, 0.0, ALU.mult, ALU.add))
                step(tt(chosen[:, :, :], logits[:, :, :], top8[:, :, 0:1].to_broadcast(E), ALU.is_equal))
                scan(flat(order), core.restart8, flat(chosen))
                nc.vector.scalar_tensor_tensor(flat(chosen), flat(order), 1.0, flat(chosen), ALU.is_le, ALU.mult).then_inc(chosen_done, 1)
                dve.wait_ge(counted, 2)
                step(nc.vector.tensor_copy(counts[:, :, :], core.bank[1][:, 0:NT * EXP1].rearrange("p (t e) -> p e t", e=EXP1)))
                scan(flat(before), core.restart32, flat(counts))
                step(tt(over[:, :, :], before[:, :, NT - 1:NT].to_broadcast([P, EXP1, NT]),
                        core.multiples.unsqueeze(1).to_broadcast([P, EXP1, NT]), ALU.is_gt))
                step(nc.vector.tensor_reduce(tiles_of[:, :], over[:, :, :], AXX, ALU.add))
                step(tt(before[:, :, :], before[:, :, :], counts[:, :, :], ALU.subtract))
                scan(tiles_to[:, :], core.ones[:, 0:EXP1], tiles_of[:, :])
                step(tt(start[:, :], tiles_to[:, :], tiles_of[:, :], ALU.subtract))
                step(nc.vector.tensor_scalar(start[:, :], start[:, :], float(P), None, ALU.mult))
                step(tt(before[:, :, :], before[:, :, :], start[:, :].unsqueeze(2).to_broadcast([P, EXP1, NT]), ALU.add))
                step(tt(order[:, :, :], core.bank[0][:, 0:NT * EXP1].rearrange("p (t e) -> p t e", e=EXP1),
                        before[:, :, :].rearrange("p e t -> p t e"), ALU.add))
                step(tt(order[:, :, :], order[:, :, :], chosen[:, :, :], ALU.mult))
                step(nc.vector.tensor_reduce(place[:, :], order[:, :, :], AXX, ALU.add))
                step(nc.vector.tensor_copy(core.place[:, :], place[:, :]))
                step(tt(passed[:, :, :], core.slot_numbers.unsqueeze(2).to_broadcast([P, SLOTS, EXP1]),
                        tiles_to[:, :].unsqueeze(1).to_broadcast([P, SLOTS, EXP1]), ALU.is_ge))
                step(nc.vector.tensor_reduce(slot_e[:, :], passed[:, :, :], AXX, ALU.add))
                step(nc.vector.tensor_scalar(slot_e[:, :], slot_e[:, :], float(EXP1 - 1), None, ALU.min))
                step(nc.vector.tensor_copy(core.slot_expert[:, :], slot_e[:, :]))


def experts1_phase(nc, core, sorted_x, sorted_y, w_up, w_down, b_up, b_down):
    with ExitStack() as ctx:
        sb = lambda name, shape, dt=F32: ctx.enter_context(nc.sbuf_tensor("e1_" + name, shape, dt))
        sem = lambda name: ctx.enter_context(nc.semaphore("e1_" + name))
        x = sb("x", [P, RING, P])
        xT = sb("xT", [P, RING, P])
        up = sb("up", [P, RING, EDIM1])
        hT = sb("hT", [P, RING, EDIM1])
        y = sb("y", [P, RING, P])
        names = "x_turned xT_done up_mm up_done up_turned hT_done down_mm y_done"
        s = type("Sems", (), {k: sem(k) for k in names.split()})
        x_in = [sem(f"x_in{u}") for u in range(RING)]
        y_out = [sem(f"y_out{u}") for u in range(RING)]
        ps_x, ps_up, ps_h, ps_y = core.bank[0], core.bank[1:4], core.bank[4:7], core.bank[7]
        ROUNDS = SLOTS // RING
        expert_of = lambda eng, slot: eng.value_load(core.slot_expert[0:1, bass.ds(slot, 1)], min_val=0, max_val=EXP1 - 1)

        def going(r, u, lag):
            return not isinstance(r, int) or 0 <= r * RING + u - lag < SLOTS

        def rounds(eng, body):
            body(0)
            body(1)
            with eng.Fori(2, ROUNDS) as r:
                body(r)

        with nc.Block() as block:
            @block.sync
            def _(sp):
                sp.wait_ge(core.scattered, 16 * NT)

                def steps(r):
                    for u in range(RING):
                        if going(r, u, 0):
                            slot = r * RING + u
                            wait(sp, s.x_turned, slot - RING + 1)
                            sp.dma_start(x[:, u, :], sorted_x[bass.ds(slot * P, P), :]).then_inc(x_in[u], 16)
                rounds(sp, steps)

            @block.gpsimd
            def _(pool):
                def steps(r):
                    for u in range(RING):
                        slot = r * RING + u
                        pool.wait_ge(s.y_done, slot + 2)
                        pool.dma_start(sorted_y[bass.ds(slot * P, P), :], y[:, u, :]).then_inc(y_out[u], 16)
                rounds(pool, steps)
                for u in range(RING):
                    pool.wait_ge(y_out[u], 16 * ROUNDS)

            @block.tensor
            def _(pe):
                def turn(r, u):
                    slot = r * RING + u
                    pe.wait_ge(x_in[u], 16 * (r + 1))
                    wait(pe, s.xT_done, slot)
                    nc.tensor.transpose(ps_x[:, 0:P], x[:, u, :], core.ident).then_inc(s.x_turned, 1)

                def widen(r, u):
                    slot = r * RING + u
                    e = expert_of(pe, slot)
                    pe.wait_ge(s.xT_done, slot + 1)
                    wait(pe, s.up_done, slot - RING + 1)
                    nc.tensor.matmul(ps_up[u][:, :], xT[:, u, :], w_up[:, bass.ds(e * EDIM1, EDIM1)], start=True, stop=True).then_inc(s.up_mm, 1)

                def turn_up(r, u):
                    slot = r * RING + u
                    pe.wait_ge(s.up_done, slot + 1)
                    wait(pe, s.hT_done, slot - RING + 1)
                    for k in range(HID1):
                        last = nc.tensor.transpose(ps_h[u][:, k * P:(k + 1) * P], up[:, u, k * P:(k + 1) * P], core.ident)
                    last.then_inc(s.up_turned, 1)

                def narrow(r, u):
                    slot = r * RING + u
                    e = expert_of(pe, slot)
                    pe.wait_ge(s.hT_done, slot + 1)
                    if not isinstance(slot, int) or slot:
                        pe.wait_ge(s.y_done, slot + 1)
                    for k in range(HID1):
                        last = nc.tensor.matmul(ps_y[:, 0:P], hT[:, u, k * P:(k + 1) * P], w_down[:, bass.ds((e * HID1 + k) * P, P)],
                                                start=(k == 0), stop=(k == HID1 - 1))
                    last.then_inc(s.down_mm, 1)

                def steps(r):
                    for u in range(RING):
                        for lag, what in ((0, turn), (1, widen), (2, turn_up), (3, narrow)):
                            if going(r, u, lag):
                                what(r + (u - lag) // RING, (u - lag) % RING)
                pe.wait_ge(core.experts_in, 16 * 4)
                rounds(pe, steps)
                steps(ROUNDS)

            @block.scalar
            def _(act):
                def steps(r):
                    for u in range(RING):
                        if going(r, u, 0):
                            slot = r * RING + u
                            act.wait_ge(s.x_turned, slot + 1)
                            wait(act, s.up_mm, slot - RING + 1)
                            nc.scalar.activation(xT[:, u, :], ps_x[:, 0:P], ACT.Copy).then_inc(s.xT_done, 1)
                        if going(r, u, 2):
                            q, v = r + (u - 2) // RING, (u - 2) % RING
                            slot = q * RING + v
                            act.wait_ge(s.up_turned, slot + 1)
                            wait(act, s.down_mm, slot - RING + 1)
                            nc.scalar.activation(hT[:, v, :], ps_h[v][:, :], ACT.Relu).then_inc(s.hT_done, 1)
                rounds(act, steps)
                steps(ROUNDS)

            @block.vector
            def _(dve):
                dve.sem_inc(s.y_done, 1)
                dve.wait_ge(core.experts_in, 16 * 4)

                def bias_up(r, u):
                    slot = r * RING + u
                    e = expert_of(dve, slot)
                    dve.wait_ge(s.up_mm, slot + 1)
                    wait(dve, s.up_turned, slot - RING + 1)
                    nc.vector.tensor_tensor(up[:, u, :], ps_up[u][:, :], b_up[:, bass.ds(e * EDIM1, EDIM1)], ALU.add).then_inc(s.up_done, 1)

                def bias_down(r, u):
                    slot = r * RING + u
                    e = expert_of(dve, slot)
                    dve.wait_ge(s.down_mm, slot + 1)
                    if not isinstance(r, int) or r:
                        wait(dve, y_out[u], 16 * r)
                    nc.vector.tensor_tensor(y[:, u, :], ps_y[:, 0:P], b_down[:, bass.ds(e * P, P)], ALU.add).then_inc(s.y_done, 1)

                def steps(r):
                    for u in range(RING):
                        if going(r, u, 1):
                            bias_up(r + (u - 1) // RING, (u - 1) % RING)
                        if going(r, u, 3):
                            bias_down(r - 1, u)
                rounds(dve, steps)
                steps(ROUNDS)


def gather_phase(nc, core, out_rows):
    with ExitStack() as ctx:
        gathered = [ctx.enter_context(nc.semaphore(f"gathered{n}")) for n in range(BATCH)]
        added, out_done = ctx.enter_context(nc.semaphore("added")), ctx.enter_context(nc.semaphore("out_done"))
        with nc.Block() as block:
            @block.gpsimd
            def _(pool):
                for t in range(NT):
                    nc.gpsimd.indirect_dma_start(
                        out=core.xn2[:, t * P:(t + 1) * P], out_offset=None, in_=core.sorted_y,
                        in_offset=bass.IndirectOffsetOnAxis(ap=core.place[:, t:t + 1], axis=0)).then_inc(gathered[t // TILES], 16)

            @block.vector
            def _(dve):
                for n in range(BATCH):
                    here = slice(n * SEQ, (n + 1) * SEQ)
                    dve.wait_ge(gathered[n], 16 * TILES)
                    nc.vector.tensor_tensor(core.x[:, here], core.x[:, here], core.xn2[:, here], ALU.add).then_inc(added, 1)

            @block.sync
            def _(sp):
                for n in range(BATCH):
                    sp.wait_ge(added, n + 1)
                    sp.dma_start(out_rows[:, n * TILES:(n + 1) * TILES, :],
                                 core.x[:, n * SEQ:(n + 1) * SEQ].rearrange("p (c d) -> p c d", d=P)).then_inc(out_done, 16)
                sp.wait_ge(out_done, 16 * BATCH)


def routing1(nc, core, ins, layer, logits, top8):
    lsb = lambda name, shape, dt=F32: layer.enter_context(nc.sbuf_tensor(name, shape, dt))
    more = lsb("more_consts", [P, P + 3 * NT * EXP1 + SLOTS])
    zeros = lsb("zeros", [P, P])
    core.place = lsb("place", [P, NT], mybir.dt.uint32)
    core.slot_expert = lsb("slot_expert", [P, SLOTS], mybir.dt.int32)
    core.more_in, zero_set = layer.enter_context(nc.semaphore("more_in")), layer.enter_context(nc.semaphore("zero_set"))
    core.cleared = layer.enter_context(nc.semaphore("cleared"))
    core.scattered = layer.enter_context(nc.semaphore("scattered"))
    core.sorted_x = nc.dram_tensor("sorted_x", (SLOTS * P, P), F32, kind="Internal").ap()
    core.sorted_y = nc.dram_tensor("sorted_y", (SLOTS * P, P), F32, kind="Internal").ap()
    with nc.Block() as block:
        @block.vector
        def _(dve):
            nc.vector.memset(zeros[:, :], 0.0).then_inc(zero_set, 1)

        @block.sync
        def _(sp):
            sp.dma_start(more[:, :], ins["more_consts"]).then_inc(core.more_in, 16)
            sp.wait_ge(zero_set, 1)
            sp.dma_start(core.sorted_x.rearrange("(s p) d -> p s d", p=P),
                         zeros[:, :].unsqueeze(1).to_broadcast([P, SLOTS, P])).then_inc(core.cleared, 16)
    core.strict = more[:, 0:P]
    width = NT * EXP1
    core.restart8 = more[:, P:P + width]
    core.restart32 = more[:, P + width:P + 2 * width]
    core.multiples = more[:, P + 2 * width:P + 2 * width + NT]
    core.slot_numbers = more[:, P + 3 * width:P + 3 * width + SLOTS]


def scatter_tile(nc, core, t):
    nc.gpsimd.indirect_dma_start(
        out=core.sorted_x, out_offset=bass.IndirectOffsetOnAxis(ap=core.place[:, t:t + 1], axis=0),
        in_=core.xn2[:, t * P:(t + 1) * P], in_offset=None).then_inc(core.scattered, 16)


def experts1_load(nc, core, ins, layer):
    lsb = lambda name, shape, dt=F32: layer.enter_context(nc.sbuf_tensor(name, shape, dt))
    widths = {"w_up1": EXP1 * EDIM1, "w_down1": EXP1 * EDIM1, "b_up1": EXP1 * EDIM1, "b_down1": EXP1 * P}
    core.expert_weights = [lsb(name, [P, width]) for name, width in widths.items()]
    core.experts_in = layer.enter_context(nc.semaphore("experts_in"))
    with nc.Block() as block:
        @block.sync
        def _(sp):
            for name, to in zip(widths, core.expert_weights):
                source = ins[name].partition_broadcast(P) if name.startswith("b_") else ins[name]
                sp.dma_start(to[:, :], source).then_inc(core.experts_in, 16)


def experts1_arrays(a):
    row = lambda v, n: np.broadcast_to(np.asarray(v, np.float32), (P, n))
    width = NT * EXP1
    multiples = np.zeros(width)
    multiples[:NT] = np.arange(NT) * P
    return {
        "more_consts": np.concatenate([np.triu(np.ones((P, P)), 1), row(np.arange(width) % EXP1 != 0, width),
                                       row(np.arange(width) % NT != 0, width), row(multiples, width), row(np.arange(SLOTS), SLOTS)],
                                      1).astype(np.float32),
        "w_up1": a["L1_ffn_w1"].transpose(2, 0, 1).reshape(P, -1),
        "w_down1": a["L1_ffn_w2"].transpose(0, 2, 1).reshape(EXP1 * HID1, P, P).transpose(1, 0, 2).reshape(P, -1),
        "b_up1": a["L1_ffn_b1"].reshape(-1),
        "b_down1": a["L1_ffn_b2"].reshape(-1),
    }


LAST_PHASE = 6


def build(nc, ins, out, last_phase=99):
    with ExitStack() as ctx:
        core = Core(nc, ctx)
        sb, sem = core.sb, core.sem
        core.banks = ctx.enter_context(nc.psum_tensor("banks", [P, 8, 512], F32))
        core.bank = [core.banks[:, i, :] for i in range(8)]
        core.x = sb("x", [P, NT * P])
        core.xnT = sb("xnT", [P, NT * P])
        at_w0, n_w0 = columns(W0)
        at_c0, n_c0 = columns(C0)
        at_r0, n_r0 = columns(R0)
        w0 = sb("w0", [P, n_w0])
        c0 = sb("c0", [P, n_c0])
        r0 = sb("r0", [P, n_r0])
        consts = sb("consts", [P, 4 * P])
        core.ident, core.upper, core.ones = consts[:, 0:P], consts[:, P:2 * P], consts[:, 2 * P:3 * P]
        core.minus_half, core.eps = consts[:, 3 * P:3 * P + 64], consts[:, 3 * P + 64:4 * P]
        core.spare = sb("spare", [P, 1])
        core.restart = sb("restart", [P, NT * EXP0])
        x_in = [sem("x_in_first"), sem("x_in_rest")]
        core.params_in, out_done = sem("params_in"), sem("x_out_done")
        core.params_count = 16 * 5
        W = lambda name: w0[:, at_w0[name][0]:at_w0[name][1]]
        C = lambda name: c0[:, at_c0[name][0]:at_c0[name][1]]
        R = lambda name: r0[:, at_r0[name][0]:at_r0[name][1]]
        x_rows = ins["x"].rearrange("b (c p) d -> p (b c) d", p=P)
        out_rows = out.rearrange("b (c p) d -> p (b c) d", p=P)

        def load_x(sp, n):
            sp.dma_start(core.x[:, n * SEQ:(n + 1) * SEQ].rearrange("p (c d) -> p c d", d=P),
                         x_rows[:, n * TILES:(n + 1) * TILES, :]).then_inc(x_in[min(n, 1)], 16)

        with nc.Block() as block:
            @block.sync
            def _(sp):
                load_x(sp, 0)
                sp.dma_start(consts[:, :], ins["consts"]).then_inc(core.params_in, 16)
                sp.dma_start(core.restart[:, :], ins["restart"]).then_inc(core.params_in, 16)
                sp.dma_start(c0[:, :], ins["c0"]).then_inc(core.params_in, 16)
                sp.dma_start(r0[:, :], ins["r0"].partition_broadcast(P)).then_inc(core.params_in, 16)
                sp.dma_start(w0[:, :], ins["w0"]).then_inc(core.params_in, 16)
                for n in range(1, BATCH):
                    load_x(sp, n)

        with ExitStack() as layer:
            lsb = lambda name, shape, dt=F32: layer.enter_context(nc.sbuf_tensor(name, shape, dt))
            core.gates0 = lsb("gates0", [P, NT, EXP0])
            core.dt = lsb("dt", [P, NT, HEADS])
            core.cum = lsb("cum", [P, NT, HEADS])
            core.exp_cum = lsb("exp_cum", [P, NT, HEADS])
            core.exp_total = lsb("exp_total", [P, NT, HEADS])
            core.w_end = lsb("w_end", [P, NT, HEADS])
            with ExitStack() as routing:
                logits = routing.enter_context(nc.sbuf_tensor("logits0", [P, NT, EXP0 + HEADS], F32))
                top8 = routing.enter_context(nc.sbuf_tensor("top0", [P, NT, 8], F32))
                norm_phase(nc, core, "n0_", core.x, x_in, W("w_small0"), EXP0 + HEADS, EXP0, None, logits, top8, None)
                routing0_phase(nc, core, logits, top8, R("dt_bias"), R("a_log"))
            if last_phase >= 1:
                experts0_phase(nc, core, W("w_up0"), W("w_down0"))
            if last_phase >= 2:
                skip_phase(nc, core, W("w_zx"), W("w_out"))
            if last_phase >= 3:
                core.x_tokens = lsb("x_tokens", [P, NT, INNER + NSTATE])
                core.b_rows = lsb("b_rows", [NSTATE, 2, NT * P])
                conv_phase(nc, core, W("w_xbc"), C("conv_w"), C("conv_b"))
                ssm_phase(nc, core, W("w_gate"), W("w_out"), C("gamma"), C("beta"), C("b_gate"), R("d_param"))
        if last_phase >= 4:
            layer1(nc, core, ins, out_rows)
            return

        with nc.Block() as block:
            @block.sync
            def _(sp):
                for n in range(BATCH):
                    sp.dma_start(out_rows[:, n * TILES:(n + 1) * TILES, :],
                                 core.x[:, n * SEQ:(n + 1) * SEQ].rearrange("p (c d) -> p c d", d=P)).then_inc(out_done, 16)
                sp.wait_ge(out_done, 16 * BATCH)


def kernel(**inputs):
    import concourse.bacc as bacc
    from concourse.bass_utils import run_bass_kernel_spmd

    a = {k: np.asarray(v) for k, v in inputs.items()}

    def pack(layout, parts):
        cols, width = columns(layout)
        packed = np.zeros((P, width), np.float32)
        for name, value in parts.items():
            packed[:value.shape[0], cols[name][0]:cols[name][0] + value.shape[1]] = value
        return packed

    def slices(m):
        return m.reshape(-1, P, m.shape[1]).transpose(1, 0, 2).reshape(P, -1)

    w_in = a["L0_attn_W_in"].T
    xbc = w_in[:, 3 * INNER:]
    conv = a["L0_attn_conv_w"][:, 0, :]
    zero = np.zeros((P, 16), np.float32)
    third = lambda m: np.concatenate([m[256:272], zero[:16, :m.shape[1]], m[272:288]])
    arrays = {
        "x": a["L0_attn_u"],
        "w0": pack(W0, {
            "w_small0": np.concatenate([a["L0_ffn_router_w"].T, w_in[:, -HEADS:]], 1),
            "w_up0": np.concatenate([a["L0_ffn_shared_up"].reshape(-1, P), a["L0_ffn_routed_up"].reshape(-1, P)]).T,
            "w_down0": slices(np.concatenate([a["L0_ffn_shared_down"].transpose(0, 2, 1).reshape(-1, P),
                                              a["L0_ffn_routed_down"].transpose(0, 2, 1).reshape(-1, P)])),
            "w_zx": np.concatenate([w_in[:, 0:128], w_in[:, 256:384], w_in[:, 128:256], w_in[:, 384:512]], 1),
            "w_xbc": np.concatenate([xbc[:, 0:272], zero, xbc[:, 272:288]], 1),
            "w_out": slices(a["L0_attn_W_out"].T),
            "w_gate": slices(a["L0_attn_W_gate"].T)}),
        "c0": pack(C0, {
            "conv_w": np.concatenate([conv[0:128], conv[128:256], np.concatenate([third(conv), np.zeros((80, 4), np.float32)])], 1),
            "conv_b": np.stack([a["L0_attn_conv_b"][0:128], a["L0_attn_conv_b"][128:256],
                                np.concatenate([third(a["L0_attn_conv_b"][:, None])[:, 0], np.zeros(80, np.float32)])], 1),
            "gamma": a["L0_attn_ln_gamma"].reshape(2, P).T, "beta": a["L0_attn_ln_beta"].reshape(2, P).T,
            "b_gate": a["L0_attn_b_gate"].reshape(2, P).T}),
        "r0": np.concatenate([a["L0_attn_dt_bias"], a["L0_attn_A_log"], a["L0_attn_D_param"]]),
        "consts": np.concatenate([np.eye(P), np.triu(np.ones((P, P))), np.ones((P, P)), np.full((P, 64), -0.5), np.full((P, 64), EPS)], 1).astype(np.float32),
        "restart": np.broadcast_to((np.arange(NT * EXP0) % EXP0 != 0).astype(np.float32), (P, NT * EXP0)).copy(),
    }
    arrays.update(layer1_arrays(a, pack, slices))
    nc = bacc.Bacc("TRN2", target_bir_lowering=False, num_devices=1)
    arrays = {f"in_{k}": np.ascontiguousarray(v) for k, v in arrays.items()}
    ins = {k[3:]: nc.dram_tensor(k, v.shape, mybir.dt.from_np(v.dtype), kind="ExternalInput").ap() for k, v in arrays.items()}
    out = nc.dram_tensor("out", (BATCH, SEQ, P), F32, kind="ExternalOutput").ap()
    build(nc, ins, out, LAST_PHASE)
    result = run_bass_kernel_spmd(nc, [arrays], core_ids=[0])
    return result.results[0]["out"]
```

```python
from contextlib import ExitStack

import numpy as np

import concourse.bass as bass
from concourse import mybir

F32 = mybir.dt.float32
BF16 = mybir.dt.bfloat16
ALU = mybir.AluOpType
ACT = mybir.ActivationFunctionType
AXX = mybir.AxisListType.X

P = 128
BATCH, SEQ = 8, 512
TILES = SEQ // P
NT = BATCH * TILES
EPS = 1e-5
HEADS, HDIM, NSTATE, INNER, TAPS = 8, 32, 16, 256, 4
EXP0, TOP0, EDIM0 = 16, 4, 64
UPS = (2 + EXP0) * EDIM0 // P
AH, AHD, WIN = 16, 8, 32
BLOCKS = SEQ // WIN
GROUPS = 4
KEYS = 3 * WIN
FFN = 512
EXP1, EDIM1 = 8, 512

W0 = [("w_small0", HEADS + EXP0), ("w_up0", UPS * P), ("w_down0", UPS * P), ("w_zx", 4 * P),
      ("w_xbc", 3 * P), ("w_out", 4 * P), ("w_gate", 4 * P)]
C0 = [("conv_w", 3 * TAPS), ("conv_b", 3), ("gamma", 2), ("beta", 2), ("b_gate", 2)]
R0 = [("dt_bias", HEADS), ("a_log", HEADS), ("d_param", HEADS)]
W1 = [("w_small1", EXP1), ("wq", P), ("wk", P), ("wv", P), ("wo", P), ("w_f1", FFN), ("w_f2", FFN)]
C1 = [("bq", 1), ("bk", 1), ("bv", 1), ("c1", FFN // P)]
R1 = [("gate_b", EXP1), ("bo", P), ("g1", P), ("b1", P), ("c2", P), ("g2", P), ("b2", P)]


def columns(layout):
    at, out = 0, {}
    for name, width in layout:
        out[name] = (at, at + width)
        at += width
    return out, at


def wait(eng, sem, value):
    if isinstance(value, int) and value <= 0:
        return
    eng.wait_ge(sem, value)


def live(n, c, lag):
    return not isinstance(n, int) or 0 <= n * TILES + c - lag < NT


def back(n, c, lag):
    return n + (c - lag) // TILES, (c - lag) % TILES


def over_sequences(eng, body):
    body(0)
    with eng.Fori(1, BATCH) as n:
        body(n)


class Core:

    def __init__(self, nc, ctx):
        self.nc, self.ctx = nc, ctx

    def sb(self, name, shape, dt=F32):
        t = self.ctx.enter_context(self.nc.sbuf_tensor(name, shape, dt))
        return t

    def sem(self, name):
        return self.ctx.enter_context(self.nc.semaphore(name))


def norm_phase(nc, core, tag, x, x_loaded, w_small, n_small, n_exp, bias_row, logits, top8, xn_tokens):
    with ExitStack() as ctx:
        sb = lambda name, shape, dt=F32: ctx.enter_context(nc.sbuf_tensor(tag + name, shape, dt))
        stats = sb("stats", [P, 2, TILES, 6])
        mean_var = sb("mean_var", [P, 2, TILES, 2])
        var_eps = sb("var_eps", [P, 2, TILES])
        rstd = sb("rstd", [P, 2, TILES])
        xn = sb("xn", [P, 2, TILES, P])
        xnT_local = sb("xnT_local", [P, 2, SEQ])
        small = sb("small", [P, 2, TILES, n_small])
        top = sb("top", [P, 2, TILES, 8])
        names = "stats_done mv_done vareps_done rstd_done xn_done turned local_done xnT_done tokens_done small_mm small_done top_done kept"
        sems = {k: nc.alloc_semaphore(name=tag + k) for k in names.split()}
        s = type("Sems", (), sems)
        ps_turn, ps_small = core.bank[0:2], core.bank[2:4]
        params_in, params_count = ((core.params_in, core.params_count) if x_loaded is not None else
                                   (core.params1_in, core.params1_count))
        PRODUCTS = 2

        def steps_of(eng, stages):
            def pair(r):
                for u in range(2):
                    for lag, what in stages:
                        n = 2 * r + u - lag
                        if not isinstance(r, int) or 0 <= n < BATCH:
                            what(n, (u - lag) % 2)
            pair(0)
            with eng.Fori(1, BATCH // 2) as r:
                pair(r)
            pair(BATCH // 2)

        with nc.Block() as block:
            @block.vector
            def _(dve):
                def statistics(n, u):
                    if x_loaded is not None:
                        if isinstance(n, int) and n == 0:
                            dve.wait_ge(x_loaded[0], 16)
                        else:
                            dve.wait_ge(x_loaded[1], 16 * (BATCH - 1))
                    wait(dve, s.xn_done, TILES * (n - 1))
                    for c in range(TILES):
                        nc.vector.bn_stats(stats[:, u, c, :], x[:, bass.ds((n * TILES + c) * P, P)]).then_inc(s.stats_done, 1)
                    dve.wait_ge(s.stats_done, TILES * n + TILES)
                    nc.vector.memset(core.spare[:, 0:1], 0.0)
                    for c in range(TILES):
                        nc.vector.bn_aggr(mean_var[:, u, c, :], stats[:, u, c, :]).then_inc(s.mv_done, 1)

                def normalise(n, u):
                    dve.wait_ge(s.rstd_done, n + 1)
                    wait(dve, s.turned, n - 1)
                    if xn_tokens is not None:
                        wait(dve, s.tokens_done, n - 1)
                    for c in range(TILES):
                        nc.vector.tensor_scalar(xn[:, u, c, :], x[:, bass.ds((n * TILES + c) * P, P)], mean_var[:, u, c, 0:1],
                                                rstd[:, u, c:c + 1], ALU.subtract, ALU.mult).then_inc(s.xn_done, 1)

                def router(n, u):
                    dve.wait_ge(s.small_mm, n + 1)
                    dve.wait_ge(s.kept, 2 * n + 2)
                    products = ps_small[u][:, 0:TILES * n_small].rearrange("p (c e) -> p c e", c=TILES)
                    if bias_row is None:
                        nc.vector.tensor_copy(small[:, u, :, :], products).then_inc(s.small_done, 1)
                    else:
                        nc.vector.tensor_tensor(small[:, u, :, :], products, bias_row.unsqueeze(1).to_broadcast([P, TILES, n_small]),
                                                ALU.add).then_inc(s.small_done, 1)
                    dve.wait_ge(s.small_done, n + 3)
                    nc.vector.memset(core.spare[:, 0:1], 0.0)
                    for c in range(TILES):
                        nc.vector.max(top[:, u, c, :], small[:, u, c, 0:n_exp]).then_inc(s.top_done, 1)
                    nc.vector.tensor_copy(logits[:, bass.ds(n * TILES, TILES), :], small[:, u, :, :]).then_inc(s.kept, 1)
                    dve.wait_ge(s.top_done, TILES * n + TILES)
                    nc.vector.tensor_copy(top8[:, bass.ds(n * TILES, TILES), :], top[:, u, :, :]).then_inc(s.kept, 1)
                dve.wait_ge(params_in, params_count)
                dve.sem_inc(s.kept, 4)
                dve.sem_inc(s.small_done, 2)
                steps_of(dve, [(0, statistics), (PRODUCTS, router), (1, normalise)])

            @block.gpsimd
            def _(pool):
                def root(n, u):
                    pool.wait_ge(s.mv_done, TILES * n + TILES)
                    wait(pool, s.xn_done, TILES * (n - 1))
                    nc.gpsimd.tensor_tensor(var_eps[:, u, :], mean_var[:, u, :, 1], core.eps[:, 0:TILES], ALU.add).then_inc(s.vareps_done, 1)
                    pool.wait_ge(s.vareps_done, n + 1)
                    nc.gpsimd.tensor_tensor(rstd[:, u, :], var_eps[:, u, :], core.minus_half[:, 0:TILES], ALU.pow).then_inc(s.rstd_done, 1)
                pool.wait_ge(params_in, params_count)
                steps_of(pool, [(0, root)])

            @block.tensor
            def _(pe):
                def turn(n, u):
                    wait(pe, s.xnT_done, n - 1)
                    for c in range(TILES):
                        pe.wait_ge(s.xn_done, n * TILES + c + 1)
                        last = nc.tensor.transpose(ps_turn[u][:, c * P:(c + 1) * P], xn[:, u, c, :], core.ident[:, :])
                    last.then_inc(s.turned, 1)

                def small_product(n, u):
                    pe.wait_ge(s.local_done, n + 1)
                    pe.wait_ge(s.small_done, n + 1)
                    for c in range(TILES):
                        last = nc.tensor.matmul(ps_small[u][:, c * n_small:(c + 1) * n_small], xnT_local[:, u, c * P:(c + 1) * P], w_small,
                                                start=True, stop=True)
                    last.then_inc(s.small_mm, 1)
                pe.wait_ge(params_in, params_count)
                steps_of(pe, [(PRODUCTS, small_product), (1, turn)])

            @block.scalar
            def _(act):
                def copy(n, u):
                    act.wait_ge(s.turned, n + 1)
                    wait(act, s.small_mm, n - 1)
                    nc.scalar.activation(xnT_local[:, u, :], ps_turn[u][:, :], ACT.Copy).then_inc(s.local_done, 1)
                    nc.scalar.activation(core.xnT[:, bass.ds(n * SEQ, SEQ)], ps_turn[u][:, :], ACT.Copy).then_inc(s.xnT_done, 1)
                    if xn_tokens is not None:
                        nc.scalar.activation(xn_tokens[:, bass.ds(n * SEQ, SEQ)], xn[:, u, :, :].rearrange("p c d -> p (c d)"),
                                             ACT.Copy).then_inc(s.tokens_done, 1)
                steps_of(act, [(1, copy)])
        nc.clear_and_free_semaphores(list(sems.values()))
        nc.all_engine_barrier()


def routing0_phase(nc, core, logits, top8, dt_bias, a_log):
    with ExitStack() as ctx:
        sb = lambda name, shape, dt=F32: ctx.enter_context(nc.sbuf_tensor("r0_" + name, shape, dt))
        sem = lambda name: ctx.enter_context(nc.semaphore("r0_" + name))
        shifted = sb("shifted", [P, NT, EXP0])
        above = sb("above", [P, NT, EXP0])
        equal = sb("equal", [P, NT, EXP0])
        order = sb("order", [P, NT, EXP0])
        total = sb("total", [P, NT])
        n_above = sb("n_above", [P, NT])
        pre = sb("pre", [P, NT, HEADS])
        small_exp = sb("small_exp", [P, NT, HEADS])
        one_plus = sb("one_plus", [P, NT, HEADS])
        log_1p = sb("log_1p", [P, NT, HEADS])
        ratio = sb("ratio", [P, NT, HEADS])
        decay = sb("decay", [P, NT, HEADS])
        a_exp = sb("a_exp", [P, HEADS])
        dve_step, a_ready, act_ready, decay_ready, sums_ready, sums_copied = (
            sem("dve_step"), sem("a_ready"), sem("act_ready"), sem("decay_ready"), sem("sums_ready"), sem("sums_copied"))
        abs_done = sem("abs_done")
        E = [P, NT, EXP0]
        H = [P, NT, HEADS]
        lg = logits[:, :, 0:EXP0]
        largest = top8[:, :, 0:1].to_broadcast(E)
        fourth = top8[:, :, TOP0 - 1:TOP0].to_broadcast(E)
        flat = lambda t: t[:, :, :].rearrange("p t h -> p (t h)")

        with nc.Block() as block:
            @block.vector
            def _(dve):
                count = [0]

                def step(ins):
                    count[0] += 1
                    ins.then_inc(dve_step, 1)
                    dve.wait_ge(dve_step, count[0])
                step(nc.vector.tensor_tensor(pre[:, :, :], logits[:, :, EXP0:EXP0 + HEADS],
                                             dt_bias.unsqueeze(1).to_broadcast(H), ALU.add))
                step(nc.vector.tensor_tensor(shifted[:, :, :], lg, largest, ALU.subtract))
                step(nc.vector.tensor_tensor(above[:, :, :], lg, fourth, ALU.is_gt))
                step(nc.vector.tensor_tensor(equal[:, :, :], lg, fourth, ALU.is_equal))
                step(nc.vector.tensor_reduce(n_above[:, :], above[:, :, :], AXX, ALU.add))
                step(nc.vector.tensor_tensor_scan(flat(order), core.restart[:, 0:NT * EXP0], flat(equal), 0.0,
                                                  ALU.mult, ALU.add))
                step(nc.vector.tensor_tensor(order[:, :, :], order[:, :, :], n_above[:, :].unsqueeze(2).to_broadcast(E), ALU.add))
                step(nc.vector.scalar_tensor_tensor(flat(equal), flat(order), float(TOP0), flat(equal), ALU.is_le, ALU.mult))
                step(nc.vector.tensor_tensor(above[:, :, :], above[:, :, :], equal[:, :, :], ALU.add))
                dve.wait_ge(act_ready, 2)
                step(nc.vector.tensor_scalar(one_plus[:, :, :], small_exp[:, :, :], 1.0, None, ALU.add))
                dve.wait_ge(act_ready, 3)
                step(nc.vector.tensor_reduce(total[:, :], shifted[:, :, :], AXX, ALU.add))
                step(nc.vector.reciprocal(total[:, :], total[:, :]))
                step(nc.vector.tensor_tensor(shifted[:, :, :], shifted[:, :, :], total[:, :].unsqueeze(2).to_broadcast(E), ALU.mult))
                step(nc.vector.tensor_tensor(core.gates0[:, :, :], shifted[:, :, :], above[:, :, :], ALU.mult))
                step(nc.vector.tensor_scalar(ratio[:, :, :], one_plus[:, :, :], -1.0, None, ALU.add))
                step(nc.vector.scalar_tensor_tensor(flat(decay), flat(ratio), 0.0, flat(small_exp), ALU.is_equal, ALU.mult))
                step(nc.vector.tensor_scalar(ratio[:, :, :], ratio[:, :, :], 1e-30, None, ALU.max))
                step(nc.vector.reciprocal(ratio[:, :, :], ratio[:, :, :]))
                step(nc.vector.tensor_tensor(ratio[:, :, :], ratio[:, :, :], small_exp[:, :, :], ALU.mult))
                dve.wait_ge(act_ready, 4)
                step(nc.vector.tensor_tensor(log_1p[:, :, :], log_1p[:, :, :], ratio[:, :, :], ALU.mult))
                step(nc.vector.tensor_tensor(log_1p[:, :, :], log_1p[:, :, :], decay[:, :, :], ALU.add))
                step(nc.vector.scalar_tensor_tensor(flat(core.dt), flat(pre), 0.0, flat(log_1p), ALU.max, ALU.add))
                step(nc.vector.tensor_scalar(a_exp[:, :], a_exp[:, :], -1.0, None, ALU.mult))
                nc.vector.tensor_tensor(decay[:, :, :], core.dt[:, :, :], a_exp[:, :].unsqueeze(1).to_broadcast(H),
                                        ALU.mult).then_inc(decay_ready, 1)
                dve.wait_ge(sums_ready, 2)
                nc.vector.tensor_copy(flat(core.cum), core.bank[0][:, 0:NT * HEADS]).then_inc(sums_copied, 1)
                dve.wait_ge(sums_copied, 1)
                nc.vector.tensor_tensor(flat(core.w_end), core.bank[1][:, 0:NT * HEADS], flat(core.cum),
                                        ALU.subtract).then_inc(sums_copied, 1)
                dve.wait_ge(act_ready, 7)
                nc.vector.tensor_tensor(core.w_end[:, :, :], core.w_end[:, :, :], core.dt[:, :, :], ALU.mult)

            @block.scalar
            def _(act):
                act.wait_ge(dve_step, 1)
                nc.scalar.activation(one_plus[:, :, :], pre[:, :, :], ACT.Abs).then_inc(abs_done, 1)
                act.wait_ge(abs_done, 1)
                nc.scalar.activation(small_exp[:, :, :], one_plus[:, :, :], ACT.Exp, scale=-1.0).then_inc(act_ready, 1)
                nc.scalar.activation(a_exp[:, :], a_log, ACT.Exp).then_inc(act_ready, 1)
                act.wait_ge(dve_step, 2)
                nc.scalar.activation(shifted[:, :, :], shifted[:, :, :], ACT.Exp).then_inc(act_ready, 1)
                act.wait_ge(dve_step, 10)
                nc.scalar.activation(log_1p[:, :, :], one_plus[:, :, :], ACT.Ln).then_inc(act_ready, 1)
                act.wait_ge(sums_copied, 2)
                nc.scalar.activation(core.exp_cum[:, :, :], core.cum[:, :, :], ACT.Exp).then_inc(act_ready, 1)
                nc.scalar.activation(flat(core.exp_total), core.bank[1][:, 0:NT * HEADS], ACT.Exp).then_inc(act_ready, 1)
                nc.scalar.activation(core.w_end[:, :, :], core.w_end[:, :, :], ACT.Exp).then_inc(act_ready, 1)

            @block.tensor
            def _(pe):
                pe.wait_ge(decay_ready, 1)
                nc.tensor.matmul(core.bank[0][:, 0:NT * HEADS], core.upper[:, :], flat(decay), start=True, stop=True).then_inc(sums_ready, 1)
                nc.tensor.matmul(core.bank[1][:, 0:NT * HEADS], core.ones[:, :], flat(decay), start=True, stop=True).then_inc(sums_ready, 1)


def experts0_phase(nc, core, w_up, w_down):
    with ExitStack() as ctx:
        sb = lambda name, shape, dt=F32: ctx.enter_context(nc.sbuf_tensor("m0_" + name, shape, dt))
        sem = lambda name: ctx.enter_context(nc.semaphore("m0_" + name))
        hidden = sb("hidden", [P, 2, SEQ])
        gated = sb("gated", [P, UPS, SEQ])
        gates = sb("gates", [P, 2, TILES, P])
        up_done, gelu_done, gates_in, spread_done, gated_done, down_done, added = (
            sem("up_done"), sem("gelu_done"), sem("gates_in"), sem("spread_done"), sem("gated_done"),
            sem("down_done"), sem("added"))
        ps_up = core.bank[0:3]
        ps_spread = core.bank[3:5]
        ps_down = core.bank[5]
        ROUTED = UPS - 1

        with nc.Block() as block:
            @block.tensor
            def _(pe):
                def up(n, m):
                    wait(pe, gelu_done, n * UPS + m - 2)
                    nc.tensor.matmul(ps_up[m % 3][:, :], w_up[:, m * P:(m + 1) * P], core.xnT[:, bass.ds(n * SEQ, SEQ)],
                                     start=True, stop=True).then_inc(up_done, 1)

                def spread(n, m):
                    pe.wait_ge(gates_in, n * ROUTED + m)
                    wait(pe, gated_done, n * ROUTED + m - 2)
                    for c in range(TILES):
                        last = nc.tensor.transpose(ps_spread[(m - 1) % 2][:, c * P:(c + 1) * P],
                                                   gates[:, (m - 1) % 2, c, :], core.ident[:, :])
                    last.then_inc(spread_done, 1)

                def down(n, m):
                    if m == 0:
                        pe.wait_ge(gelu_done, n * UPS + 1)
                        wait(pe, added, n)
                    else:
                        pe.wait_ge(gated_done, n * ROUTED + m)
                    for c in range(TILES):
                        last = nc.tensor.matmul(ps_down[:, c * P:(c + 1) * P], gated[:, m, c * P:(c + 1) * P],
                                                w_down[:, m * P:(m + 1) * P], start=(m == 0 and c == 0),
                                                stop=(m == UPS - 1), skip_group_check=True)
                    last.then_inc(down_done, 1)

                def sequence(n):
                    for m in range(UPS):
                        up(n, m)
                        if m:
                            spread(n, m)
                        if m >= 2:
                            down(n, m - 2)
                        elif live(n, 0, 1):
                            down(n - 1, UPS + m - 2)
                over_sequences(pe, sequence)
                down(BATCH - 1, UPS - 2)
                down(BATCH - 1, UPS - 1)

            @block.scalar
            def _(act):
                def sequence(n):
                    for m in range(UPS):
                        act.wait_ge(up_done, n * UPS + m + 1)
                        if m == 0:
                            wait(act, down_done, (n - 1) * UPS + 1)
                            out = gated[:, 0, :]
                        else:
                            wait(act, gated_done, n * ROUTED + m - 2)
                            out = hidden[:, (m - 1) % 2, :]
                        nc.scalar.activation(out, ps_up[m % 3][:, :], ACT.Gelu).then_inc(gelu_done, 1)
                over_sequences(act, sequence)

            @block.gpsimd
            def _(pool):
                def sequence(n):
                    for m in range(1, UPS):
                        wait(pool, spread_done, n * ROUTED + m - 2)
                        nc.gpsimd.tensor_copy(
                            gates[:, (m - 1) % 2, :, :].rearrange("p c (e u) -> p c e u", e=2),
                            core.gates0[:, bass.ds(n * TILES, TILES), 2 * (m - 1):2 * m].unsqueeze(3).to_broadcast(
                                [P, TILES, 2, EDIM0])).then_inc(gates_in, 1)
                over_sequences(pool, sequence)

            @block.vector
            def _(dve):
                def add(n):
                    dve.wait_ge(down_done, (n + 1) * UPS)
                    here = core.x[:, bass.ds(n * SEQ, SEQ)]
                    nc.vector.tensor_tensor(here, ps_down[:, :], here, ALU.add).then_inc(added, 1)

                def sequence(n):
                    for m in range(1, UPS):
                        dve.wait_ge(gelu_done, n * UPS + m + 1)
                        dve.wait_ge(spread_done, n * ROUTED + m)
                        wait(dve, down_done, (n - 1) * UPS + m + 1)
                        nc.vector.tensor_tensor(gated[:, m, :], ps_spread[(m - 1) % 2][:, :], hidden[:, (m - 1) % 2, :],
                                                ALU.mult).then_inc(gated_done, 1)
                        if m == 1 and live(n, 0, 1):
                            add(n - 1)
                over_sequences(dve, sequence)
                add(BATCH - 1)


def skip_conv_phase(nc, core, w_zx, w_out, w_xbc, conv_w, conv_b):
    with ExitStack() as ctx:
        sb = lambda name, shape, dt=F32: ctx.enter_context(nc.sbuf_tensor("sc_" + name, shape, dt))
        sem = lambda name: ctx.enter_context(nc.semaphore("sc_" + name))
        silu_z = sb("silu_z", [P, 2, SEQ])
        skip = sb("skip", [P, 2, SEQ])
        PAD = TAPS - 1
        padded = sb("padded", [P, 2, 3, PAD + SEQ])
        summed = sb("summed", [P, 2, 3, SEQ])
        x_act = sb("x_act", [P, 2, SEQ])
        b_act = sb("b_act", [NSTATE, SEQ])
        ROWS = [P, P, 48]
        TAPPED = [5, 6, 9]
        names = "z_mm x0_mm silu_z_done skip_done out_mm added pads_zero xbc_mm first_tap taps_done silu_done turned kept"
        s = type("Sems", (), {k: sem(k) for k in names.split()})
        ps_z, ps_x0, ps_out = core.bank[0], core.bank[1], core.bank[2]
        ps_xbc, ps_turn = core.bank[3:6], core.bank[6:8]

        def pairs(eng, sequence):
            sequence(0, 0)
            sequence(1, 1)
            with eng.Fori(1, BATCH // 2) as r:
                sequence(2 * r, 0)
                sequence(2 * r + 1, 1)

        with nc.Block() as block:
            @block.tensor
            def _(pe):
                def project_z(n, k):
                    xnT = core.xnT[:, bass.ds(n * SEQ, SEQ)]
                    wait(pe, s.silu_z_done, 2 * n + k)
                    nc.tensor.matmul(ps_z[:, :], w_zx[:, 2 * k * P:(2 * k + 1) * P], xnT, start=True, stop=True).then_inc(s.z_mm, 1)

                def project_x0(n, k):
                    xnT = core.xnT[:, bass.ds(n * SEQ, SEQ)]
                    wait(pe, s.skip_done, 2 * n + k)
                    nc.tensor.matmul(ps_x0[:, :], w_zx[:, (2 * k + 1) * P:(2 * k + 2) * P], xnT, start=True, stop=True).then_inc(s.x0_mm, 1)

                def project_conv(n, m):
                    wait(pe, s.first_tap, 3 * (n - 1) + m + 1)
                    nc.tensor.matmul(ps_xbc[m][:, :], w_xbc[:, m * P:(m + 1) * P],
                                     core.xnT[:, bass.ds(n * SEQ, SEQ)], start=True, stop=True).then_inc(s.xbc_mm, 1)

                def out(n):
                    pe.wait_ge(s.skip_done, 2 * n + 2)
                    wait(pe, s.added, n)
                    for k in range(2):
                        for c in range(TILES):
                            last = nc.tensor.matmul(ps_out[:, c * P:(c + 1) * P], skip[:, k, c * P:(c + 1) * P],
                                                    w_out[:, k * P:(k + 1) * P], start=(k == 0 and c == 0), stop=(k == 1),
                                                    skip_group_check=True)
                    last.then_inc(s.out_mm, 1)

                def turn(n, tiles):
                    pe.wait_ge(s.silu_done, 3 * n + 3)
                    for c in tiles:
                        pe.wait_ge(s.kept, n * TILES + c + 1)
                        for k in range(2):
                            nc.tensor.transpose(ps_turn[c % 2][:, k * P:(k + 1) * P], x_act[:, k, c * P:(c + 1) * P], core.ident[:, :])
                        nc.tensor.transpose(ps_turn[c % 2][:, INNER:INNER + NSTATE], b_act[:, c * P:(c + 1) * P],
                                            core.ident[0:NSTATE, 0:NSTATE]).then_inc(s.turned, 1)

                def sequence(n, u):
                    project_conv(n, 0)
                    project_conv(n, 1)
                    project_z(n, 0)
                    project_x0(n, 0)
                    project_conv(n, 2)
                    project_z(n, 1)
                    if live(n, 0, 1):
                        out(n - 1)
                        turn(n - 1, (0, 1))
                    project_x0(n, 1)
                    if live(n, 0, 1):
                        turn(n - 1, (2, 3))
                pairs(pe, sequence)
                out(BATCH - 1)
                turn(BATCH - 1, range(TILES))

            @block.scalar
            def _(act):
                def silu_of_z(n, k):
                    act.wait_ge(s.z_mm, 2 * n + k + 1)
                    wait(act, s.skip_done, 2 * (n - 1) + k + 1)
                    nc.scalar.activation(silu_z[:, k, :], ps_z[:, :], ACT.Silu).then_inc(s.silu_z_done, 1)

                def taps(n, u, m):
                    r = ROWS[m]
                    act.wait_ge(s.xbc_mm, 3 * n + m + 1)
                    wait(act, s.taps_done, 9 * (n - 2) + TAPPED[m])
                    wait(act, s.silu_done, 3 * (n - 2) + m + 1)
                    nc.scalar.activation(padded[0:r, u, m, PAD:], ps_xbc[m][0:r, :], ACT.Copy)
                    nc.scalar.activation(summed[0:r, u, m, :], ps_xbc[m][0:r, :], ACT.Identity, bias=conv_b[0:r, m:m + 1],
                                         scale=conv_w[0:r, TAPS * m + PAD:TAPS * m + TAPS]).then_inc(s.first_tap, 1)

                def silus(n, u):
                    wait(act, s.turned, TILES * n)
                    for m in range(2):
                        act.wait_ge(s.taps_done, 9 * n + TAPPED[m])
                        nc.scalar.activation(x_act[:, m, :], summed[:, u, m, :], ACT.Silu).then_inc(s.silu_done, 1)
                    act.wait_ge(s.taps_done, 9 * n + 9)
                    nc.scalar.activation(b_act[:, :], summed[0:NSTATE, u, 2, :], ACT.Silu)
                    nc.scalar.activation(core.b_rows[:, 0, bass.ds(n * SEQ, SEQ)], summed[0:NSTATE, u, 2, :], ACT.Silu)
                    nc.scalar.activation(core.b_rows[:, 1, bass.ds(n * SEQ, SEQ)], summed[32:32 + NSTATE, u, 2, :],
                                         ACT.Silu).then_inc(s.silu_done, 1)

                def sequence(n, u):
                    taps(n, u, 0)
                    taps(n, u, 1)
                    silu_of_z(n, 0)
                    taps(n, u, 2)
                    if live(n, 0, 1):
                        silus(n - 1, 1 - u)
                    silu_of_z(n, 1)
                pairs(act, sequence)
                silus(BATCH - 1, 1)

            @block.vector
            def _(dve):
                dve.sem_inc(s.kept, 2)
                nc.vector.memset(padded[:, :, :, 0:PAD], 0.0).then_inc(s.pads_zero, 1)
                dve.wait_ge(s.pads_zero, 1)

                def multiply(n, k):
                    if k == 0:
                        wait(dve, s.out_mm, n)
                    dve.wait_ge(s.silu_z_done, 2 * n + k + 1)
                    dve.wait_ge(s.x0_mm, 2 * n + k + 1)
                    nc.vector.tensor_tensor(skip[:, k, :], ps_x0[:, :], silu_z[:, k, :], ALU.mult).then_inc(s.skip_done, 1)

                def add(n):
                    dve.wait_ge(s.out_mm, n + 1)
                    here = core.x[:, bass.ds(n * SEQ, SEQ)]
                    nc.vector.tensor_tensor(here, ps_out[:, :], here, ALU.add).then_inc(s.added, 1)

                def taps(n, u):
                    for k in range(PAD):
                        for m in (0, 1):
                            if k == 0:
                                dve.wait_ge(s.first_tap, 3 * n + m + 1)
                            tap(n, u, m, k)
                    dve.wait_ge(s.first_tap, 3 * n + 3)
                    for k in range(PAD):
                        tap(n, u, 2, k)

                def tap(n, u, m, k):
                    r = ROWS[m]
                    if k:
                        dve.wait_ge(s.taps_done, 9 * n + (2 * (k - 1) + m + 1 if m < 2 else 6 + k))
                    nc.vector.scalar_tensor_tensor(summed[0:r, u, m, :], padded[0:r, u, m, k:k + SEQ],
                                                   conv_w[0:r, TAPS * m + k:TAPS * m + k + 1], summed[0:r, u, m, :],
                                                   ALU.mult, ALU.add).then_inc(s.taps_done, 1)

                def keep(n):
                    for c in range(TILES):
                        t = n * TILES + c
                        dve.wait_ge(s.turned, t + 1)
                        nc.vector.tensor_copy(core.x_tokens[:, bass.ds(t, 1), :].rearrange("p o c -> p (o c)"),
                                              ps_turn[c % 2][:, 0:INNER + NSTATE]).then_inc(s.kept, 1)

                def sequence(n, u):
                    taps(n, u)
                    multiply(n, 0)
                    if live(n, 0, 1):
                        keep(n - 1)
                    multiply(n, 1)
                    if live(n, 0, 1):
                        add(n - 1)
                pairs(dve, sequence)
                add(BATCH - 1)
                keep(BATCH - 1)


def ssm_phase(nc, core, w_gate, w_out, gamma, beta, b_gate, d_param):
    with ExitStack() as ctx:
        sb = lambda name, shape, dt=F32: ctx.enter_context(nc.sbuf_tensor("ss_" + name, shape, dt))
        sem = lambda name: ctx.enter_context(nc.semaphore("ss_" + name))
        cum_local = sb("cum_local", [P, TILES, HEADS])
        b_local = sb("b_local", [NSTATE, TILES, P])
        c_local = sb("c_local", [NSTATE, TILES, P])
        b_tokens = sb("b_tokens", [P, TILES, NSTATE])
        x_dt = sb("x_dt", [P, TILES, INNER])
        x_end = sb("x_end", [P, TILES, INNER])
        x_d = sb("x_d", [P, TILES, INNER])
        mix = sb("mix", [P, 2, HEADS, P])
        bc = sb("bc", [P, 2, P])
        weights = sb("weights", [P, 2, HEADS, P])
        state = sb("state", [NSTATE, TILES, INNER])
        y = sb("y", [P, 2, INNER])
        stats = sb("stats", [P, 2, 6])
        mean_var = sb("mean_var", [P, 2, 2])
        var_eps = sb("var_eps", [P, 2])
        rstd = sb("rstd", [P, 2])
        y_norm = sb("y_norm", [P, 2, INNER])
        yT = sb("yT", [P, 2, SEQ])
        tanh = sb("tanh", [P, 2, SEQ])
        half_bias = sb("half_bias", [P, 2])
        half_out = sb("half_out", [P, 2 * P])
        names = ("halves_ready local_ready spread_done diff_done exp_done weights_done bc_mm bc_done state_mm state_done "
                 "y_mm y_free y_done stats_done mv_done vareps_done rstd_done norm_done turned yT_done gate_mm tanh_done "
                 "gated_done out_done added inter_done scaled_done")
        s = type("Sems", (), {k: sem(k) for k in names.split()})
        ps_spread = core.bank[0:2]
        ps_bc, ps_state, ps_y, ps_turn = core.bank[2], core.bank[3], core.bank[4], core.bank[5]
        ps_gate = core.bank[6:8]
        ps_out = core.bank[6]
        HALF = HEADS // 2
        WEIGH, OUTPUTS, FINISH, ROOT, NORMALISE, TURN = 1, 2, 2, 3, 3, 4
        GATE, APPLY, OUT, ADD = 4, 5, 6, 7
        COPIES = 7
        tile = lambda n, c: n * TILES + c

        def sequence_due(n, c, lag):
            return back(n, c, lag)[0] if (c - lag) % TILES == TILES - 1 and live(n, c, lag) else None

        def sequences(eng, steps):
            steps(0)
            steps(1)
            with eng.Fori(2, BATCH) as n:
                steps(n)
            steps(BATCH)
            steps(BATCH + 1)

        with nc.Block() as block:
            @block.gpsimd
            def _(pool):
                def prepare(n, c):
                    t = tile(n, c)
                    b = c
                    columns_ = bass.ds(t * P, P)
                    of_tile = lambda a: a[:, bass.ds(t, 1), :].rearrange("p o h -> p (o h)")
                    heads = lambda a: a.unsqueeze(2).to_broadcast([P, HEADS, HDIM])
                    x_t = core.x_tokens[:, bass.ds(t, 1), 0:INNER].rearrange("p o (h d) -> p (o h) d", h=HEADS)
                    wait(pool, s.spread_done, 2 * (t - 3))
                    nc.gpsimd.tensor_copy(cum_local[:, b, :], of_tile(core.cum)).then_inc(s.local_ready, 1)
                    wait(pool, s.y_mm, t - 3)
                    wait(pool, s.y_done, t - 3)
                    nc.gpsimd.tensor_copy(b_local[:, b, :], core.b_rows[:, 0, columns_]).then_inc(s.local_ready, 1)
                    nc.gpsimd.tensor_copy(c_local[:, b, :], core.b_rows[:, 1, columns_]).then_inc(s.local_ready, 1)
                    nc.gpsimd.tensor_copy(b_tokens[:, b, :], core.x_tokens[:, bass.ds(t, 1), INNER:INNER + NSTATE].rearrange(
                        "p o c -> p (o c)")).then_inc(s.local_ready, 1)
                    nc.gpsimd.tensor_tensor(x_dt[:, b, :].rearrange("p (h d) -> p h d", h=HEADS), x_t,
                                            heads(of_tile(core.dt)), ALU.mult).then_inc(s.local_ready, 1)
                    nc.gpsimd.tensor_tensor(x_end[:, b, :].rearrange("p (h d) -> p h d", h=HEADS), x_t,
                                            heads(of_tile(core.w_end)), ALU.mult).then_inc(s.local_ready, 1)
                    nc.gpsimd.tensor_tensor(x_d[:, b, :].rearrange("p (h d) -> p h d", h=HEADS), x_t,
                                            heads(d_param), ALU.mult).then_inc(s.local_ready, 1)

                def root(n, c):
                    t = tile(n, c)
                    b = c % 2
                    pool.wait_ge(s.mv_done, t + 1)
                    nc.gpsimd.tensor_tensor(var_eps[:, b:b + 1], mean_var[:, b, 1:2], core.eps[:, 0:1], ALU.add).then_inc(s.vareps_done, 1)
                    wait(pool, s.norm_done, t - 1)
                    pool.wait_ge(s.vareps_done, t + 1)
                    nc.gpsimd.tensor_tensor(rstd[:, b:b + 1], var_eps[:, b:b + 1], core.minus_half[:, 0:1], ALU.pow).then_inc(s.rstd_done, 1)

                def steps(n):
                    for c in range(TILES):
                        if live(n, c, 0):
                            prepare(n, c)
                        if live(n, c, ROOT):
                            root(*back(n, c, ROOT))
                sequences(pool, steps)

            @block.tensor
            def _(pe):
                def chunk(n, c):
                    t = tile(n, c)
                    b = c
                    pe.wait_ge(s.local_ready, COPIES * (t + 1))
                    for half in range(2):
                        wait(pe, s.diff_done, 2 * (t - 1) + half + 1)
                        for h in range(HALF):
                            last = nc.tensor.transpose(ps_spread[half][:, h * P:(h + 1) * P],
                                                       cum_local[:, b, half * HALF + h:half * HALF + h + 1].to_broadcast([P, P]),
                                                       core.ident[:, :])
                        last.then_inc(s.spread_done, 1)
                    wait(pe, s.bc_done, t)
                    nc.tensor.matmul(ps_bc[:, 0:P], b_local[:, b, :], c_local[:, b, :], start=True, stop=True).then_inc(s.bc_mm, 1)
                    if c < TILES - 1:
                        wait(pe, s.state_done, 3 * n + c)
                        nc.tensor.matmul(ps_state[0:NSTATE, 0:INNER], b_tokens[:, b, :], x_end[:, b, :],
                                         start=True, stop=True).then_inc(s.state_mm, 1)

                def outputs(n, c):
                    t = tile(n, c)
                    b = c
                    pe.wait_ge(s.weights_done, 2 * t + 2)
                    wait(pe, s.y_free, t)
                    if c:
                        pe.wait_ge(s.state_done, 3 * n + c)
                        nc.tensor.matmul(ps_y[:, INNER:2 * INNER], c_local[:, b, :], state[:, c, :], start=True, stop=True)
                    for h in range(HEADS):
                        last = nc.tensor.matmul(ps_y[:, h * HDIM:(h + 1) * HDIM], weights[:, c % 2, h, :],
                                                x_dt[:, b, h * HDIM:(h + 1) * HDIM], start=True, stop=True)
                    last.then_inc(s.y_mm, 1)

                def turn(n, c):
                    t = tile(n, c)
                    pe.wait_ge(s.norm_done, t + 1)
                    wait(pe, s.yT_done, 2 * t)
                    for k in range(2):
                        last = nc.tensor.transpose(ps_turn[:, k * P:(k + 1) * P], y_norm[:, c % 2, k * P:(k + 1) * P], core.ident[:, :])
                    last.then_inc(s.turned, 1)

                def gate(n):
                    pe.wait_ge(s.yT_done, 2 * TILES * (n + 1))
                    pe.wait_ge(s.added, n + 1)
                    for m in range(2):
                        for k in range(2):
                            last = nc.tensor.matmul(ps_gate[m][:, :], w_gate[:, (2 * k + m) * P:(2 * k + m + 1) * P], yT[:, k, :],
                                                    start=(k == 0), stop=(k == 1))
                        last.then_inc(s.gate_mm, 1)

                def out(n):
                    pe.wait_ge(s.gated_done, 2 * n + 2)
                    for k in range(2):
                        for c in range(TILES):
                            last = nc.tensor.matmul(ps_out[:, c * P:(c + 1) * P], tanh[:, k, c * P:(c + 1) * P],
                                                    half_out[:, k * P:(k + 1) * P], start=(k == 0 and c == 0), stop=(k == 1),
                                                    skip_group_check=True)
                    last.then_inc(s.out_done, 1)

                def steps(n):
                    for c in range(TILES):
                        if live(n, c, 0):
                            chunk(n, c)
                        if live(n, c, TURN):
                            turn(*back(n, c, TURN))
                        if live(n, c, OUTPUTS):
                            outputs(*back(n, c, OUTPUTS))
                        if (m := sequence_due(n, c, GATE)) is not None:
                            gate(m)
                        if (m := sequence_due(n, c, OUT)) is not None:
                            out(m)
                pe.sem_inc(s.out_done, 1)
                pe.wait_ge(s.halves_ready, 2)
                sequences(pe, steps)

            @block.scalar
            def _(act):
                def exponentials(n, c):
                    t = tile(n, c)
                    for half in range(2):
                        act.wait_ge(s.diff_done, 2 * t + half + 1)
                        here = mix[:, c % 2, half * HALF:(half + 1) * HALF, :]
                        nc.scalar.activation(here, here, ACT.Exp).then_inc(s.exp_done, 1)

                def keep(n, c):
                    t = tile(n, c)
                    act.wait_ge(s.turned, t + 1)
                    if c == 0:
                        wait(act, s.gated_done, 2 * n)
                    for k in range(2):
                        nc.scalar.activation(yT[:, k, c * P:(c + 1) * P], ps_turn[:, k * P:(k + 1) * P], ACT.Identity,
                                             bias=beta[:, k:k + 1], scale=gamma[:, k:k + 1]).then_inc(s.yT_done, 1)

                def squash(n):
                    act.wait_ge(s.out_done, n + 1)
                    for m in range(2):
                        act.wait_ge(s.gate_mm, 2 * n + m + 1)
                        nc.scalar.activation(tanh[:, m, :], ps_gate[m][:, :], ACT.Tanh, bias=half_bias[:, m:m + 1],
                                             scale=0.5).then_inc(s.tanh_done, 1)

                def steps(n):
                    for c in range(TILES):
                        if live(n, c, 0):
                            exponentials(n, c)
                        if live(n, c, TURN):
                            keep(*back(n, c, TURN))
                        if (m := sequence_due(n, c, GATE)) is not None:
                            squash(m)
                act.wait_ge(s.halves_ready, 2)
                sequences(act, steps)

            @block.vector
            def _(dve):
                dve.sem_inc(s.added, 1)
                nc.vector.tensor_scalar(half_bias[:, :], b_gate, 0.5, None, ALU.mult).then_inc(s.halves_ready, 1)
                nc.vector.tensor_scalar(half_out[:, :], w_out[:, 2 * P:4 * P], 0.5, None, ALU.mult).then_inc(s.halves_ready, 1)

                def differences(n, c):
                    t = tile(n, c)
                    for half in range(2):
                        wait(dve, s.weights_done, 2 * (t - 2) + half + 1)
                        dve.wait_ge(s.spread_done, 2 * t + half + 1)
                        here = core.cum[:, bass.ds(t, 1), half * HALF:(half + 1) * HALF].rearrange("p o h -> p (o h)")
                        nc.vector.tensor_tensor(mix[:, c % 2, half * HALF:(half + 1) * HALF, :],
                                                ps_spread[half][:, :].rearrange("p (h t) -> p h t", h=HALF),
                                                here.unsqueeze(2).to_broadcast([P, HALF, P]), ALU.subtract).then_inc(s.diff_done, 1)
                    wait(dve, s.weights_done, 2 * (t - 1))
                    dve.wait_ge(s.bc_mm, t + 1)
                    nc.vector.tensor_tensor(bc[:, c % 2, :], ps_bc[:, 0:P], core.upper[:, :], ALU.mult).then_inc(s.bc_done, 1)

                def update_state(n, c):
                    old, new = state[:, c, :], state[:, c + 1, :]
                    dve.wait_ge(s.state_mm, 3 * n + c + 1)
                    wait(dve, s.y_mm, tile(n, c) - 2)
                    if c == 0:
                        nc.vector.tensor_copy(new, ps_state[0:NSTATE, 0:INNER]).then_inc(s.state_done, 1)
                        return
                    fade = core.exp_total[0:NSTATE, bass.ds(tile(n, c), 1), :].rearrange("p o h -> p (o h)")
                    nc.vector.tensor_tensor(new.rearrange("p (h d) -> p h d", h=HEADS), old.rearrange("p (h d) -> p h d", h=HEADS),
                                            fade.unsqueeze(2).to_broadcast([NSTATE, HEADS, HDIM]), ALU.mult).then_inc(s.scaled_done, 1)
                    dve.wait_ge(s.scaled_done, 2 * n + c)
                    nc.vector.tensor_tensor(new, ps_state[0:NSTATE, 0:INNER], new, ALU.add).then_inc(s.state_done, 1)

                def finish(n, c):
                    t = tile(n, c)
                    b = c % 2
                    here = y[:, b, :]
                    wait(dve, s.norm_done, t - 1)
                    dve.wait_ge(s.y_mm, t + 1)
                    dve.wait_ge(s.local_ready, COPIES * (t + 1))
                    if c:
                        fade = core.exp_cum[:, bass.ds(t, 1), :].rearrange("p o h -> p (o h)")
                        nc.vector.tensor_tensor(here.rearrange("p (h d) -> p h d", h=HEADS),
                                                ps_y[:, INNER:2 * INNER].rearrange("p (h d) -> p h d", h=HEADS),
                                                fade.unsqueeze(2).to_broadcast([P, HEADS, HDIM]), ALU.mult).then_inc(s.inter_done, 1)
                        dve.wait_ge(s.inter_done, 6 * n + 2 * c - 1)
                        nc.vector.tensor_tensor(here, here, x_d[:, c, :], ALU.add).then_inc(s.inter_done, 1)
                        dve.wait_ge(s.inter_done, 6 * n + 2 * c)
                        nc.vector.tensor_tensor(here, ps_y[:, 0:INNER], here, ALU.add).then_inc(s.y_free, 1)
                    else:
                        nc.vector.tensor_tensor(here, ps_y[:, 0:INNER], x_d[:, c, :], ALU.add).then_inc(s.y_free, 1)
                    dve.wait_ge(s.y_free, t + 1)
                    nc.vector.bn_stats(stats[:, b, :], here).then_inc(s.y_done, 1)
                    dve.wait_ge(s.y_done, t + 1)
                    nc.vector.memset(core.spare[:, 0:1], 0.0)
                    nc.vector.bn_aggr(mean_var[:, b, :], stats[:, b, :]).then_inc(s.mv_done, 1)

                def weigh(n, c):
                    t = tile(n, c)
                    dve.wait_ge(s.bc_done, t + 1)
                    wait(dve, s.y_mm, t - 1)
                    for half in range(2):
                        dve.wait_ge(s.exp_done, 2 * t + half + 1)
                        nc.vector.scalar_tensor_tensor(weights[:, c % 2, half * HALF:(half + 1) * HALF, :],
                                                       mix[:, c % 2, half * HALF:(half + 1) * HALF, :], 1.0,
                                                       bc[:, c % 2, :].unsqueeze(1).to_broadcast([P, HALF, P]),
                                                       ALU.min, ALU.mult).then_inc(s.weights_done, 1)

                def normalise(n, c):
                    t = tile(n, c)
                    b = c % 2
                    dve.wait_ge(s.rstd_done, t + 1)
                    wait(dve, s.turned, t - 1)
                    nc.vector.tensor_scalar(y_norm[:, b, :], y[:, b, :], mean_var[:, b, 0:1], rstd[:, b:b + 1],
                                            ALU.subtract, ALU.mult).then_inc(s.norm_done, 1)

                def apply_gate(n):
                    for m in range(2):
                        dve.wait_ge(s.tanh_done, 2 * n + m + 1)
                        nc.vector.scalar_tensor_tensor(tanh[:, m, :], tanh[:, m, :], 1.0, yT[:, m, :],
                                                       ALU.add, ALU.mult).then_inc(s.gated_done, 1)

                def add(n):
                    dve.wait_ge(s.out_done, n + 2)
                    here = core.x[:, bass.ds(n * SEQ, SEQ)]
                    nc.vector.tensor_tensor(here, ps_out[:, :], here, ALU.add).then_inc(s.added, 1)

                def steps(n):
                    for c in range(TILES):
                        if (m := sequence_due(n, c, APPLY)) is not None:
                            apply_gate(m)
                        if live(n, c, 0):
                            differences(n, c)
                            if c < TILES - 1:
                                update_state(n, c)
                        if live(n, c, NORMALISE):
                            normalise(*back(n, c, NORMALISE))
                        if live(n, c, WEIGH):
                            weigh(*back(n, c, WEIGH))
                        if live(n, c, FINISH):
                            finish(*back(n, c, FINISH))
                        if (m := sequence_due(n, c, ADD)) is not None:
                            add(m)
                dve.wait_ge(s.halves_ready, 2)
                sequences(dve, steps)


def attention_phase(nc, core, wq, wk, wv, bq, bk, bv, head_mask, same_head, one_hot, key_mask):
    with ExitStack() as ctx:
        sb = lambda name, shape, dt=F32: ctx.enter_context(nc.sbuf_tensor("at_" + name, shape, dt))
        sem = lambda name: ctx.enter_context(nc.semaphore("at_" + name))
        STEPS = TILES * GROUPS
        BT = P // WIN
        RING = 4
        VALUES, VALUES_OUT, SCORES, TURN, WEIGH, PACK, DIVIDE, FINAL = 5, 6, 8, 10, 12, 16, 18, 19
        x_rep = sb("x_rep", [P, BLOCKS, GROUPS, WIN])
        kT = sb("kT", [P, GROUPS, WIN + SEQ + WIN])
        q_rows = sb("q_rows", [P, 2, P])
        q_spread = sb("q_spread", [P, GROUPS, BLOCKS, GROUPS, WIN])
        v_ones = sb("v_ones", [P, BLOCKS * GROUPS, 2 * WIN])
        probs = sb("probs", [P, RING, BT * KEYS])
        probsT = sb("probsT", [P, RING, 3 * BT, WIN])
        largest = sb("largest", [P, RING, BT])
        packed = sb("packed", [P, 2, 2, P])
        inverse = sb("inverse", [P, P])
        attended = sb("attended", [P, 2, P])
        names = ("keys_in cleared set_up x_ready kq_mm k_done q_rows_done q_done v_mm v_done score_mm max_done diff_done exp_done turned "
                 "pv_mm packed_done inverse_done attended_done final_done")
        s = type("Sems", (), {k: sem(k) for k in names.split()})
        ps_score = core.bank[0:RING]
        ps_out = core.bank[4:6]
        ps_kq, ps_v = core.bank[6], core.bank[7]

        def step_back(n, u, lag):
            return n + (u - lag) // STEPS, (u - lag) % STEPS

        def alive(n, u, lag):
            return not isinstance(n, int) or 0 <= n * STEPS + u - lag < BATCH * STEPS

        def one_hot_rows(copy, g):
            others = [r for r in range(GROUPS) if r != g]
            for which, r in enumerate(others):
                rows, blocks = slice(WIN * r, WIN * r + WIN), len(range(which, BLOCKS, 3))
                for h in range(GROUPS):
                    last = copy(q_spread[rows, g, which:BLOCKS:3, h, :], one_hot[rows, :].unsqueeze(1).to_broadcast([WIN, blocks, WIN]))
            last.then_inc(s.set_up, 1)

        def tile_due(n, u, lag):
            if (u - lag) % GROUPS or not alive(n, u, lag):
                return None
            m, v = step_back(n, u, lag)
            return m, v // GROUPS

        def step_due(n, u, lag):
            return step_back(n, u, lag) if alive(n, u, lag) else None

        with nc.Block() as block:
            @block.gpsimd
            def _(pool):
                half = q_spread[:, 2:4, :, :, :]
                nc.gpsimd.memset(half.rearrange("p g b h q -> p (g b h q)"), 0.0).then_inc(s.cleared, 1)

                def repeat_tokens(n, j):
                    t = TILES * n + j
                    wait(pool, s.v_mm, t - TILES + 1 if isinstance(n, int) else TILES * (n - 1) + j + 1)
                    wait(pool, s.q_done, GROUPS * (t - 2))
                    nc.gpsimd.tensor_copy(x_rep[:, j * BT:(j + 1) * BT, :, :],
                                          core.xnT[:, bass.ds(t * P, P)].rearrange("p (b q) -> p b q", q=WIN)
                                          .unsqueeze(2).to_broadcast([P, BT, GROUPS, WIN])).then_inc(s.x_ready, 1)

                def spread_queries(n, j):
                    pool.wait_ge(s.q_rows_done, TILES * n + j + 1)
                    wait(pool, s.score_mm, STEPS * n + GROUPS * (j - 3))
                    pool.wait_ge(s.x_ready, min(TILES * n + j + 3, NT) if isinstance(n, int) else TILES * n + j + 3)
                    for g in range(GROUPS):
                        rows = slice(WIN * g, WIN * g + WIN)
                        all_heads = [WIN, BT, GROUPS, WIN]
                        wait(pool, s.q_done, GROUPS * (TILES * n + j) + g)
                        nc.gpsimd.tensor_tensor(
                            q_spread[rows, g, j * BT:(j + 1) * BT, :, :],
                            q_rows[rows, j % 2, :].rearrange("p (b q) -> p b q", q=WIN).unsqueeze(2).to_broadcast(all_heads),
                            head_mask[rows, :].unsqueeze(1).unsqueeze(3).to_broadcast(all_heads), ALU.mult).then_inc(s.q_done, 1)

                SENDING = 4
                A_TILE = NT // (SENDING * TILES)

                def steps(n):
                    for j in range(TILES):
                        if live(n, j, 0):
                            repeat_tokens(n, j)
                        if live(n, j, 2):
                            if isinstance(n, int) and n == 0 and j == 2:
                                pool.wait_ge(s.set_up, 5)
                            if isinstance(n, int):
                                pool.wait_ge(core.scattered, 16 * A_TILE * (n * TILES + j))
                            spread_queries(*back(n, j, 2))
                        if isinstance(n, int) and n < SENDING:
                            if n == 0 and j == 0:
                                pool.wait_ge(core.cleared, 16)
                            wait(pool, s.q_done, GROUPS * (n * TILES + j - 1))
                            for i in range(A_TILE):
                                scatter_tile(nc, core, (n * TILES + j) * A_TILE + i)
                for n in range(SENDING):
                    steps(n)
                pool.wait_ge(core.scattered, 16 * NT)
                with pool.Fori(SENDING, BATCH) as n:
                    steps(n)
                spread_queries(BATCH - 1, TILES - 2)
                spread_queries(BATCH - 1, TILES - 1)

            @block.sync
            def _(sp):
                sp.dma_start(kT[:, :, :].rearrange("p g k -> p (g k)"), key_mask).then_inc(s.keys_in, 16)

            @block.tensor
            def _(pe):
                def keys_queries(n, j):
                    t = TILES * n + j
                    pe.wait_ge(s.x_ready, t + 1)
                    wait(pe, s.q_rows_done, t)
                    tokens = x_rep[:, j * BT:(j + 1) * BT, 0, :]
                    nc.tensor.matmul(ps_kq[:, 0:P], wk, tokens, start=True, stop=True)
                    nc.tensor.matmul(ps_kq[:, P:2 * P], wq, tokens, start=True, stop=True).then_inc(s.kq_mm, 1)

                def values(n, j):
                    wait(pe, s.v_done, TILES * n + j)
                    for b in range(BT):
                        last = nc.tensor.matmul(ps_v[:, b * P:(b + 1) * P], x_rep[:, j * BT + b, :, :].rearrange("p r k -> p (r k)"),
                                                wv, start=True, stop=True)
                    last.then_inc(s.v_mm, 1)

                def scores(n, u):
                    j, g = u // GROUPS, u % GROUPS
                    t = n * STEPS + u
                    bank = ps_score[u % RING]
                    if g == 0:
                        pe.wait_ge(s.q_done, GROUPS * (TILES * n + j + 1))
                        pe.wait_ge(s.k_done, TILES * n + j + (1 if j == TILES - 1 else 2))
                    wait(pe, s.diff_done, t - RING + 1)
                    for b in range(BT):
                        blk = j * BT + b
                        last = nc.tensor.matmul(bank[:, b * KEYS:(b + 1) * KEYS],
                                                q_spread[:, g, blk, :, :].rearrange("p h q -> p (h q)"),
                                                kT[:, g, blk * WIN:blk * WIN + KEYS], start=True, stop=True)
                    last.then_inc(s.score_mm, 1)

                def weigh_values(n, u):
                    t = n * STEPS + u
                    j, g = u // GROUPS, u % GROUPS
                    if g == 0:
                        pe.wait_ge(s.v_done, TILES * n + j + (1 if j == TILES - 1 else 2))
                        wait(pe, s.packed_done, TILES * n + j - 1)
                    pe.wait_ge(s.turned, t + 1)
                    half = slice(64 * (g % 2), 64 * (g % 2) + 64)
                    first = g < 2
                    for d in range(-1, BT + 1):
                        c = j * BT + d
                        if not 0 <= c < BLOCKS:
                            continue
                        b0, b1 = max(0, d - 1), min(BT - 1, d + 1)
                        nb, at = b1 - b0 + 1, b0 * 3 + d + 1 - b0
                        last = nc.tensor.matmul(ps_out[j % 2][half, (g // 2) * P + b0 * WIN:(g // 2) * P + (b1 + 1) * WIN],
                                                v_ones[:, c * GROUPS + g, :], probsT[:, u % RING, at:at + 2 * nb - 1:2, :],
                                                start=first, stop=True, skip_group_check=True)
                        first = False
                    last.then_inc(s.pv_mm, 1)

                def steps(n):
                    for u in range(STEPS):
                        if tile := tile_due(n, u, 0):
                            keys_queries(*tile)
                        if tile := tile_due(n, u, VALUES):
                            values(*tile)
                        if step := step_due(n, u, SCORES):
                            scores(*step)
                        if step := step_due(n, u, WEIGH):
                            weigh_values(*step)
                pe.wait_ge(s.set_up, 5)
                over_sequences(pe, steps)
                steps(BATCH)

            @block.scalar
            def _(act):
                def keys_queries(n, j):
                    t = TILES * n + j
                    act.wait_ge(s.kq_mm, t + 1)
                    wait(act, s.score_mm, STEPS * n + GROUPS * (j - 2))
                    for g in range(GROUPS):
                        rows = slice(WIN * g, WIN * g + WIN)
                        last = nc.scalar.activation(kT[rows, g, WIN + j * P:WIN + (j + 1) * P], ps_kq[rows, 0:P], ACT.Identity, bias=bk[rows, :])
                    last.then_inc(s.k_done, 1)
                    wait(act, s.q_done, GROUPS * (t - 1))
                    nc.scalar.activation(q_rows[:, j % 2, :], ps_kq[:, P:2 * P], ACT.Identity, bias=bq).then_inc(s.q_rows_done, 1)

                def exponential(n, u):
                    act.wait_ge(s.diff_done, n * STEPS + u + 1)
                    here = probs[:, u % RING, :]
                    nc.scalar.activation(here, here, ACT.Exp).then_inc(s.exp_done, 1)

                def pack(n, j):
                    t = TILES * n + j
                    act.wait_ge(s.pv_mm, GROUPS * (t + 1))
                    if live(n, j, 1):
                        act.wait_ge(s.attended_done, t)
                    for g in range(GROUPS):
                        for what in range(2):
                            at = 64 * (g % 2) + WIN * what
                            last = nc.scalar.activation(packed[WIN * g:WIN * (g + 1), j % 2, what, :],
                                                        ps_out[j % 2][at:at + WIN, (g // 2) * P:(g // 2 + 1) * P], ACT.Copy)
                    last.then_inc(s.packed_done, 1)

                def final(n, j):
                    t = TILES * n + j
                    act.wait_ge(s.attended_done, t + 2)
                    nc.scalar.activation(core.xnT[:, bass.ds(t * P, P)], attended[:, j % 2, :], ACT.Identity, bias=bv).then_inc(s.final_done, 1)

                def steps(n):
                    for u in range(STEPS):
                        if tile := tile_due(n, u, 0):
                            keys_queries(*tile)
                        if step := step_due(n, u, SCORES):
                            exponential(*step)
                        if tile := tile_due(n, u, PACK):
                            pack(*tile)
                        if tile := tile_due(n, u, FINAL):
                            final(*tile)
                act.sem_inc(s.final_done, 1)
                act.wait_ge(s.keys_in, 16)
                act.wait_ge(s.cleared, 2)
                for g in (2, 3):
                    one_hot_rows(nc.scalar.copy, g)
                over_sequences(act, steps)
                steps(BATCH)

            @block.vector
            def _(dve):
                dve.wait_ge(core.params1_in, core.params1_count)
                nc.vector.memset(q_spread[:, 0:2, :, :, :].rearrange("p g b h q -> p (g b h q)"), 0.0).then_inc(s.cleared, 1)
                dve.wait_ge(s.cleared, 2)
                for g in (0, 1):
                    one_hot_rows(nc.vector.tensor_copy, g)
                heads = same_head.unsqueeze(1)
                dve.sem_inc(s.attended_done, 1)
                nc.vector.tensor_copy(v_ones[:, :, WIN:], heads.to_broadcast([P, BLOCKS * GROUPS, WIN])).then_inc(s.set_up, 1)

                def values(n, j):
                    t = TILES * n + j
                    dve.wait_ge(s.v_mm, t + 1)
                    wait(dve, s.pv_mm, STEPS * n + GROUPS * (j - 2))
                    nc.vector.tensor_tensor(v_ones[:, j * STEPS:(j + 1) * STEPS, 0:WIN], ps_v[:, :].rearrange("k (a d) -> k a d", d=WIN),
                                            heads.to_broadcast([P, STEPS, WIN]), ALU.mult).then_inc(s.v_done, 1)

                def maximum(n, u):
                    t = n * STEPS + u
                    dve.wait_ge(s.score_mm, t + 1)
                    wait(dve, s.diff_done, t - RING + 1)
                    nc.vector.tensor_reduce(largest[:, u % RING, :], ps_score[u % RING][:, 0:BT * KEYS].rearrange("p (b k) -> p b k", k=KEYS),
                                            AXX, ALU.max).then_inc(s.max_done, 1)

                def differences(n, u):
                    t = n * STEPS + u
                    dve.wait_ge(s.max_done, t + 1)
                    wait(dve, s.turned, t - RING + 1)
                    nc.vector.tensor_tensor(probs[:, u % RING, :].rearrange("p (b k) -> p b k", k=KEYS),
                                            ps_score[u % RING][:, 0:BT * KEYS].rearrange("p (b k) -> p b k", k=KEYS),
                                            largest[:, u % RING, :].unsqueeze(2).to_broadcast([P, BT, KEYS]),
                                            ALU.subtract).then_inc(s.diff_done, 1)

                def turn(n, u):
                    t = n * STEPS + u
                    dve.wait_ge(s.exp_done, t + 1)
                    wait(dve, s.pv_mm, t - RING + 1)
                    nc.vector.transpose(probsT[:, u % RING, :, :].rearrange("p a q -> p (a q)"), probs[:, u % RING, :]).then_inc(s.turned, 1)

                def divide(n, j):
                    t = TILES * n + j
                    dve.wait_ge(s.packed_done, t + 1)
                    dve.wait_ge(s.attended_done, t + 1)
                    nc.vector.reciprocal(inverse[:, :], packed[:, j % 2, 1, :]).then_inc(s.inverse_done, 1)
                    dve.wait_ge(s.inverse_done, t + 1)
                    wait(dve, s.final_done, t)
                    nc.vector.tensor_tensor(attended[:, j % 2, :], packed[:, j % 2, 0, :], inverse[:, :], ALU.mult).then_inc(s.attended_done, 1)

                def steps(n):
                    for u in range(STEPS):
                        if tile := tile_due(n, u, VALUES_OUT):
                            values(*tile)
                        if step := step_due(n, u, SCORES):
                            maximum(*step)
                        if step := step_due(n, u, TURN):
                            turn(*step)
                        if step := step_due(n, u, SCORES):
                            differences(*step)
                        if tile := tile_due(n, u, DIVIDE):
                            divide(*tile)
                over_sequences(dve, steps)
                steps(BATCH)


def mlp_phase(nc, core, wo, w_f1, w_f2, c1, bo, g1, b1, c2, g2, b2):
    with ExitStack() as ctx:
        sb = lambda name, shape, dt=F32: ctx.enter_context(nc.sbuf_tensor("ml_" + name, shape, dt))
        sem = lambda name: ctx.enter_context(nc.semaphore("ml_" + name))
        HID = FFN // P
        ALL = [P, TILES, P]
        aT = sb("aT", [P, SEQ])
        base = sb("base", ALL)
        raw = [sb("raw0", ALL), sb("raw1", ALL)]
        stats = [sb("stats0", [P, TILES, 6]), sb("stats1", [P, TILES, 6])]
        mean_var = [sb("mv0", [P, TILES, 2]), sb("mv1", [P, TILES, 2])]
        var_eps = [sb("ve0", [P, TILES]), sb("ve1", [P, TILES])]
        rstd = [sb("rstd0", [P, TILES]), sb("rstd1", [P, TILES])]
        h = sb("h", ALL)
        h_c2 = sb("h_c2", ALL)
        hT = sb("hT", [P, SEQ])
        hidden = sb("hidden", [P, HID, SEQ])
        names = "a_ready base_ready wo_mm h_done h_c2_done turned hT_done f1_mm gelu_done f2_mm x_b2_done added"
        s = type("Sems", (), {k: sem(k) for k in names.split()})
        raw_done, stats_done, mv_done, vareps_done, rstd_done, scaled_done = (
            [sem(f"{k}{i}") for i in range(2)] for k in ("raw_done", "stats_done", "mv_done", "vareps_done", "rstd_done", "scaled_done"))
        ps_wo, ps_turn, ps_f2 = core.bank[0], core.bank[1], core.bank[2]
        ps_f1 = core.bank[3:5]
        row = lambda r: r.unsqueeze(1).to_broadcast(ALL)
        tiles = lambda bank: bank[:, :].rearrange("p (c d) -> p c d", c=TILES)
        here = lambda t, n: t[:, bass.ds(n * SEQ, SEQ)].rearrange("p (c d) -> p c d", c=TILES)

        with nc.Block() as block:
            @block.gpsimd
            def _(pool):
                def inputs(n):
                    wait(pool, raw_done[0], n)
                    nc.gpsimd.tensor_tensor(base[:, :, :], here(core.xn2, n), row(bo), ALU.add).then_inc(s.base_ready, 1)
                    nc.gpsimd.tensor_tensor(here(core.x, n), here(core.x, n), row(b2), ALU.add).then_inc(s.x_b2_done, 1)

                def root(n, i):
                    pool.wait_ge(mv_done[i], TILES * (n + 1))
                    nc.gpsimd.tensor_tensor(var_eps[i][:, :], mean_var[i][:, :, 1], core.eps[:, 0:TILES], ALU.add).then_inc(vareps_done[i], 1)
                    pool.wait_ge(vareps_done[i], n + 1)
                    nc.gpsimd.tensor_tensor(rstd[i][:, :], var_eps[i][:, :], core.minus_half[:, 0:TILES], ALU.pow).then_inc(rstd_done[i], 1)

                def add_c2(n):
                    pool.wait_ge(s.h_done, TILES * (n + 1))
                    if live(n, 0, 1):
                        pool.wait_ge(raw_done[1], n + 1)
                    nc.gpsimd.tensor_tensor(h_c2[:, :, :], h[:, :, :], row(c2), ALU.add).then_inc(s.h_c2_done, 1)

                def steps(n):
                    if live(n, 0, 0):
                        inputs(n)
                        root(n, 0)
                    if live(n, 0, 1):
                        root(n - 1, 1)
                    if live(n, 0, 0):
                        add_c2(n)
                over_sequences(pool, steps)
                steps(BATCH)

            @block.tensor
            def _(pe):
                def project(n):
                    pe.wait_ge(s.a_ready, n + 1)
                    wait(pe, raw_done[0], n)
                    for c in range(TILES):
                        last = nc.tensor.matmul(ps_wo[:, c * P:(c + 1) * P], aT[:, c * P:(c + 1) * P], wo, start=True, stop=True)
                    last.then_inc(s.wo_mm, 1)

                def mlp(n):
                    pe.wait_ge(s.h_done, TILES * (n + 1))
                    for c in range(TILES):
                        last = nc.tensor.transpose(ps_turn[:, c * P:(c + 1) * P], h[:, c, :], core.ident[:, :])
                    last.then_inc(s.turned, 1)
                    pe.wait_ge(s.hT_done, n + 1)
                    for m in range(HID):
                        if m >= 2:
                            pe.wait_ge(s.gelu_done, HID * n + m - 1)
                        nc.tensor.matmul(ps_f1[m % 2][:, :], w_f1[:, m * P:(m + 1) * P], hT[:, :], start=True, stop=True).then_inc(s.f1_mm, 1)
                    if not isinstance(n, int) or n:
                        pe.wait_ge(raw_done[1], n + 1)
                    for m in range(HID):
                        pe.wait_ge(s.gelu_done, HID * n + m + 1)
                        for c in range(TILES):
                            last = nc.tensor.matmul(ps_f2[:, c * P:(c + 1) * P], hidden[:, m, c * P:(c + 1) * P],
                                                    w_f2[:, m * P:(m + 1) * P], start=(m == 0 and c == 0), stop=(m == HID - 1),
                                                    skip_group_check=True)
                    last.then_inc(s.f2_mm, 1)

                def steps(n):
                    if live(n, 0, 0):
                        project(n)
                    if live(n, 0, 1):
                        mlp(n - 1)
                over_sequences(pe, steps)
                steps(BATCH)

            @block.scalar
            def _(act):
                def inputs(n):
                    wait(act, s.wo_mm, n)
                    nc.scalar.activation(aT[:, :], core.xnT[:, bass.ds(n * SEQ, SEQ)], ACT.Copy).then_inc(s.a_ready, 1)

                def mlp(n):
                    act.wait_ge(s.turned, n + 1)
                    nc.scalar.activation(hT[:, :], ps_turn[:, :], ACT.Copy).then_inc(s.hT_done, 1)
                    wait(act, s.f2_mm, n)
                    for m in range(HID):
                        act.wait_ge(s.f1_mm, HID * n + m + 1)
                        nc.scalar.activation(hidden[:, m, :], ps_f1[m % 2][:, :], ACT.Gelu_apprx_tanh,
                                             bias=c1[:, m:m + 1]).then_inc(s.gelu_done, 1)

                def steps(n):
                    if live(n, 0, 0):
                        inputs(n)
                    if live(n, 0, 1):
                        mlp(n - 1)
                over_sequences(act, steps)
                steps(BATCH)

            @block.vector
            def _(dve):
                dve.sem_inc(raw_done[1], 1)

                def statistics(n, i):
                    for c in range(TILES):
                        nc.vector.bn_stats(stats[i][:, c, :], raw[i][:, c, :]).then_inc(stats_done[i], 1)
                    dve.wait_ge(stats_done[i], TILES * (n + 1))
                    nc.vector.memset(core.spare[:, 0:1], 0.0)
                    for c in range(TILES):
                        nc.vector.bn_aggr(mean_var[i][:, c, :], stats[i][:, c, :]).then_inc(mv_done[i], 1)

                def normalise(n, i, gain, shift, to, done):
                    dve.wait_ge(mv_done[i], TILES * (n + 1))
                    for c in range(TILES):
                        nc.vector.scalar_tensor_tensor(raw[i][:, c, :], raw[i][:, c, :], mean_var[i][:, c, 0:1], gain,
                                                       ALU.subtract, ALU.mult).then_inc(scaled_done[i], 1)
                    dve.wait_ge(scaled_done[i], TILES * (n + 1))
                    dve.wait_ge(rstd_done[i], n + 1)
                    for c in range(TILES):
                        nc.vector.scalar_tensor_tensor(to(c), raw[i][:, c, :], rstd[i][:, c:c + 1], shift(c),
                                                       ALU.mult, ALU.add).then_inc(done, 1)

                def first(n):
                    dve.wait_ge(s.wo_mm, n + 1)
                    dve.wait_ge(s.base_ready, n + 1)
                    wait(dve, s.h_done, TILES * n)
                    nc.vector.tensor_tensor(raw[0][:, :, :], tiles(ps_wo), base[:, :, :], ALU.add).then_inc(raw_done[0], 1)
                    dve.wait_ge(raw_done[0], n + 1)
                    statistics(n, 0)
                    wait(dve, s.turned, n)
                    wait(dve, s.h_c2_done, n)
                    normalise(n, 0, g1, lambda c: b1, lambda c: h[:, c, :], s.h_done)

                def second(n):
                    dve.wait_ge(s.f2_mm, n + 1)
                    dve.wait_ge(s.h_c2_done, n + 1)
                    wait(dve, s.added, TILES * n)
                    nc.vector.tensor_tensor(raw[1][:, :, :], tiles(ps_f2), h_c2[:, :, :], ALU.add).then_inc(raw_done[1], 1)
                    dve.wait_ge(raw_done[1], n + 2)
                    statistics(n, 1)
                    dve.wait_ge(s.x_b2_done, n + 1)
                    x_tile = lambda c: core.x[:, bass.ds((n * TILES + c) * P, P)]
                    normalise(n, 1, g2, x_tile, x_tile, s.added)

                def steps(n):
                    if live(n, 0, 0):
                        first(n)
                    if live(n, 0, 1):
                        second(n - 1)
                over_sequences(dve, steps)
                steps(BATCH)


def layer1_memory(nc, core):
    core.w1 = core.sb("w1", [P, columns(W1)[1]])
    core.c1 = core.sb("c1", [P, columns(C1)[1] + GROUPS + 2 * WIN])
    core.r1 = core.sb("r1", [P, columns(R1)[1]])
    core.more = core.sb("more_consts", [P, P + 3 * NT * EXP1 + SLOTS])
    core.zeros = core.sb("zeros", [P, P])
    core.params1_in, core.params1_count, core.more_in = core.sem("params1_in"), 48, core.sem("more_in")
    core.zero_set, core.cleared = core.sem("zero_set"), core.sem("cleared")
    core.sorted_x = nc.dram_tensor("sorted_x", (SLOTS * P, P), F32, kind="Internal").ap()
    core.sorted_y = nc.dram_tensor("sorted_y", (SLOTS * P, P), F32, kind="Internal").ap()


def layer1_loads(sp, core, ins):
    sp.dma_start(core.w1[:, :], ins["w1"]).then_inc(core.params1_in, 16)
    sp.dma_start(core.c1[:, :], ins["c1"]).then_inc(core.params1_in, 16)
    sp.dma_start(core.r1[:, :], ins["r1"].partition_broadcast(P)).then_inc(core.params1_in, 16)
    sp.dma_start(core.more[:, :], ins["more_consts"]).then_inc(core.more_in, 16)
    sp.wait_ge(core.zero_set, 1)
    sp.dma_start(core.sorted_x.rearrange("(s p) d -> p s d", p=P),
                 core.zeros[:, :].unsqueeze(1).to_broadcast([P, SLOTS, P])).then_inc(core.cleared, 16)


def layer1(nc, core, ins, out_rows):
    with ExitStack() as layer:
        lsb = lambda name, shape, dt=F32: layer.enter_context(nc.sbuf_tensor(name, shape, dt))
        at_w1, at_c1, at_r1 = columns(W1)[0], columns(C1)[0], columns(R1)[0]
        n_c1 = columns(C1)[1]
        core.xn2 = lsb("xn2", [P, NT * P])
        logits = lsb("logits1", [P, NT, EXP1])
        top8 = lsb("top1", [P, NT, 8])
        core.place = lsb("place", [P, NT], mybir.dt.uint32)
        core.slot_expert = lsb("slot_expert", [P, SLOTS], mybir.dt.int32)
        core.scattered = layer.enter_context(nc.semaphore("scattered"))
        W = lambda name: core.w1[:, at_w1[name][0]:at_w1[name][1]]
        C = lambda name: core.c1[:, at_c1[name][0]:at_c1[name][1]]
        R = lambda name: core.r1[:, at_r1[name][0]:at_r1[name][1]]
        heads, same_head, one_hot = (core.c1[:, n_c1 + a:n_c1 + b] for a, b in
                                     ((0, GROUPS), (GROUPS, GROUPS + WIN), (GROUPS + WIN, GROUPS + 2 * WIN)))
        norm_phase(nc, core, "n1_", core.x, None, W("w_small1"), EXP1, EXP1, R("gate_b"), logits, top8, core.xn2)
        places_phase(nc, core, logits, top8)
        attention_phase(nc, core, W("wq"), W("wk"), W("wv"), C("bq"), C("bk"), C("bv"), heads, same_head, one_hot, ins["key_mask"])
        experts1_load(nc, core, ins, layer)
        mlp_phase(nc, core, W("wo"), W("w_f1"), W("w_f2"), C("c1"), R("bo"), R("g1"), R("b1"), R("c2"), R("g2"), R("b2"))
        experts1_phase(nc, core, core.sorted_x, core.sorted_y, *core.expert_weights)
        gather_phase(nc, core, out_rows)


def layer1_arrays(a, pack, slices):
    channel = np.arange(P)
    query, key = np.arange(WIN)[:, None], np.arange(WIN)[None, :]
    key_mask = np.zeros((GROUPS, WIN, GROUPS, BLOCKS + 2, WIN), np.float32)
    for g in range(GROUPS):
        for which, r in enumerate([r for r in range(GROUPS) if r != g]):
            for blk in range(which, BLOCKS, 3):
                key_mask[r, :, g, blk] = np.where((key >= query) & (blk > 0), 0.0, -1e30)
                key_mask[r, :, g, blk + 2] = np.where((key <= query) & (blk < BLOCKS - 1), 0.0, -1e30)
    head_mask = ((channel[:, None] // AHD) % GROUPS == np.arange(GROUPS)) / np.sqrt(AHD)
    one_hot = channel[:, None] % WIN == np.arange(WIN)
    same_head = channel[:, None] // WIN == np.arange(WIN) // AHD
    arrays = {
        "w1": pack(W1, {"w_small1": a["L1_ffn_gate_w"].T, "wq": a["L1_attn_Wq"], "wk": a["L1_attn_Wk"], "wv": a["L1_attn_Wv"],
                        "wo": a["L1_attn_Wo"], "w_f1": a["L1_attn_W1"], "w_f2": slices(a["L1_attn_W2"])}),
        "c1": np.concatenate([pack(C1, {"bq": a["L1_attn_bq"][:, None], "bk": a["L1_attn_bk"][:, None], "bv": a["L1_attn_bv"][:, None],
                                        "c1": a["L1_attn_c1"].reshape(-1, P).T}), head_mask.astype(np.float32),
                              same_head.astype(np.float32), one_hot.astype(np.float32)], 1),
        "r1": np.concatenate([a["L1_ffn_gate_b"], a["L1_attn_bo"], a["L1_attn_g1"], a["L1_attn_b1"], a["L1_attn_c2"],
                              a["L1_attn_g2"], a["L1_attn_b2"]]),
        "key_mask": key_mask.reshape(P, -1),
    }
    arrays.update(experts1_arrays(a))
    return arrays


SLOTS = NT + EXP1 - 1
HID1 = EDIM1 // P
RING = 3


def places_phase(nc, core, logits, top8):
    with ExitStack() as ctx:
        sb = lambda name, shape, dt=F32: ctx.enter_context(nc.sbuf_tensor("pl_" + name, shape, dt))
        sem = lambda name: ctx.enter_context(nc.semaphore("pl_" + name))
        width = NT * EXP1
        restart8, restart32, multiples, slot_numbers = (core.more[:, P + a:P + b] for a, b in (
            (0, width), (width, 2 * width), (2 * width, 2 * width + NT), (3 * width, 3 * width + SLOTS)))
        E = [P, NT, EXP1]
        chosen = sb("chosen", E)
        order = sb("order", E)
        counts = sb("counts", [P, EXP1, NT])
        before = sb("before", [P, EXP1, NT])
        over = sb("over", [P, EXP1, NT])
        tiles_of = sb("tiles_of", [P, EXP1])
        tiles_to = sb("tiles_to", [P, EXP1])
        start = sb("start", [P, EXP1])
        passed = sb("passed", [P, SLOTS, EXP1])
        slot_e = sb("slot_e", [P, SLOTS])
        place = sb("place", [P, NT])
        dve_step, chosen_done, counted = sem("dve_step"), sem("chosen_done"), sem("counted")
        flat = lambda t: t[:, :, :].rearrange("p a b -> p (a b)")
        with nc.Block() as block:
            @block.tensor
            def _(pe):
                pe.wait_ge(core.more_in, 16)
                pe.wait_ge(chosen_done, 1)
                nc.tensor.matmul(core.bank[0][:, 0:NT * EXP1], core.more[:, 0:P], flat(chosen), start=True, stop=True).then_inc(counted, 1)
                nc.tensor.matmul(core.bank[1][:, 0:NT * EXP1], core.ones, flat(chosen), start=True, stop=True).then_inc(counted, 1)

            @block.vector
            def _(dve):
                count = [0]

                def step(ins):
                    count[0] += 1
                    ins.then_inc(dve_step, 1)
                    dve.wait_ge(dve_step, count[0])
                tt = nc.vector.tensor_tensor
                dve.wait_ge(core.more_in, 16)
                scan = lambda out, keep, data: step(nc.vector.tensor_tensor_scan(out, keep, data, 0.0, ALU.mult, ALU.add))
                step(tt(chosen[:, :, :], logits[:, :, :], top8[:, :, 0:1].to_broadcast(E), ALU.is_equal))
                scan(flat(order), restart8, flat(chosen))
                nc.vector.scalar_tensor_tensor(flat(chosen), flat(order), 1.0, flat(chosen), ALU.is_le, ALU.mult).then_inc(chosen_done, 1)
                dve.wait_ge(counted, 2)
                step(nc.vector.tensor_copy(counts[:, :, :], core.bank[1][:, 0:NT * EXP1].rearrange("p (t e) -> p e t", e=EXP1)))
                scan(flat(before), restart32, flat(counts))
                step(tt(over[:, :, :], before[:, :, NT - 1:NT].to_broadcast([P, EXP1, NT]),
                        multiples.unsqueeze(1).to_broadcast([P, EXP1, NT]), ALU.is_gt))
                step(nc.vector.tensor_reduce(tiles_of[:, :], over[:, :, :], AXX, ALU.add))
                step(tt(before[:, :, :], before[:, :, :], counts[:, :, :], ALU.subtract))
                scan(tiles_to[:, :], core.ones[:, 0:EXP1], tiles_of[:, :])
                step(tt(start[:, :], tiles_to[:, :], tiles_of[:, :], ALU.subtract))
                step(nc.vector.tensor_scalar(start[:, :], start[:, :], float(P), None, ALU.mult))
                step(tt(before[:, :, :], before[:, :, :], start[:, :].unsqueeze(2).to_broadcast([P, EXP1, NT]), ALU.add))
                step(tt(order[:, :, :], core.bank[0][:, 0:NT * EXP1].rearrange("p (t e) -> p t e", e=EXP1),
                        before[:, :, :].rearrange("p e t -> p t e"), ALU.add))
                step(tt(order[:, :, :], order[:, :, :], chosen[:, :, :], ALU.mult))
                step(nc.vector.tensor_reduce(place[:, :], order[:, :, :], AXX, ALU.add))
                step(nc.vector.tensor_copy(core.place[:, :], place[:, :]))
                step(tt(passed[:, :, :], slot_numbers.unsqueeze(2).to_broadcast([P, SLOTS, EXP1]),
                        tiles_to[:, :].unsqueeze(1).to_broadcast([P, SLOTS, EXP1]), ALU.is_ge))
                step(nc.vector.tensor_reduce(slot_e[:, :], passed[:, :, :], AXX, ALU.add))
                step(nc.vector.tensor_scalar(slot_e[:, :], slot_e[:, :], float(EXP1 - 1), None, ALU.min))
                step(nc.vector.tensor_copy(core.slot_expert[:, :], slot_e[:, :]))


def experts1_phase(nc, core, sorted_x, sorted_y, w_up, w_down, b_up, b_down):
    with ExitStack() as ctx:
        sb = lambda name, shape, dt=F32: ctx.enter_context(nc.sbuf_tensor("e1_" + name, shape, dt))
        sem = lambda name: ctx.enter_context(nc.semaphore("e1_" + name))
        x = sb("x", [P, RING, P])
        xT = sb("xT", [P, RING, P])
        up = sb("up", [P, RING, EDIM1])
        hT = sb("hT", [P, RING, EDIM1])
        y = sb("y", [P, RING, P])
        names = "x_turned xT_done up_mm up_done up_turned hT_done down_mm y_done"
        s = type("Sems", (), {k: sem(k) for k in names.split()})
        x_in = [sem(f"x_in{u}") for u in range(RING)]
        y_out = [sem(f"y_out{u}") for u in range(RING)]
        ps_x, ps_up, ps_h, ps_y = core.bank[0], core.bank[1:4], core.bank[4:7], core.bank[7]
        ROUNDS = SLOTS // RING
        expert_of = lambda eng, slot: eng.value_load(core.slot_expert[0:1, bass.ds(slot, 1)], min_val=0, max_val=EXP1 - 1)

        def going(r, u, lag):
            return not isinstance(r, int) or 0 <= r * RING + u - lag < SLOTS

        def rounds(eng, body):
            body(0)
            body(1)
            with eng.Fori(2, ROUNDS) as r:
                body(r)

        with nc.Block() as block:
            @block.sync
            def _(sp):
                sp.wait_ge(core.scattered, 16 * NT)

                def steps(r):
                    for u in range(RING):
                        if going(r, u, 0):
                            slot = r * RING + u
                            wait(sp, s.x_turned, slot - RING + 1)
                            sp.dma_start(x[:, u, :], sorted_x[bass.ds(slot * P, P), :]).then_inc(x_in[u], 16)
                rounds(sp, steps)

            @block.gpsimd
            def _(pool):
                def steps(r):
                    for u in range(RING):
                        slot = r * RING + u
                        pool.wait_ge(s.y_done, slot + 2)
                        pool.dma_start(sorted_y[bass.ds(slot * P, P), :], y[:, u, :]).then_inc(y_out[u], 16)
                rounds(pool, steps)
                for u in range(RING):
                    pool.wait_ge(y_out[u], 16 * ROUNDS)

            @block.tensor
            def _(pe):
                def turn(r, u):
                    slot = r * RING + u
                    pe.wait_ge(x_in[u], 16 * (r + 1))
                    wait(pe, s.xT_done, slot)
                    nc.tensor.transpose(ps_x[:, 0:P], x[:, u, :], core.ident).then_inc(s.x_turned, 1)

                def widen(r, u):
                    slot = r * RING + u
                    e = expert_of(pe, slot)
                    pe.wait_ge(s.xT_done, slot + 1)
                    wait(pe, s.up_done, slot - RING + 1)
                    nc.tensor.matmul(ps_up[u][:, :], xT[:, u, :], w_up[:, bass.ds(e * EDIM1, EDIM1)], start=True, stop=True).then_inc(s.up_mm, 1)

                def turn_up(r, u):
                    slot = r * RING + u
                    pe.wait_ge(s.up_done, slot + 1)
                    wait(pe, s.hT_done, slot - RING + 1)
                    for k in range(HID1):
                        last = nc.tensor.transpose(ps_h[u][:, k * P:(k + 1) * P], up[:, u, k * P:(k + 1) * P], core.ident)
                    last.then_inc(s.up_turned, 1)

                def narrow(r, u):
                    slot = r * RING + u
                    e = expert_of(pe, slot)
                    pe.wait_ge(s.hT_done, slot + 1)
                    if not isinstance(slot, int) or slot:
                        pe.wait_ge(s.y_done, slot + 1)
                    for k in range(HID1):
                        last = nc.tensor.matmul(ps_y[:, 0:P], hT[:, u, k * P:(k + 1) * P], w_down[:, bass.ds((e * HID1 + k) * P, P)],
                                                start=(k == 0), stop=(k == HID1 - 1))
                    last.then_inc(s.down_mm, 1)

                def steps(r):
                    for u in range(RING):
                        for lag, what in ((0, turn), (1, widen), (2, turn_up), (3, narrow)):
                            if going(r, u, lag):
                                what(r + (u - lag) // RING, (u - lag) % RING)
                pe.wait_ge(core.experts_in, 16 * 4)
                rounds(pe, steps)
                steps(ROUNDS)

            @block.scalar
            def _(act):
                def steps(r):
                    for u in range(RING):
                        if going(r, u, 0):
                            slot = r * RING + u
                            act.wait_ge(s.x_turned, slot + 1)
                            wait(act, s.up_mm, slot - RING + 1)
                            nc.scalar.activation(xT[:, u, :], ps_x[:, 0:P], ACT.Copy).then_inc(s.xT_done, 1)
                        if going(r, u, 2):
                            q, v = r + (u - 2) // RING, (u - 2) % RING
                            slot = q * RING + v
                            act.wait_ge(s.up_turned, slot + 1)
                            wait(act, s.down_mm, slot - RING + 1)
                            nc.scalar.activation(hT[:, v, :], ps_h[v][:, :], ACT.Relu).then_inc(s.hT_done, 1)
                rounds(act, steps)
                steps(ROUNDS)

            @block.vector
            def _(dve):
                dve.sem_inc(s.y_done, 1)
                dve.wait_ge(core.experts_in, 16 * 4)

                def bias_up(r, u):
                    slot = r * RING + u
                    e = expert_of(dve, slot)
                    dve.wait_ge(s.up_mm, slot + 1)
                    wait(dve, s.up_turned, slot - RING + 1)
                    nc.vector.tensor_tensor(up[:, u, :], ps_up[u][:, :], b_up[:, bass.ds(e * EDIM1, EDIM1)], ALU.add).then_inc(s.up_done, 1)

                def bias_down(r, u):
                    slot = r * RING + u
                    e = expert_of(dve, slot)
                    dve.wait_ge(s.down_mm, slot + 1)
                    if not isinstance(r, int) or r:
                        wait(dve, y_out[u], 16 * r)
                    nc.vector.tensor_tensor(y[:, u, :], ps_y[:, 0:P], b_down[:, bass.ds(e * P, P)], ALU.add).then_inc(s.y_done, 1)

                def steps(r):
                    for u in range(RING):
                        if going(r, u, 1):
                            bias_up(r + (u - 1) // RING, (u - 1) % RING)
                        if going(r, u, 3):
                            bias_down(r - 1, u)
                rounds(dve, steps)
                steps(ROUNDS)


def gather_phase(nc, core, out_rows):
    with ExitStack() as ctx:
        gathered = [ctx.enter_context(nc.semaphore(f"gathered{n}")) for n in range(BATCH)]
        added, out_done = ctx.enter_context(nc.semaphore("added")), ctx.enter_context(nc.semaphore("out_done"))
        with nc.Block() as block:
            @block.gpsimd
            def _(pool):
                for t in range(NT):
                    nc.gpsimd.indirect_dma_start(
                        out=core.xn2[:, t * P:(t + 1) * P], out_offset=None, in_=core.sorted_y,
                        in_offset=bass.IndirectOffsetOnAxis(ap=core.place[:, t:t + 1], axis=0)).then_inc(gathered[t // TILES], 16)

            @block.vector
            def _(dve):
                for n in range(BATCH):
                    here = slice(n * SEQ, (n + 1) * SEQ)
                    dve.wait_ge(gathered[n], 16 * TILES)
                    nc.vector.tensor_tensor(core.x[:, here], core.x[:, here], core.xn2[:, here], ALU.add).then_inc(added, 1)

            @block.sync
            def _(sp):
                for n in range(BATCH):
                    sp.wait_ge(added, n + 1)
                    sp.dma_start(out_rows[:, n * TILES:(n + 1) * TILES, :],
                                 core.x[:, n * SEQ:(n + 1) * SEQ].rearrange("p (c d) -> p c d", d=P)).then_inc(out_done, 16)
                sp.wait_ge(out_done, 16 * BATCH)


def scatter_tile(nc, core, t):
    nc.gpsimd.indirect_dma_start(
        out=core.sorted_x, out_offset=bass.IndirectOffsetOnAxis(ap=core.place[:, t:t + 1], axis=0),
        in_=core.xn2[:, t * P:(t + 1) * P], in_offset=None).then_inc(core.scattered, 16)


def experts1_load(nc, core, ins, layer):
    lsb = lambda name, shape, dt=F32: layer.enter_context(nc.sbuf_tensor(name, shape, dt))
    widths = {"w_up1": EXP1 * EDIM1, "w_down1": EXP1 * EDIM1, "b_up1": EXP1 * EDIM1, "b_down1": EXP1 * P}
    core.expert_weights = [lsb(name, [P, width]) for name, width in widths.items()]
    core.experts_in = layer.enter_context(nc.semaphore("experts_in"))
    with nc.Block() as block:
        @block.sync
        def _(sp):
            for name, to in zip(widths, core.expert_weights):
                source = ins[name].partition_broadcast(P) if name.startswith("b_") else ins[name]
                sp.dma_start(to[:, :], source).then_inc(core.experts_in, 16)


def experts1_arrays(a):
    row = lambda v, n: np.broadcast_to(np.asarray(v, np.float32), (P, n))
    width = NT * EXP1
    multiples = np.zeros(width)
    multiples[:NT] = np.arange(NT) * P
    return {
        "more_consts": np.concatenate([np.triu(np.ones((P, P)), 1), row(np.arange(width) % EXP1 != 0, width),
                                       row(np.arange(width) % NT != 0, width), row(multiples, width), row(np.arange(SLOTS), SLOTS)],
                                      1).astype(np.float32),
        "w_up1": a["L1_ffn_w1"].transpose(2, 0, 1).reshape(P, -1),
        "w_down1": a["L1_ffn_w2"].transpose(0, 2, 1).reshape(EXP1 * HID1, P, P).transpose(1, 0, 2).reshape(P, -1),
        "b_up1": a["L1_ffn_b1"].reshape(-1),
        "b_down1": a["L1_ffn_b2"].reshape(-1),
    }



def build(nc, ins, out):
    with ExitStack() as ctx:
        core = Core(nc, ctx)
        sb, sem = core.sb, core.sem
        core.banks = ctx.enter_context(nc.psum_tensor("banks", [P, 8, 512], F32))
        core.bank = [core.banks[:, i, :] for i in range(8)]
        core.x = sb("x", [P, NT * P])
        core.xnT = sb("xnT", [P, NT * P])
        at_w0, n_w0 = columns(W0)
        at_c0, n_c0 = columns(C0)
        at_r0, n_r0 = columns(R0)
        w0 = sb("w0", [P, n_w0])
        c0 = sb("c0", [P, n_c0])
        r0 = sb("r0", [P, n_r0])
        consts = sb("consts", [P, 4 * P])
        core.ident, core.upper, core.ones = consts[:, 0:P], consts[:, P:2 * P], consts[:, 2 * P:3 * P]
        core.minus_half, core.eps = consts[:, 3 * P:3 * P + 64], consts[:, 3 * P + 64:4 * P]
        core.spare = sb("spare", [P, 1])
        core.restart = sb("restart", [P, NT * EXP0])
        layer1_memory(nc, core)
        x_in = [sem("x_in_first"), sem("x_in_rest")]
        core.params_in = sem("params_in")
        core.params_count = 16 * 5
        W = lambda name: w0[:, at_w0[name][0]:at_w0[name][1]]
        C = lambda name: c0[:, at_c0[name][0]:at_c0[name][1]]
        R = lambda name: r0[:, at_r0[name][0]:at_r0[name][1]]
        x_rows = ins["x"].rearrange("b (c p) d -> p (b c) d", p=P)
        out_rows = out.rearrange("b (c p) d -> p (b c) d", p=P)

        def load_x(sp, n):
            sp.dma_start(core.x[:, n * SEQ:(n + 1) * SEQ].rearrange("p (c d) -> p c d", d=P),
                         x_rows[:, n * TILES:(n + 1) * TILES, :]).then_inc(x_in[min(n, 1)], 16)

        with nc.Block() as block:
            @block.sync
            def _(sp):
                load_x(sp, 0)
                sp.dma_start(consts[:, :], ins["consts"]).then_inc(core.params_in, 16)
                sp.dma_start(core.restart[:, :], ins["restart"]).then_inc(core.params_in, 16)
                sp.dma_start(c0[:, :], ins["c0"]).then_inc(core.params_in, 16)
                sp.dma_start(r0[:, :], ins["r0"].partition_broadcast(P)).then_inc(core.params_in, 16)
                sp.dma_start(w0[:, :], ins["w0"]).then_inc(core.params_in, 16)
                for n in range(1, BATCH):
                    load_x(sp, n)
                layer1_loads(sp, core, ins)

            @block.vector
            def _(dve):
                nc.vector.memset(core.zeros[:, :], 0.0).then_inc(core.zero_set, 1)

        with ExitStack() as layer:
            lsb = lambda name, shape, dt=F32: layer.enter_context(nc.sbuf_tensor(name, shape, dt))
            core.gates0 = lsb("gates0", [P, NT, EXP0])
            core.dt = lsb("dt", [P, NT, HEADS])
            core.cum = lsb("cum", [P, NT, HEADS])
            core.exp_cum = lsb("exp_cum", [P, NT, HEADS])
            core.exp_total = lsb("exp_total", [P, NT, HEADS])
            core.w_end = lsb("w_end", [P, NT, HEADS])
            with ExitStack() as routing:
                logits = routing.enter_context(nc.sbuf_tensor("logits0", [P, NT, EXP0 + HEADS], F32))
                top8 = routing.enter_context(nc.sbuf_tensor("top0", [P, NT, 8], F32))
                norm_phase(nc, core, "n0_", core.x, x_in, W("w_small0"), EXP0 + HEADS, EXP0, None, logits, top8, None)
                routing0_phase(nc, core, logits, top8, R("dt_bias"), R("a_log"))
            experts0_phase(nc, core, W("w_up0"), W("w_down0"))
            core.x_tokens = lsb("x_tokens", [P, NT, INNER + NSTATE])
            core.b_rows = lsb("b_rows", [NSTATE, 2, NT * P])
            skip_conv_phase(nc, core, W("w_zx"), W("w_out"), W("w_xbc"), C("conv_w"), C("conv_b"))
            ssm_phase(nc, core, W("w_gate"), W("w_out"), C("gamma"), C("beta"), C("b_gate"), R("d_param"))
        layer1(nc, core, ins, out_rows)


def kernel(**inputs):
    import concourse.bacc as bacc
    from concourse.bass_utils import run_bass_kernel_spmd

    a = {k: np.asarray(v) for k, v in inputs.items()}

    def pack(layout, parts):
        cols, width = columns(layout)
        packed = np.zeros((P, width), np.float32)
        for name, value in parts.items():
            packed[:value.shape[0], cols[name][0]:cols[name][0] + value.shape[1]] = value
        return packed

    def slices(m):
        return m.reshape(-1, P, m.shape[1]).transpose(1, 0, 2).reshape(P, -1)

    w_in = a["L0_attn_W_in"].T
    xbc = w_in[:, 3 * INNER:]
    conv = a["L0_attn_conv_w"][:, 0, :]
    zero = np.zeros((P, 16), np.float32)
    third = lambda m: np.concatenate([m[256:272], zero[:16, :m.shape[1]], m[272:288]])
    arrays = {
        "x": a["L0_attn_u"],
        "w0": pack(W0, {
            "w_small0": np.concatenate([a["L0_ffn_router_w"].T, w_in[:, -HEADS:]], 1),
            "w_up0": np.concatenate([a["L0_ffn_shared_up"].reshape(-1, P), a["L0_ffn_routed_up"].reshape(-1, P)]).T,
            "w_down0": slices(np.concatenate([a["L0_ffn_shared_down"].transpose(0, 2, 1).reshape(-1, P),
                                              a["L0_ffn_routed_down"].transpose(0, 2, 1).reshape(-1, P)])),
            "w_zx": np.concatenate([w_in[:, 0:128], w_in[:, 256:384], w_in[:, 128:256], w_in[:, 384:512]], 1),
            "w_xbc": np.concatenate([xbc[:, 0:272], zero, xbc[:, 272:288]], 1),
            "w_out": slices(a["L0_attn_W_out"].T),
            "w_gate": slices(a["L0_attn_W_gate"].T)}),
        "c0": pack(C0, {
            "conv_w": np.concatenate([conv[0:128], conv[128:256], np.concatenate([third(conv), np.zeros((80, 4), np.float32)])], 1),
            "conv_b": np.stack([a["L0_attn_conv_b"][0:128], a["L0_attn_conv_b"][128:256],
                                np.concatenate([third(a["L0_attn_conv_b"][:, None])[:, 0], np.zeros(80, np.float32)])], 1),
            "gamma": a["L0_attn_ln_gamma"].reshape(2, P).T, "beta": a["L0_attn_ln_beta"].reshape(2, P).T,
            "b_gate": a["L0_attn_b_gate"].reshape(2, P).T}),
        "r0": np.concatenate([a["L0_attn_dt_bias"], a["L0_attn_A_log"], a["L0_attn_D_param"]]),
        "consts": np.concatenate([np.eye(P), np.triu(np.ones((P, P))), np.ones((P, P)), np.full((P, 64), -0.5), np.full((P, 64), EPS)], 1).astype(np.float32),
        "restart": np.broadcast_to((np.arange(NT * EXP0) % EXP0 != 0).astype(np.float32), (P, NT * EXP0)).copy(),
    }
    arrays.update(layer1_arrays(a, pack, slices))
    nc = bacc.Bacc("TRN2", target_bir_lowering=False, num_devices=1)
    arrays = {f"in_{k}": np.ascontiguousarray(v) for k, v in arrays.items()}
    ins = {k[3:]: nc.dram_tensor(k, v.shape, mybir.dt.from_np(v.dtype), kind="ExternalInput").ap() for k, v in arrays.items()}
    out = nc.dram_tensor("out", (BATCH, SEQ, P), F32, kind="ExternalOutput").ap()
    build(nc, ins, out)
    result = run_bass_kernel_spmd(nc, [arrays], core_ids=[0])
    return result.results[0]["out"]
```
